# Optimizing a Trainium2 kernel written in Bass

```python
import numpy as np
import jax
import jax.numpy as jnp

def _softmax(x, axis=-1):
    return jax.nn.softmax(x, axis=axis)

def _gelu(x):
    return jax.nn.gelu(x, approximate=True)

def _silu(x):
    return jax.nn.silu(x)

def _sigmoid(x):
    return jax.nn.sigmoid(x)

def _layernorm(x, axis=-1, eps=1e-05):
    m = jnp.mean(x, axis=axis, keepdims=True)
    v = jnp.var(x, axis=axis, keepdims=True)
    return (x - m) / jnp.sqrt(v + eps)

def _scatter_add(tgt, idx, src, axis=0):
    return tgt.at[idx].add(src)

def _segment_sum(src, seg, n):
    return jax.ops.segment_sum(src, seg, n)
kernel_name = 'mk_decoder_preln_d1_seqx_r4_4a2bb2'

def setup_inputs(seed: int=0):
    np.random.seed(seed)
    _w = jnp.asarray

    def _rec_inputs():
        import jax
        import jax.numpy as jnp
        _rk = jax.random.key(seed)
        x = -0.0002928 + 1 * jax.random.normal(jax.random.fold_in(_rk, 1), (16, 256, 256), jnp.float32)
        _lenS = 256 - jax.random.randint(jax.random.fold_in(_rk, 7), (16,), 0, max(1, 256 // 4) + 1, jnp.int32)
        _lenS2 = 77 - jax.random.randint(jax.random.fold_in(_rk, 8), (16,), 0, max(1, 77 // 4) + 1, jnp.int32)
        _ctx_1024P = jax.random.normal(jax.random.fold_in(_rk, 11), (16, 16, 256), jnp.float32)
        _ctx_1024c = jax.random.dirichlet(jax.random.fold_in(_rk, 511), 0.3 * jnp.ones((16,), jnp.float32), (16, 77))
        _ctx_1024t = jnp.einsum('bsk,bkd->bsd', _ctx_1024c, _ctx_1024P)
        _ctx_1024t = _ctx_1024t * jax.lax.rsqrt(jnp.mean(jnp.square(_ctx_1024t)) + 1e-12) * 0.953939
        ctx_1024 = -1.39393e-06 + 0.999914 * (_ctx_1024t + 0.3 * jax.random.normal(jax.random.fold_in(_rk, 611), (16, 77, 256), jnp.float32))
        return (x, ctx_1024)
    x, ctx_1024 = _rec_inputs()

    def _L0_attn_setup():
        import jax, jax.numpy as jnp
        import numpy as np
        import math
        N_HEAD = 16
        V_HEAD = 32
        NOPE = 32
        ROPE_D = 64
        KEEP = 64
        EPS = 1e-06

        def _freqs(T, dim=ROPE_D, theta=10000.0):
            f = 1.0 / theta ** (jnp.arange(0, dim, 2, dtype=jnp.float32) / dim)
            t = jnp.arange(T, dtype=jnp.float32)
            a = jnp.outer(t, f)
            return (jnp.cos(a), jnp.sin(a))

        def _rope(x, cos, sin):
            S = x.shape[-2]
            c = cos[:S][None, None]
            s = sin[:S][None, None]
            x1, x2 = jnp.split(x, 2, axis=-1)
            return jnp.concatenate([x1 * c - x2 * s, x1 * s + x2 * c], axis=-1)

        def _rms(x, g, eps=EPS):
            return x * jax.lax.rsqrt(jnp.mean(x * x, axis=-1, keepdims=True) + eps) * g

        def _attn(q, k, v, causal):
            scale = 1.0 / math.sqrt(q.shape[-1])
            s = jnp.einsum('bhqd,bhkd->bhqk', q, k) * scale
            if causal:
                Tq, Tk = (s.shape[-2], s.shape[-1])
                mask = jnp.tril(jnp.ones((Tq, Tk), dtype=bool))
                s = jnp.where(mask, s, jnp.finfo(s.dtype).min)
            return jnp.einsum('bhqk,bhkd->bhqd', jax.nn.softmax(s, axis=-1), v)

        def _forward(x, w_cq, g_qnorm, w_dq_nope, w_dq_rope, w_ckv, g_kvnorm, w_dk_nope, w_dv, w_krope, w_imp, w_selk, w_selv, w_wink, w_winv, w_gate, w_proj):
            B, T, C = x.shape
            cos, sin = _freqs(T)
            nq = _rms(x @ w_cq, g_qnorm)
            q_nope = (nq @ w_dq_nope).reshape(B, T, N_HEAD, NOPE).transpose(0, 2, 1, 3)
            q_rope = (nq @ w_dq_rope).reshape(B, T, N_HEAD, ROPE_D).transpose(0, 2, 1, 3)
            q_rope = _rope(q_rope, cos, sin)
            q = jnp.concatenate([q_nope, q_rope], axis=-1)
            gate = jax.nn.softmax((x @ w_gate).mean(axis=1), axis=-1)
            ckv = _rms(x @ w_ckv, g_kvnorm)
            k_nope = (ckv @ w_dk_nope).reshape(B, T, N_HEAD, NOPE).transpose(0, 2, 1, 3)
            v1 = (ckv @ w_dv).reshape(B, T, N_HEAD, V_HEAD).transpose(0, 2, 1, 3)
            k_rope = (x @ w_krope).reshape(B, T, 1, ROPE_D).transpose(0, 2, 1, 3) / N_HEAD
            k_rope = _rope(k_rope, cos, sin)
            k1 = jnp.concatenate([k_nope, jnp.broadcast_to(k_rope, (B, N_HEAD, T, ROPE_D))], axis=-1)
            scores = (x @ w_imp)[..., 0]
            _, idx = jax.lax.top_k(scores, KEEP)
            idx = jnp.sort(idx, axis=1)
            sel = jnp.take_along_axis(x, idx[:, :, None], axis=1)
            ks = (sel @ w_selk).reshape(B, KEEP, N_HEAD, NOPE + ROPE_D).transpose(0, 2, 1, 3)
            vs = (sel @ w_selv).reshape(B, KEEP, N_HEAD, V_HEAD).transpose(0, 2, 1, 3)
            ks = jnp.concatenate([ks[..., :NOPE], _rope(ks[..., NOPE:], cos, sin)], axis=-1)
            kw = (x @ w_wink).reshape(B, T, N_HEAD, NOPE + ROPE_D).transpose(0, 2, 1, 3)
            vw = (x @ w_winv).reshape(B, T, N_HEAD, V_HEAD).transpose(0, 2, 1, 3)
            kw = jnp.concatenate([kw[..., :NOPE], _rope(kw[..., NOPE:], cos, sin)], axis=-1)
            a1 = _attn(q, k1, v1, causal=True)
            a2 = _attn(q, ks, vs, causal=False)
            a3 = _attn(q, kw, vw, causal=True)
            g = gate[:, :, None, None, None]
            out = g[:, 0] * a1 + g[:, 1] * a2 + g[:, 2] * a3
            out = out.transpose(0, 2, 1, 3).reshape(B, T, N_HEAD * V_HEAD)
            return out @ w_proj
        key = jax.random.key(seed)
        ks = jax.random.split(key, 20)
        B, T, C = (2, 256, 256)
        q_lora, kv_lora = (96, 32)
        std = 0.02

        def w(k, shape):
            return jax.random.normal(k, shape, dtype=jnp.float32) * std
        return {'x': jax.random.normal(ks[0], (B, T, C), dtype=jnp.float32), 'w_cq': w(ks[1], (C, q_lora)), 'g_qnorm': jnp.ones((q_lora,), jnp.float32), 'w_dq_nope': w(ks[2], (q_lora, N_HEAD * NOPE)), 'w_dq_rope': w(ks[3], (q_lora, N_HEAD * ROPE_D)), 'w_ckv': w(ks[4], (C, kv_lora)), 'g_kvnorm': jnp.ones((kv_lora,), jnp.float32), 'w_dk_nope': w(ks[5], (kv_lora, N_HEAD * NOPE)), 'w_dv': w(ks[6], (kv_lora, N_HEAD * V_HEAD)), 'w_krope': w(ks[7], (C, ROPE_D)), 'w_imp': w(ks[8], (C, 1)), 'w_selk': w(ks[9], (C, N_HEAD * (NOPE + ROPE_D))), 'w_selv': w(ks[10], (C, N_HEAD * V_HEAD)), 'w_wink': w(ks[11], (C, N_HEAD * (NOPE + ROPE_D))), 'w_winv': w(ks[12], (C, N_HEAD * V_HEAD)), 'w_gate': w(ks[13], (C, 3)), 'w_proj': w(ks[14], (N_HEAD * V_HEAD, C))}
    _L0_attn_all = _L0_attn_setup()
    _L0_attn_in = {k: v for k, v in _L0_attn_all.items() if k in ('w_cq', 'g_qnorm', 'w_dq_nope', 'w_dq_rope', 'w_ckv', 'g_kvnorm', 'w_dk_nope', 'w_dv', 'w_krope', 'w_imp', 'w_selk', 'w_selv', 'w_wink', 'w_winv', 'w_gate', 'w_proj')}
    del _L0_attn_all

    def _L0_xattn_setup():
        import jax, jax.numpy as jnp
        import numpy as np
        import math
        H = 16
        D_MODEL = 256
        D_K = D_MODEL // H

        def _split_heads(x):
            b, s, _ = x.shape
            return x.reshape(b, s, H, D_K).transpose(0, 2, 1, 3)
        key = jax.random.key(seed)
        ks = jax.random.split(key, 11)
        B, S = (2, 512)
        scale = 1.0 / math.sqrt(D_MODEL)
        inp = {'query': jax.random.normal(ks[0], (B, S, D_MODEL), dtype=jnp.float32), 'key': jax.random.normal(ks[1], (B, S, D_MODEL), dtype=jnp.float32), 'value': jax.random.normal(ks[2], (B, S, D_MODEL), dtype=jnp.float32), 'Wq': jax.random.normal(ks[3], (D_MODEL, D_MODEL), dtype=jnp.float32) * scale, 'bq': jnp.zeros((D_MODEL,), dtype=jnp.float32), 'Wk': jax.random.normal(ks[4], (D_MODEL, D_MODEL), dtype=jnp.float32) * scale, 'bk': jnp.zeros((D_MODEL,), dtype=jnp.float32), 'Wv': jax.random.normal(ks[5], (D_MODEL, D_MODEL), dtype=jnp.float32) * scale, 'bv': jnp.zeros((D_MODEL,), dtype=jnp.float32), 'Wo': jax.random.normal(ks[6], (D_MODEL, D_MODEL), dtype=jnp.float32) * scale, 'bo': jnp.zeros((D_MODEL,), dtype=jnp.float32)}
        return inp
    _L0_xattn_all = _L0_xattn_setup()
    _L0_xattn_in = {k: v for k, v in _L0_xattn_all.items() if k in ('Wq', 'bq', 'Wk', 'bk', 'Wv', 'bv', 'Wo', 'bo')}
    del _L0_xattn_all

    def _L0_ffn_setup():
        import jax, jax.numpy as jnp
        import numpy as np
        BLOCK = 32
        W_BITS = 4
        ACT_BITS = 16

        def act_qdq(x):
            qmax = 2.0 ** (ACT_BITS - 1) - 1.0
            scale = jnp.maximum(jnp.max(jnp.abs(x)) / qmax, 1e-12)
            return jnp.clip(jnp.round(x / scale), -qmax - 1.0, qmax) * scale

        def fixed_qdq_u16(x):
            scale = 1.0 / 65536.0
            return jnp.clip(jnp.round(x / scale), 0.0, 65535.0) * scale

        def lpbq_dequant(w):
            O, I = w.shape
            qmax = 2.0 ** (W_BITS - 1) - 1.0
            wb = w.reshape(O, I // BLOCK, BLOCK)
            s = jnp.maximum(jnp.max(jnp.abs(wb), axis=-1, keepdims=True) / qmax, 1e-12)
            wq = jnp.clip(jnp.round(wb / s), -qmax - 1.0, qmax) * s
            return wq.reshape(O, I)
        key = jax.random.key(seed)
        k1, k2, k3, k4 = jax.random.split(key, 4)
        B, S, H, I = (2, 1024, 256, 768)
        x = jax.random.normal(k1, (B, S, H), jnp.float32)
        w_gate = jax.random.normal(k2, (I, H), jnp.float32) * 0.02
        w_up = jax.random.normal(k3, (I, H), jnp.float32) * 0.02
        w_down = jax.random.normal(k4, (H, I), jnp.float32) * 0.02
        return {'x': x, 'w_gate': w_gate, 'w_up': w_up, 'w_down': w_down}
    _L0_ffn_all = _L0_ffn_setup()
    _L0_ffn_in = {k: v for k, v in _L0_ffn_all.items() if k in ('w_gate', 'w_up', 'w_down')}
    del _L0_ffn_all
    return {'x': x, 'ctx_1024': ctx_1024, 'L0_attn_w_cq': _L0_attn_in['w_cq'], 'L0_attn_g_qnorm': _L0_attn_in['g_qnorm'], 'L0_attn_w_dq_nope': _L0_attn_in['w_dq_nope'], 'L0_attn_w_dq_rope': _L0_attn_in['w_dq_rope'], 'L0_attn_w_ckv': _L0_attn_in['w_ckv'], 'L0_attn_g_kvnorm': _L0_attn_in['g_kvnorm'], 'L0_attn_w_dk_nope': _L0_attn_in['w_dk_nope'], 'L0_attn_w_dv': _L0_attn_in['w_dv'], 'L0_attn_w_krope': _L0_attn_in['w_krope'], 'L0_attn_w_imp': _L0_attn_in['w_imp'], 'L0_attn_w_selk': _L0_attn_in['w_selk'], 'L0_attn_w_selv': _L0_attn_in['w_selv'], 'L0_attn_w_wink': _L0_attn_in['w_wink'], 'L0_attn_w_winv': _L0_attn_in['w_winv'], 'L0_attn_w_gate': _L0_attn_in['w_gate'], 'L0_attn_w_proj': _L0_attn_in['w_proj'], 'L0_xattn_Wq': _L0_xattn_in['Wq'], 'L0_xattn_bq': _L0_xattn_in['bq'], 'L0_xattn_Wk': _L0_xattn_in['Wk'], 'L0_xattn_bk': _L0_xattn_in['bk'], 'L0_xattn_Wv': _L0_xattn_in['Wv'], 'L0_xattn_bv': _L0_xattn_in['bv'], 'L0_xattn_Wo': _L0_xattn_in['Wo'], 'L0_xattn_bo': _L0_xattn_in['bo'], 'L0_ffn_w_gate': _L0_ffn_in['w_gate'], 'L0_ffn_w_up': _L0_ffn_in['w_up'], 'L0_ffn_w_down': _L0_ffn_in['w_down']}

def reference(x, ctx_1024, L0_attn_w_cq, L0_attn_g_qnorm, L0_attn_w_dq_nope, L0_attn_w_dq_rope, L0_attn_w_ckv, L0_attn_g_kvnorm, L0_attn_w_dk_nope, L0_attn_w_dv, L0_attn_w_krope, L0_attn_w_imp, L0_attn_w_selk, L0_attn_w_selv, L0_attn_w_wink, L0_attn_w_winv, L0_attn_w_gate, L0_attn_w_proj, L0_xattn_Wq, L0_xattn_bq, L0_xattn_Wk, L0_xattn_bk, L0_xattn_Wv, L0_xattn_bv, L0_xattn_Wo, L0_xattn_bo, L0_ffn_w_gate, L0_ffn_w_up, L0_ffn_w_down):
    import jax
    import jax.numpy as jnp

    def _L0_attn_ref(x, w_cq, g_qnorm, w_dq_nope, w_dq_rope, w_ckv, g_kvnorm, w_dk_nope, w_dv, w_krope, w_imp, w_selk, w_selv, w_wink, w_winv, w_gate, w_proj):
        import jax, jax.numpy as jnp
        import numpy as np
        import math
        N_HEAD = 16
        V_HEAD = 32
        NOPE = 32
        ROPE_D = 64
        KEEP = 64
        EPS = 1e-06

        def _freqs(T, dim=ROPE_D, theta=10000.0):
            f = 1.0 / theta ** (jnp.arange(0, dim, 2, dtype=jnp.float32) / dim)
            t = jnp.arange(T, dtype=jnp.float32)
            a = jnp.outer(t, f)
            return (jnp.cos(a), jnp.sin(a))

        def _rope(x, cos, sin):
            S = x.shape[-2]
            c = cos[:S][None, None]
            s = sin[:S][None, None]
            x1, x2 = jnp.split(x, 2, axis=-1)
            return jnp.concatenate([x1 * c - x2 * s, x1 * s + x2 * c], axis=-1)

        def _rms(x, g, eps=EPS):
            return x * jax.lax.rsqrt(jnp.mean(x * x, axis=-1, keepdims=True) + eps) * g

        def _attn(q, k, v, causal):
            scale = 1.0 / math.sqrt(q.shape[-1])
            s = jnp.einsum('bhqd,bhkd->bhqk', q, k) * scale
            if causal:
                Tq, Tk = (s.shape[-2], s.shape[-1])
                mask = jnp.tril(jnp.ones((Tq, Tk), dtype=bool))
                s = jnp.where(mask, s, jnp.finfo(s.dtype).min)
            return jnp.einsum('bhqk,bhkd->bhqd', jax.nn.softmax(s, axis=-1), v)

        def _forward(x, w_cq, g_qnorm, w_dq_nope, w_dq_rope, w_ckv, g_kvnorm, w_dk_nope, w_dv, w_krope, w_imp, w_selk, w_selv, w_wink, w_winv, w_gate, w_proj):
            B, T, C = x.shape
            cos, sin = _freqs(T)
            nq = _rms(x @ w_cq, g_qnorm)
            q_nope = (nq @ w_dq_nope).reshape(B, T, N_HEAD, NOPE).transpose(0, 2, 1, 3)
            q_rope = (nq @ w_dq_rope).reshape(B, T, N_HEAD, ROPE_D).transpose(0, 2, 1, 3)
            q_rope = _rope(q_rope, cos, sin)
            q = jnp.concatenate([q_nope, q_rope], axis=-1)
            gate = jax.nn.softmax((x @ w_gate).mean(axis=1), axis=-1)
            ckv = _rms(x @ w_ckv, g_kvnorm)
            k_nope = (ckv @ w_dk_nope).reshape(B, T, N_HEAD, NOPE).transpose(0, 2, 1, 3)
            v1 = (ckv @ w_dv).reshape(B, T, N_HEAD, V_HEAD).transpose(0, 2, 1, 3)
            k_rope = (x @ w_krope).reshape(B, T, 1, ROPE_D).transpose(0, 2, 1, 3) / N_HEAD
            k_rope = _rope(k_rope, cos, sin)
            k1 = jnp.concatenate([k_nope, jnp.broadcast_to(k_rope, (B, N_HEAD, T, ROPE_D))], axis=-1)
            scores = (x @ w_imp)[..., 0]
            _, idx = jax.lax.top_k(scores, KEEP)
            idx = jnp.sort(idx, axis=1)
            sel = jnp.take_along_axis(x, idx[:, :, None], axis=1)
            ks = (sel @ w_selk).reshape(B, KEEP, N_HEAD, NOPE + ROPE_D).transpose(0, 2, 1, 3)
            vs = (sel @ w_selv).reshape(B, KEEP, N_HEAD, V_HEAD).transpose(0, 2, 1, 3)
            ks = jnp.concatenate([ks[..., :NOPE], _rope(ks[..., NOPE:], cos, sin)], axis=-1)
            kw = (x @ w_wink).reshape(B, T, N_HEAD, NOPE + ROPE_D).transpose(0, 2, 1, 3)
            vw = (x @ w_winv).reshape(B, T, N_HEAD, V_HEAD).transpose(0, 2, 1, 3)
            kw = jnp.concatenate([kw[..., :NOPE], _rope(kw[..., NOPE:], cos, sin)], axis=-1)
            a1 = _attn(q, k1, v1, causal=True)
            a2 = _attn(q, ks, vs, causal=False)
            a3 = _attn(q, kw, vw, causal=True)
            g = gate[:, :, None, None, None]
            out = g[:, 0] * a1 + g[:, 1] * a2 + g[:, 2] * a3
            out = out.transpose(0, 2, 1, 3).reshape(B, T, N_HEAD * V_HEAD)
            return out @ w_proj
        return _forward(x, w_cq, g_qnorm, w_dq_nope, w_dq_rope, w_ckv, g_kvnorm, w_dk_nope, w_dv, w_krope, w_imp, w_selk, w_selv, w_wink, w_winv, w_gate, w_proj)

    def _L0_xattn_ref(query, key, value, Wq, bq, Wk, bk, Wv, bv, Wo, bo):
        import jax, jax.numpy as jnp
        import numpy as np
        import math
        H = 16
        D_MODEL = 256
        D_K = D_MODEL // H

        def _split_heads(x):
            b, s, _ = x.shape
            return x.reshape(b, s, H, D_K).transpose(0, 2, 1, 3)
        q = _split_heads(query @ Wq.T + bq)
        k = _split_heads(key @ Wk.T + bk)
        v = _split_heads(value @ Wv.T + bv)
        scores = jnp.einsum('bhqd,bhkd->bhqk', q, k) / math.sqrt(D_K)
        attn = jax.nn.softmax(scores, axis=-1)
        ctx = jnp.einsum('bhqk,bhkd->bhqd', attn, v)
        b, h, s, d = ctx.shape
        ctx = ctx.transpose(0, 2, 1, 3).reshape(b, s, h * d)
        return ctx @ Wo.T + bo

    def _L0_ffn_ref(x, w_gate, w_up, w_down):
        import jax, jax.numpy as jnp
        import numpy as np
        BLOCK = 32
        W_BITS = 4
        ACT_BITS = 16

        def act_qdq(x):
            qmax = 2.0 ** (ACT_BITS - 1) - 1.0
            scale = jnp.maximum(jnp.max(jnp.abs(x)) / qmax, 1e-12)
            return jnp.clip(jnp.round(x / scale), -qmax - 1.0, qmax) * scale

        def fixed_qdq_u16(x):
            scale = 1.0 / 65536.0
            return jnp.clip(jnp.round(x / scale), 0.0, 65535.0) * scale

        def lpbq_dequant(w):
            O, I = w.shape
            qmax = 2.0 ** (W_BITS - 1) - 1.0
            wb = w.reshape(O, I // BLOCK, BLOCK)
            s = jnp.maximum(jnp.max(jnp.abs(wb), axis=-1, keepdims=True) / qmax, 1e-12)
            wq = jnp.clip(jnp.round(wb / s), -qmax - 1.0, qmax) * s
            return wq.reshape(O, I)
        x = act_qdq(x)
        up = act_qdq(x @ lpbq_dequant(w_up).T)
        gate = act_qdq(x @ lpbq_dequant(w_gate).T)
        sig = fixed_qdq_u16(jax.nn.sigmoid(gate))
        gate = act_qdq(gate * sig)
        o = act_qdq(gate * up)
        return o @ lpbq_dequant(w_down).T
    x = x + _L0_attn_ref(_layernorm(x, axis=-1), L0_attn_w_cq, L0_attn_g_qnorm, L0_attn_w_dq_nope, L0_attn_w_dq_rope, L0_attn_w_ckv, L0_attn_g_kvnorm, L0_attn_w_dk_nope, L0_attn_w_dv, L0_attn_w_krope, L0_attn_w_imp, L0_attn_w_selk, L0_attn_w_selv, L0_attn_w_wink, L0_attn_w_winv, L0_attn_w_gate, L0_attn_w_proj)
    x = x + _L0_xattn_ref(_layernorm(x, axis=-1), ctx_1024, ctx_1024, L0_xattn_Wq, L0_xattn_bq, L0_xattn_Wk, L0_xattn_bk, L0_xattn_Wv, L0_xattn_bv, L0_xattn_Wo, L0_xattn_bo)
    x = x + _L0_ffn_ref(_layernorm(x, axis=-1), L0_ffn_w_gate, L0_ffn_w_up, L0_ffn_w_down)
    return x

_drawn_inputs = setup_inputs


def setup_inputs(seed=0):
    import zlib

    import numpy as np

    out = dict(_drawn_inputs(seed))
    spreads = {'L0_attn_g_qnorm': (1.0, 0.6),
     'L0_attn_g_kvnorm': (1.0, 0.6),
     'L0_xattn_bq': (0.0, 0.384),
     'L0_xattn_bk': (0.0, 2.0),
     'L0_xattn_bv': (0.0, 0.1),
     'L0_xattn_bo': (0.0, 0.1)}
    factors = {'L0_attn_w_cq': 8.0,
     'L0_attn_w_dq_nope': 8.0,
     'L0_attn_w_dq_rope': 8.0,
     'L0_attn_w_ckv': 8.0,
     'L0_attn_w_dk_nope': 8.0,
     'L0_attn_w_dv': 8.0,
     'L0_attn_w_krope': 8.0,
     'L0_attn_w_imp': 8.0,
     'L0_attn_w_selk': 8.0,
     'L0_attn_w_selv': 8.0,
     'L0_attn_w_wink': 8.0,
     'L0_attn_w_winv': 8.0,
     'L0_attn_w_gate': 8.0,
     'L0_attn_w_proj': 6.073,
     'L0_ffn_w_gate': 5.502,
     'L0_ffn_w_up': 5.4,
     'L0_ffn_w_down': 5.413}
    for name, (base, spread) in spreads.items():
        noise = np.random.default_rng([zlib.crc32(name.encode()), seed]).standard_normal(out[name].shape)
        drawn = base * np.exp(spread * noise) if base else spread * noise
        out[name] = jnp.asarray(drawn.astype(out[name].dtype))
    for name, factor in factors.items():
        out[name] = (out[name] * factor).astype(out[name].dtype)
    return out
```

```python
from contextlib import ExitStack

import numpy as np
import concourse.bass as bass
from concourse import mybir

ALU = mybir.AluOpType
ACT = mybir.ActivationFunctionType
AX = mybir.AxisListType
F32 = mybir.dt.float32
BF16 = mybir.dt.bfloat16

P = 128
B, T, C = 16, 256, 256
TT, CT = T // P, C // P
HEADS, GROUP = 16, 4
GROUPS = HEADS // GROUP
PART = 32
PARTS = 3
DK = PART * PARTS
VD = 32
KEEP = 64
QL, KVL = 96, 32
LC = QL + KVL + 3
CTX = 77
XD = C // HEADS
XH = P // XD
INNER = 768
IT = INNER // P
BLK = 32
MAGIC = 1.5 * 2.0 ** 23
QMAX = 32767.0
LN_EPS, RMS_EPS = 1e-5, 1e-6
MASKED = -1e30
WIN, BASE, SEL = 0, 1, 2
GATE_ORDER = [2, 0, 1]
QC, WC0, SC0, BC0 = 0, T, 2 * T, 2 * T + KEEP
HCOLS = 3 * T + KEEP
S1, S0 = 64, 640
SEG = {(1, WIN): (0, 256), (1, SEL): (256, 64), (1, BASE): (320, 256),
       (0, WIN): (576, 128), (0, SEL): (704, 64), (0, BASE): (768, 128)}
PCOLS = 896
GDMA = 16 * GROUP * PARTS
PBUF = 4
LAG = 3


class Signal:

    def __init__(self, sem, per, first=0):
        self.sem, self.per, self.first = sem, per, first

    def wait(self, eng, b, k):
        assert k + self.first > 0
        eng.wait_ge(self.sem, b * self.per + k + self.first)

    def wait_all(self, eng, passes):
        eng.wait_ge(self.sem, passes * self.per + self.first)


def build(nc, io):
    with ExitStack() as outer:
        h_dram = nc.dram_tensor("h_scratch", (B, P, CT * T), F32, kind="Internal").ap()
        x2_dram = nc.dram_tensor("x2_scratch", (B, P, TT * C), F32, kind="Internal").ap()
        u_dram = nc.dram_tensor("u_scratch", (B, P, IT * T), F32, kind="Internal").ap()
        ident = outer.enter_context(nc.sbuf_tensor("ident", [P, P], F32))
        hmax = outer.enter_context(nc.sbuf_tensor("hmax", [P, 1], F32))
        phase1(nc, io, h_dram, x2_dram, ident, hmax)
        phase2(nc, io, h_dram, x2_dram, u_dram, ident, hmax)


def phase1(nc, io, h_dram, x2_dram, ident, hmax):
    with ExitStack() as ctx:
        def sb(name, shape, dt=F32):
            return ctx.enter_context(nc.sbuf_tensor(name, shape, dt))

        def signal(name, per=1, first=0):
            return Signal(ctx.enter_context(nc.semaphore("s_" + name)), per, first)

        def prime(eng, *signals):
            for s in signals:
                eng.sem_inc(s.sem, s.first)

        w_lat = sb("w_lat", [P, CT, LC])
        w_imp = sb("w_imp", [P, CT, P])
        w_win = sb("w_win", [P, CT, GROUPS * PARTS * P])
        w_sel = sb("w_sel", [P, CT, GROUPS * PARTS * P])
        w_winv = sb("w_winv", [P, CT, HEADS * VD])
        w_selv = sb("w_selv", [P, CT, HEADS * VD])
        w_q = sb("w_q", [P, GROUPS * PARTS * P])
        w_kn = sb("w_kn", [P, GROUPS * P])
        w_v1 = sb("w_v1", [P, HEADS * VD])
        w_kr = sb("w_kr", [P, CT, 2 * P])
        w_proj = sb("w_proj", [P, GROUPS, C])
        w_x = sb("w_x", [P, 4, CT, C])
        g_lat = sb("g_lat", [P, 1])
        rope_k = sb("rope_k", [P, 2, T])
        rope_q = sb("rope_q", [P, 2, T])
        maskb = sb("maskb", [P, 2 * P], BF16)
        identb = sb("identb", [P, P], BF16)
        before = sb("before", [P, TT, T])
        uptri = sb("uptri", [P, 2 * P])
        iota64 = sb("iota64", [P, KEEP])
        own16 = sb("own16", [P, XH])
        meanw = sb("meanw", [P, P])
        xb = sb("xb", [P, 2, CT])
        xrow = sb("xrow", [P, 2, C])
        bq4 = sb("bq4", [P, CT])
        minus_half = sb("minus_half", [P, 4])
        xin = sb("xin", [P, TT, C])
        ctxT = sb("ctxT", [P, CT, CTX])
        stats = sb("stats", [P, TT, 6])
        meanvar = sb("meanvar", [P, TT, 2])
        vareps = sb("vareps", [P, TT])
        rstd = sb("rstd", [P, TT])
        xn = sb("xn", [P, TT, C])
        xnT = sb("xnT", [P, CT, T])
        lat = sb("lat", [P, TT, LC])
        ms = sb("ms", [P, TT, 2])
        rlat = sb("rlat", [P, TT, 2])
        held = sb("held", [P, 4])
        nlat = sb("nlat", [P, TT, P])
        nT = sb("nT", [P, T])
        srow = sb("srow", [P, T])
        scol = sb("scol", [P, TT])
        cnt = sb("cnt", [P, TT])
        tie = sb("tie", [P, TT])
        chosen = sb("chosen", [P, TT])
        rank = sb("rank", [P, TT])
        pick = sb("pick", [P, TT, KEEP])
        selT = sb("selT", [P, CT, KEEP])
        gmax = sb("gmax", [P, 1])
        gexp = sb("gexp", [P, 3])
        gsum = sb("gsum", [P, 1])
        ginv = sb("ginv", [P, 1])
        gate = sb("gate", [P, 3])
        V = sb("V", [P, 5, HEADS * VD])
        rot1 = sb("rot1", [P, 2, T])
        rot2 = sb("rot2", [P, 2, T])
        junk, sq = rot1, rot2
        st = sb("st", [P, 2, PARTS, HCOLS])
        QK = sb("QK", [DK, GROUPS, GROUP, HCOLS])
        nmax = sb("nmax", [P, 2, 6])
        rsum = sb("rsum", [P, 2, 6])
        rinv = sb("rinv", [P, 2, 6])
        coef = sb("coef", [P, 2, 6])
        Pr = sb("Pr", [P, PBUF, PCOLS])
        PT = sb("PT", [P, GROUP, 1024])
        OT = sb("OT", [P, GROUPS, T])
        x1 = sb("x1", [P, TT, C])
        kT2 = sb("kT2", [P, CT, CTX])
        Vz = sb("Vz", [CTX, HEADS // 2, 2, 2, XD])
        nmax2 = sb("nmax2", [P, HEADS])
        rs2 = sb("rs2", [P, HEADS])
        ri2 = sb("ri2", [P, HEADS])
        hm = sb("hm", [P, 1])
        P2 = Pr[:, :, :].rearrange("p a b -> p (a b)")[:, 0:2 * HEADS * CTX].rearrange(
            "p (i h k) -> p i h k", i=TT, h=HEADS)
        pflat = Pr[:, :, :].rearrange("p a b -> p (a b)")
        after = 2 * HEADS * CTX
        hT = pflat[:, after:after + CT * T].rearrange("p (c t) -> p c t", c=CT)
        x1b = pflat[:, after + CT * T:after + CT * T + TT * C].rearrange("p (i c) -> p i c", i=TT)
        kwflat = st[:, 0, :, :].rearrange("p b c -> p (b c)")
        qflat = st[:, 1, :, :].rearrange("p b c -> p (b c)")
        Kbd = kwflat[:, 0:CT * XH * CTX].rearrange("p (f h k) -> p f h k", f=CT, h=XH)
        q2 = qflat[:, 0:CT * T].rearrange("p (f t) -> p f t", f=CT)
        O2T = qflat[:, CT * T:2 * CT * T].rearrange("p (f t) -> p f t", f=CT)
        x2 = qflat[:, 2 * CT * T:2 * CT * T + TT * C].rearrange("p (i c) -> p i c", i=TT)
        PT2 = PT[:, :, :].rearrange("p a b -> p (a b)").rearrange("p (h t) -> p h t", h=HEADS)

        ps = ctx.enter_context(nc.psum_tensor("ps", [P, 8, 512], F32))
        flat = ps[:, 0:4, :].rearrange("p a b -> p (a b)")
        b4, b5, bO, bM = ps[:, 4, :], ps[:, 5, :], ps[:, 6, :], ps[:, 7, :]

        loads = [
            (w_lat, "w_lat"), (w_imp, "w_imp"), (w_win, "w_win"), (w_sel, "w_sel"), (w_winv, "w_winv"),
            (w_selv, "w_selv"), (w_q, "w_q"), (w_kn, "w_kn"), (w_v1, "w_v1"), (w_kr, "w_kr"),
            (w_proj, "w_proj"), (w_x, "w_x"), (g_lat, "g_lat"), (rope_k, "rope_k"), (rope_q, "rope_q"),
            (maskb, "maskb"), (identb, "identb"), (before, "before"), (uptri, "uptri"),
            (iota64, "iota64"), (own16, "own16"), (meanw, "meanw"), (xb, "xb"), (xrow, "xrow"),
            (ident, "ident"),
        ]

        s_w = signal("weights", 0)
        s_init = signal("init", 0)
        s_x = signal("x_loaded", 16)
        s_ctx = signal("ctx_loaded", 16)
        s_stat = signal("ln_stats", 6)
        s_mv = signal("ln_meanvar", 6)
        s_held = signal("held", 3)
        s_ve = signal("ln_vareps", 3)
        s_rstd = signal("ln_rstd", 3)
        s_xn = signal("ln_done", 6)
        s_xnT_ps = signal("xnT_ps", 3)
        s_xnT = signal("xnT", 3)
        s_lat_ps = signal("latent_ps", 1)
        s_lat = signal("latent", 1)
        s_ms = signal("mean_square", 4)
        s_rlat = signal("latent_rms", 1)
        s_nlat = signal("latent_normed", 4)
        s_nT_ps = signal("nT_ps", 1)
        s_nT = signal("nT", 1)
        s_gate_ps = signal("gate_ps", 1)
        s_gmax = signal("gate_max", 1)
        s_gexp = signal("gate_exp", 1)
        s_ginv = signal("gate_inv", 1)
        s_gate = signal("gate", 1)
        s_srow_ps = signal("score_ps", 1)
        s_srow = signal("score_row", 1)
        s_scol = signal("score_col", 2)
        s_rankop = signal("rank_ops", 8)
        s_chosen = signal("chosen", 2)
        s_rank_ps = signal("rank_ps", 1)
        s_rank = signal("rank", 1)
        s_pick = signal("pick", 2)
        s_selT_ps = signal("selT_ps", 1)
        s_selT = signal("selT", 1)
        s_v_ps = signal("value_ps", 5)
        s_v = signal("value", 5)
        s_kr_ps = signal("krope_ps", 1)
        s_task_ps = signal("task_ps", 16)
        s_mul = signal("rope_products", 1 + GROUPS * 3)
        s_rot = signal("rope_done", 2 + GROUPS * 3, first=1)
        s_copy = signal("nope_copied", GROUPS * 3)
        s_group = [signal("even_group", 2 * GDMA, first=1), signal("odd_group", 2 * GDMA, first=1)]
        s_s = signal("scores", HEADS, first=1)
        s_max = signal("score_max", HEADS * 3)
        s_exp = signal("exp", HEADS * 6)
        s_rinv = signal("sum_inverse", HEADS)
        s_coef = signal("coefficient", HEADS)
        s_pn = signal("probs_scaled", HEADS * 6)
        s_pt_ps = signal("probsT_ps", HEADS)
        s_pta = signal("probsT_a", HEADS)
        s_ptb = signal("probsT_b", HEADS)
        s_o_ps = signal("heads_ps", GROUPS)
        s_o = signal("heads_out", GROUPS)
        s_proj = signal("proj_ps", 1)
        s_x1 = signal("x1", 2, first=1)
        s_k2_ps = signal("xk_ps", 1, first=1)
        s_v2_ps = signal("xv_ps", 1, first=1)
        s_q2_ps = signal("xq_ps", 1)
        s_k2 = signal("xk", 2)
        s_kbd = signal("xk_blocks", 2)
        s_v2 = signal("xv", 2)
        s_q2 = signal("xq", 2)
        s_s2 = signal("xscores", 2)
        s_m2 = signal("xmax", 2)
        s_sub2 = signal("xshifted", 2, first=1)
        s_e2 = signal("xexp", 2)
        s_r2 = signal("xsum", 4)
        s_n2 = signal("xprobs", 2)
        s_t2_ps = signal("xprobsT_ps", 8)
        s_t2a = signal("xprobsT_act", 4, first=1)
        s_t2v = signal("xprobsT_dve", 4, first=1)
        s_o2_ps = signal("xheads_ps", 1)
        s_o2 = signal("xheads_out", 1)
        s_y2 = signal("xproj_ps", 1)
        s_x1b = signal("x1_biased", 2)
        s_x2 = signal("x2", 2, first=1)
        s_hm = signal("h_max", 1)
        s_hmax = signal("h_running_max", 1)
        s_out = signal("stored", 32, first=1)

        block = ctx.enter_context(nc.Block())

        def head_scores(h):
            return flat[:, (h % 2) * 1024:(h % 2) * 1024 + 1024]

        @block.sync
        def _(sp):
            prime(sp, *s_group, s_out)
            for tile, name in loads:
                src = io[name]
                dims = len(tile.shape)
                dst = tile[:, :] if dims == 2 else tile[:, :, :] if dims == 3 else tile[:, :, :, :]
                sp.dma_start(dst, src).then_inc(s_w.sem, 16)
            with sp.Fori(0, B) as b:
                s_x1.wait(sp, b, 0)
                sp.dma_start(xin[:, :, :], io["x"][bass.ds(b, 1)].rearrange(
                    "o (i p) c -> p (o i) c", p=P)).then_inc(s_x.sem, 16)
                s_k2_ps.wait(sp, b, 0)
                s_v2_ps.wait(sp, b, 0)
                sp.dma_start(ctxT[:, :, :], io["ctxT"][bass.ds(b, 1)].rearrange(
                    "o (i p) c -> p (o i) c", p=P)).then_inc(s_ctx.sem, 16)
                for g in range(GROUPS):
                    if g == 0:
                        s_s.wait(sp, b, 0)
                    s_rot.wait(sp, b, 2 + 3 * (g + 1))
                    for j in range(GROUP):
                        for part in range(PARTS):
                            sp.dma_start(QK[PART * part:PART * (part + 1), g, j, :],
                                         st[PART * j:PART * (j + 1), g % 2, part, :])\
                                .then_inc(s_group[g % 2].sem, 16)
                s_x2.wait(sp, b, 2)
                sp.dma_start(x2_dram[bass.ds(b, 1)].rearrange("o p c -> p (o c)"),
                             x2.rearrange("p a b -> p (a b)")).then_inc(s_out.sem, 16)
                s_xnT.wait(sp, b, 3)
                sp.dma_start(h_dram[bass.ds(b, 1)].rearrange("o p c -> p (o c)"),
                             hT.rearrange("p a b -> p (a b)")).then_inc(s_out.sem, 16)
            s_out.wait_all(sp, B)

        @block.tensor
        def _(pe):
            prime(pe, s_k2_ps, s_s, s_v2_ps)
            pe.wait_ge(s_w.sem, 16 * len(loads))
            pe.wait_ge(s_init.sem, 6)

            def four_transposes(bank, src, signal_):
                for i in range(TT):
                    for c in range(CT):
                        m = pe.transpose(bank.rearrange("p (c t) -> p c t", c=CT)[:, c, i * P:(i + 1) * P],
                                         src[:, i, c * P:(c + 1) * P], ident[:, :])
                m.then_inc(signal_.sem, 1)

            def task(b, g, n):
                two = bM.rearrange("p (a t) -> p a t", a=2)
                if n in (1, 3):
                    s_mul.wait(pe, b, 1 + 3 * g + {1: 1, 3: 2}[n])
                elif n == 2:
                    s_copy.wait(pe, b, 3 * g + 1)
                elif g:
                    s_copy.wait(pe, b, 3 * g)
                    s_mul.wait(pe, b, 1 + 3 * g)
                col = lambda part: slice((g * PARTS + part) * P, (g * PARTS + part + 1) * P)
                if n == 0:
                    for part in (1, 2):
                        for c in range(CT):
                            m = pe.matmul(two[:, part - 1, :], w_win[:, c, col(part)], xnT[:, c, :],
                                          start=(c == 0), stop=(c == CT - 1))
                elif n == 1:
                    pe.matmul(two[:, 0, :], w_kn[:, g * P:(g + 1) * P], nT[:, :], start=True, stop=True)
                    for c in range(CT):
                        m = pe.matmul(two[:, 1, :], w_win[:, c, col(0)], xnT[:, c, :],
                                      start=(c == 0), stop=(c == CT - 1))
                elif n == 2:
                    for part in (1, 2):
                        m = pe.matmul(two[:, part - 1, :], w_q[:, col(part)], nT[:, :], start=True, stop=True)
                else:
                    pe.matmul(two[:, 0, :], w_q[:, col(0)], nT[:, :], start=True, stop=True)
                    for part in range(PARTS):
                        for c in range(CT):
                            m = pe.matmul(bM[:, T + KEEP * part:T + KEEP * (part + 1)], w_sel[:, c, col(part)],
                                          selT[:, c, :], start=(c == 0), stop=(c == CT - 1))
                m.then_inc(s_task_ps.sem, 1)

            def scores(b, h):
                g, j = h // GROUP, h % GROUP
                if j == 0:
                    s_group[g % 2].wait(pe, b, GDMA * (g // 2 + 1))
                if h >= 2:
                    s_exp.wait(pe, b, 6 * (h - 1))
                S = head_scores(h)
                qk = QK[:, g, j, :]
                q0, q1 = qk[:, QC:QC + P], qk[:, QC + P:QC + T]
                pe.matmul(S[:, 64:512], q1, qk[:, WC0:WC0 + 448], start=True, stop=False, skip_group_check=True)
                pe.matmul(S[:, 192:320], identb[:, :], maskb[:, 0:P], start=False, stop=True,
                          skip_group_check=True)
                pe.matmul(S[:, 512:640], q1, qk[:, WC0 + 448:HCOLS], start=True, stop=False,
                          skip_group_check=True)
                pe.matmul(S[:, 512:640], identb[:, :], maskb[:, 0:P], start=False, stop=False,
                          skip_group_check=True)
                pe.matmul(S[:, S0:S0 + P], q0, qk[:, WC0:WC0 + P], start=False, stop=False,
                          skip_group_check=True)
                pe.matmul(S[:, S0 + P:S0 + 2 * P + KEEP], q0, qk[:, SC0:SC0 + KEEP + P],
                          start=False, stop=False, skip_group_check=True)
                pe.matmul(S[:, S0:S0 + P], identb[:, :], maskb[:, 0:P], start=False, stop=False,
                          skip_group_check=True)
                m = pe.matmul(S[:, S0 + P + KEEP:S0 + 2 * P + KEEP], identb[:, :], maskb[:, 0:P], start=False,
                              stop=True, skip_group_check=True)
                m.then_inc(s_s.sem, 1)

            def transposes(b, h):
                s_pn.wait(pe, b, 6 * (h + 1))
                if h:
                    s_pta.wait(pe, b, h)
                    s_ptb.wait(pe, b, h)
                p = Pr[:, h % PBUF, :]
                w1, b1, e1 = SEG[1, WIN][0], SEG[1, BASE][0], SEG[1, SEL][0]
                w0, b0, e0 = SEG[0, WIN][0], SEG[0, BASE][0], SEG[0, SEL][0]
                for to, at in ((b4[:, 0:P], w0), (b4[:, P:2 * P], w1), (b4[:, 2 * P:3 * P], b0),
                               (b4[:, 3 * P:4 * P], b1), (b5[:, 0:P], w1 + P), (b5[:, P:2 * P], b1 + P)):
                    pe.transpose(to, p[:, at:at + P], ident[:, :])
                pe.transpose(b5[0:KEEP, 2 * P:3 * P], p[:, e0:e0 + KEEP], ident[:, :])
                pe.transpose(b5[0:KEEP, 3 * P:4 * P], p[:, e1:e1 + KEEP], ident[:, :]).then_inc(s_pt_ps.sem, 1)

            def values(b, g):
                s_pta.wait(pe, b, GROUP * (g + 1))
                s_ptb.wait(pe, b, GROUP * (g + 1))
                if g:
                    s_o.wait(pe, b, g)
                else:
                    s_v.wait(pe, b, 5)
                    s_lat.wait(pe, b, 1)
                for n, (tile, at, width, to) in enumerate((
                        (0, 0, T, 0), (2, T, T, 0), (4, 3 * T, T, 0), (1, 2 * T, P, P), (3, 2 * T + P, P, P))):
                    for j in range(GROUP):
                        h = g * GROUP + j
                        m = pe.matmul(bO[VD * j:VD * (j + 1), to:to + width], V[:, tile, VD * h:VD * (h + 1)],
                                      PT[:, j, at:at + width], start=(n == 0), stop=(n == 4),
                                      skip_group_check=True)
                m.then_inc(s_o_ps.sem, 1)

            with pe.Fori(0, B) as b:
                s_xn.wait(pe, b, 2)
                s_x2.wait(pe, b, 0)
                four_transposes(bM, xn, s_xnT_ps)
                s_xnT.wait(pe, b, 1)
                for i in range(TT):
                    for c in range(CT):
                        m = pe.matmul(bO[:, i * T:i * T + LC], xnT[:, c, i * P:(i + 1) * P], w_lat[:, c, :],
                                      start=(c == 0), stop=(c == CT - 1))
                m.then_inc(s_lat_ps.sem, 1)
                s_t2a.wait(pe, b, 0)
                for c in range(CT):
                    m = pe.matmul(b4[:, 0:T], w_imp[:, c, :], xnT[:, c, :], start=(c == 0), stop=(c == CT - 1))
                m.then_inc(s_srow_ps.sem, 1)
                s_sub2.wait(pe, b, 0)
                for i in range(TT):
                    for c in range(CT):
                        m = pe.matmul(ps[:, i, :], xnT[:, c, i * P:(i + 1) * P], w_winv[:, c, :],
                                      start=(c == 0), stop=(c == CT - 1))
                    m.then_inc(s_v_ps.sem, 1)
                for part in range(2):
                    for c in range(CT):
                        m = pe.matmul(ps[:, 2, part * T:(part + 1) * T], w_kr[:, c, part * P:(part + 1) * P],
                                      xnT[:, c, :], start=(c == 0), stop=(c == CT - 1))
                m.then_inc(s_kr_ps.sem, 1)
                s_lat.wait(pe, b, 1)
                s_t2v.wait(pe, b, 0)
                for i in range(TT):
                    m = pe.matmul(b5[:, 0:3], meanw[:, :], lat[:, i, QL + KVL:LC], start=(i == 0),
                                  stop=(i == TT - 1))
                m.then_inc(s_gate_ps.sem, 1)
                s_nlat.wait(pe, b, 4)
                for i in range(TT):
                    m = pe.transpose(bM[:, i * P:(i + 1) * P], nlat[:, i, :], ident[:, :])
                m.then_inc(s_nT_ps.sem, 1)
                s_nT.wait(pe, b, 1)
                for i in range(TT):
                    if i:
                        s_v.wait(pe, b, 1)
                    pe.matmul(ps[:, 0 if i else 3, :], nT[:, i * P:(i + 1) * P], w_v1[:, :], start=True,
                              stop=True).then_inc(s_v_ps.sem, 1)
                s_chosen.wait(pe, b, 2)
                s_srow.wait(pe, b, 1)
                pe.matmul(b4[:, 0:1], uptri[:, 0:P], chosen[:, 0:1], start=True, stop=True)
                pe.matmul(b4[:, 1:2], uptri[:, P:2 * P], chosen[:, 0:1], start=True, stop=False)
                pe.matmul(b4[:, 1:2], uptri[:, 0:P], chosen[:, 1:2], start=False, stop=True)\
                    .then_inc(s_rank_ps.sem, 1)
                s_pick.wait(pe, b, 2)
                s_gexp.wait(pe, b, 1)
                for c in range(CT):
                    for i in range(TT):
                        m = pe.matmul(b5[:, c * KEEP:(c + 1) * KEEP], xn[:, i, c * P:(c + 1) * P],
                                      pick[:, i, :], start=(i == 0), stop=(i == TT - 1))
                m.then_inc(s_selT_ps.sem, 1)
                s_selT.wait(pe, b, 1)
                s_v.wait(pe, b, 2)
                for c in range(CT):
                    m = pe.matmul(ps[0:KEEP, 1, :], selT[:, c, :], w_selv[:, c, :], start=(c == 0),
                                  stop=(c == CT - 1))
                m.then_inc(s_v_ps.sem, 1)
                for g in range(2):
                    for n in range(4):
                        task(b, g, n)
                s_mul.wait(pe, b, 1)
                s_v.wait(pe, b, 5)
                for h in range(HEADS + LAG):
                    if h < HEADS:
                        scores(b, h)
                    if h < 2 * GROUP:
                        task(b, 2 + h // 4, h % 4)
                    if h >= LAG:
                        transposes(b, h - LAG)
                        if (h - LAG) % GROUP == GROUP - 1:
                            values(b, (h - LAG) // GROUP)
                s_ctx.wait(pe, b, 16)
                s_ptb.wait(pe, b, HEADS)
                for f in range(CT):
                    for c in range(CT):
                        m = pe.matmul(b5[:, f * P:f * P + CTX], w_x[:, 1, c, f * P:(f + 1) * P], ctxT[:, c, :],
                                      start=(c == 0), stop=(c == CT - 1))
                m.then_inc(s_k2_ps.sem, 1)
                s_exp.wait(pe, b, 6 * HEADS)
                for c in range(CT):
                    m = pe.matmul(ps[0:CTX, 3, 0:C], ctxT[:, c, :], w_x[:, 2, c, :], start=(c == 0),
                                  stop=(c == CT - 1))
                m.then_inc(s_v2_ps.sem, 1)
                s_o.wait(pe, b, GROUPS)
                s_mul.wait(pe, b, 1 + GROUPS * 3)
                s_copy.wait(pe, b, GROUPS * 3)
                for i in range(TT):
                    for g in range(GROUPS):
                        m = pe.matmul(bM[:, i * C:(i + 1) * C], OT[:, g, i * P:(i + 1) * P], w_proj[:, g, :],
                                      start=(g == 0), stop=(g == GROUPS - 1))
                m.then_inc(s_proj.sem, 1)
                s_xn.wait(pe, b, 4)
                four_transposes(bO, xn, s_xnT_ps)
                s_xnT.wait(pe, b, 2)
                s_pta.wait(pe, b, HEADS)
                for f in range(CT):
                    for c in range(CT):
                        m = pe.matmul(b4[:, f * T:(f + 1) * T], w_x[:, 0, c, f * P:(f + 1) * P], xnT[:, c, :],
                                      start=(c == 0), stop=(c == CT - 1))
                m.then_inc(s_q2_ps.sem, 1)
                s_q2.wait(pe, b, 2)
                s_kbd.wait(pe, b, 2)
                s_v2.wait(pe, b, 2)
                for i in range(TT):
                    if i:
                        s_sub2.wait(pe, b, i)
                    for f in range(CT):
                        for n in range(2):
                            m = pe.matmul(ps[:, 2 * f + n, 0:4 * CTX], q2[:, f, i * P:(i + 1) * P],
                                          Kbd[:, f, 4 * n:4 * n + 4, :].rearrange("p a b -> p (a b)"),
                                          start=True, stop=True)
                    m.then_inc(s_s2.sem, 1)
                for i in range(TT):
                    s_n2.wait(pe, b, i + 1)
                    for n in range(4):
                        k = 4 * i + n
                        bank = (b4, b5)[n % 2]
                        if k >= 2:
                            (s_t2a, s_t2v)[n % 2].wait(pe, b, k // 2)
                        for m4 in range(4):
                            m = pe.transpose(bank[0:CTX, m4 * P:(m4 + 1) * P], P2[:, i, 4 * n + m4, :],
                                             ident[:, :])
                        m.then_inc(s_t2_ps.sem, 1)
                s_t2a.wait(pe, b, 4)
                s_t2v.wait(pe, b, 4)
                for w in range(2):
                    for pair in range(HEADS // 2):
                        j, f = pair % 4, pair // 4
                        m = pe.matmul(bO[32 * j:32 * (j + 1), f * T:(f + 1) * T],
                                      Vz[:, pair, w, :, :].rearrange("p a b -> p (a b)"),
                                      PT2[0:CTX, 2 * pair + w, :], start=(w == 0 and f == 0), stop=(w == 1),
                                      skip_group_check=True)
                m.then_inc(s_o2_ps.sem, 1)
                s_o2.wait(pe, b, 1)
                for i in range(TT):
                    for f in range(CT):
                        m = pe.matmul(bM[:, i * C:(i + 1) * C], O2T[:, f, i * P:(i + 1) * P], w_x[:, 3, f, :],
                                      start=(f == 0), stop=(f == CT - 1))
                m.then_inc(s_y2.sem, 1)
                s_xn.wait(pe, b, 6)
                four_transposes(bO, xn, s_xnT_ps)

        @block.scalar
        def _(act):
            prime(act, s_t2a)
            act.wait_ge(s_w.sem, 16 * len(loads))
            act.wait_ge(s_init.sem, 6)
            act.activation(bq4[:, :], xb[:, 0, :], ACT.Copy, scale=0.25).then_inc(s_init.sem, 1)
            act.wait_ge(s_init.sem, 7)

            def copy(out, src, sig, scale=1.0):
                act.activation(out, src, ACT.Copy, scale=scale).then_inc(sig.sem, 1)

            def nope_copies(b, g, n):
                s_task_ps.wait(act, b, 4 * g + n + 1)
                gg = g % 2
                two = bM.rearrange("p (a t) -> p a t", a=2)
                if n == 1:
                    s_group[gg].wait(act, b, GDMA * (g // 2))
                    act.activation(st[:, gg, 0, BC0:BC0 + T], two[:, 0, :], ACT.Copy)
                    copy(st[:, gg, 0, WC0:WC0 + T], two[:, 1, :], s_copy)
                if n == 3:
                    copy(st[:, gg, 0, QC:QC + T], two[:, 0, :], s_copy, scale=DK ** -0.5)
                    copy(st[:, gg, 0, SC0:SC0 + KEEP], bM[:, T:T + KEEP], s_copy)

            def exps(b, h):
                S = head_scores(h)[:, 64:64 + PCOLS]
                s_max.wait(act, b, 3 * (h + 1))
                if h == 0:
                    s_out.wait(act, b, 0)
                if h >= PBUF:
                    s_pt_ps.wait(act, b, h - PBUF + 1)
                if h >= 2:
                    s_coef.wait(act, b, h - 1)
                for i in (1, 0):
                    for a in (WIN, BASE, SEL):
                        at, width = SEG[i, a]
                        c = 3 * (1 - i) + a
                        act.activation(Pr[:, h % PBUF, at:at + width], S[:, at:at + width], ACT.Exp,
                                       bias=nmax[:, h % 2, c:c + 1], accum_out=rsum[:, h % 2, c:c + 1])\
                            .then_inc(s_exp.sem, 1)

            def evacuate(b, h):
                s_pt_ps.wait(act, b, h + 1)
                act.activation(PT[:, h % GROUP, 2 * T:3 * T], b5[:, 0:T], ACT.Copy)
                copy(PT[0:KEEP, h % GROUP, 3 * T:4 * T], b5[0:KEEP, T:2 * T], s_ptb)

            with act.Fori(0, B) as b:
                s_xnT_ps.wait(act, b, 1)
                copy(xnT[:, :, :].rearrange("p a b -> p (a b)"), bM, s_xnT)
                s_lat_ps.wait(act, b, 1)
                copy(lat[:, :, :], bO.rearrange("p (i c) -> p i c", i=TT)[:, :, 0:LC], s_lat)
                for i in range(TT):
                    s_v_ps.wait(act, b, i + 1)
                    copy(V[:, i, :], ps[:, i, :], s_v)
                s_nT_ps.wait(act, b, 1)
                act.activation(nT[:, :], bM[:, 0:T], ACT.Copy, scale=g_lat[:, 0:1]).then_inc(s_nT.sem, 1)
                s_gmax.wait(act, b, 1)
                act.activation(gexp[:, :], b5[:, 0:3], ACT.Exp, bias=gmax[:, 0:1], accum_out=gsum[:, 0:1])\
                    .then_inc(s_gexp.sem, 1)
                for i in range(TT):
                    s_v_ps.wait(act, b, 3 + i)
                    copy(V[:, 2 + i, :], ps[:, 0 if i else 3, :], s_v)
                s_selT_ps.wait(act, b, 1)
                copy(selT[:, :, :].rearrange("p a b -> p (a b)"), b5[:, 0:CT * KEEP], s_selT)
                s_v_ps.wait(act, b, 5)
                copy(V[0:KEEP, 4, :], ps[0:KEEP, 1, :], s_v)
                for g in range(2):
                    for n in (1, 3):
                        nope_copies(b, g, n)
                for h in range(HEADS + LAG):
                    if h < HEADS:
                        exps(b, h)
                    if h < 2 * GROUP and h % 2 == 1:
                        nope_copies(b, 2 + h // 4, h % 4)
                    if h >= LAG:
                        evacuate(b, h - LAG)
                        if (h - LAG) % GROUP == GROUP - 1:
                            g = (h - LAG) // GROUP
                            s_o_ps.wait(act, b, g + 1)
                            copy(OT[:, g, :], bO[:, 0:T], s_o)
                s_k2_ps.wait(act, b, 1)
                for f in range(CT):
                    act.activation(kT2[:, f, :], b5[:, f * P:f * P + CTX], ACT.Identity,
                                   bias=xb[:, 1, f:f + 1]).then_inc(s_k2.sem, 1)
                s_xnT_ps.wait(act, b, 2)
                copy(xnT[:, :, :].rearrange("p a b -> p (a b)"), bO, s_xnT)
                s_q2_ps.wait(act, b, 1)
                for f in range(CT):
                    act.activation(q2[:, f, :], b4[:, f * T:(f + 1) * T], ACT.Identity,
                                   bias=bq4[:, f:f + 1], scale=0.25).then_inc(s_q2.sem, 1)
                for i in range(TT):
                    s_sub2.wait(act, b, i + 1)
                    p = P2[:, i, :, :].rearrange("p h k -> p (h k)")
                    act.activation(p, p, ACT.Exp).then_inc(s_e2.sem, 1)
                for k in range(0, 8, 2):
                    s_t2_ps.wait(act, b, k + 1)
                    i, n = k // 4, k % 4
                    copy(PT2[0:CTX, 4 * n:4 * n + 4, i * P:(i + 1) * P],
                         b4[0:CTX, :].rearrange("p (h t) -> p h t", h=4), s_t2a)
                s_o2_ps.wait(act, b, 1)
                copy(O2T.rearrange("p a b -> p (a b)"), bO, s_o2)
                s_xnT_ps.wait(act, b, 3)
                copy(hT.rearrange("p a b -> p (a b)"), bO, s_xnT)

        @block.gpsimd
        def _(pool):
            prime(pool, s_rot)
            pool.memset(minus_half[:, :], -0.5).then_inc(s_init.sem, 1)
            pool.memset(PT[:, :, :], 0.0).then_inc(s_init.sem, 1)
            pool.memset(V[:, 4, :], 0.0).then_inc(s_init.sem, 1)
            pool.memset(Vz[:, :, :, :, :], 0.0).then_inc(s_init.sem, 1)
            pool.memset(hmax[:, :], 0.0).then_inc(s_init.sem, 1)
            pool.memset(rot1[:, :, :], 0.0).then_inc(s_init.sem, 1)
            pool.wait_ge(s_w.sem, 16 * len(loads))
            pool.wait_ge(s_init.sem, 6)

            def inverse_root(b, k, out, src, n, ready, done):
                ready.wait(pool, b, k)
                pool.tensor_tensor(out, src, minus_half[:, 0:n], ALU.pow).then_inc(done.sem, 1)

            def rotate(b, k, out, width):
                s_mul.wait(pool, b, k + 1)
                pool.tensor_tensor(out, rot1[:, :, 0:width], rot2[:, :, 0:width], ALU.add)\
                    .then_inc(s_rot.sem, 1)

            def rotations(b, g, n):
                gg = g % 2
                if n == 0 and g >= 2:
                    s_group[gg].wait(pool, b, GDMA * (g // 2))
                at, width = {0: (WC0, T), 2: (QC, T), 3: (SC0, KEEP)}[n]
                rotate(b, {0: 1, 2: 2, 3: 3}[n] + 3 * g, st[:, gg, 1:3, at:at + width], width)

            def scale(b, h):
                s_coef.wait(pool, b, h + 1)
                pool.tensor_tensor(held[:, 1 + h % 2:2 + h % 2], minus_half[:, 0:1], minus_half[:, 1:2], ALU.add)
                for i in (1, 0):
                    for a in (WIN, BASE, SEL):
                        at, width = SEG[i, a]
                        c = 3 * (1 - i) + a
                        p = Pr[:, h % PBUF, at:at + width]
                        pool.tensor_scalar(p, p, coef[:, h % 2, c:c + 1], 1.0, ALU.mult, ALU.mult)\
                            .then_inc(s_pn.sem, 1)

            with pool.Fori(0, B) as b:
                inverse_root(b, 1, rstd[:, :], vareps[:, :], TT, s_ve, s_rstd)
                inverse_root(b, 4, rlat[:, :, :].rearrange("p a b -> p (a b)"),
                             ms[:, :, :].rearrange("p a b -> p (a b)"), 4, s_ms, s_rlat)
                s_out.wait(pool, b, 0)
                for gg in range(2):
                    s_group[gg].wait(pool, b, 0)
                    rotate(b, 0, st[:, gg, 1:3, BC0:BC0 + T], T)
                for g in range(2):
                    for n in (0, 2, 3):
                        rotations(b, g, n)
                for h in range(HEADS + 1):
                    if h:
                        scale(b, h - 1)
                    if h < 2 * GROUP and h % 4 != 1:
                        rotations(b, 2 + h // 4, h % 4)
                for f in range(CT):
                    s_k2.wait(pool, b, f + 1)
                    pool.tensor_tensor(Kbd[:, f, :, :], kT2[:, f:f + 1, :].to_broadcast([P, XH, CTX]),
                                       own16[:, :].unsqueeze(2).to_broadcast([P, XH, CTX]), ALU.mult)\
                        .then_inc(s_kbd.sem, 1)
                inverse_root(b, 2, rstd[:, :], vareps[:, :], TT, s_ve, s_rstd)
                for i in range(TT):
                    s_x1.wait(pool, b, i + 1)
                    pool.tensor_tensor(x1b[:, i, :], x1[:, i, :], xrow[:, 1, :], ALU.add)\
                        .then_inc(s_x1b.sem, 1)
                for i in range(TT):
                    s_r2.wait(pool, b, 2 * i + 2)
                    pool.tensor_tensor(P2[:, i, :, :], P2[:, i, :, :],
                                       ri2[:, :].unsqueeze(2).to_broadcast([P, HEADS, CTX]), ALU.mult)\
                        .then_inc(s_n2.sem, 1)
                inverse_root(b, 3, rstd[:, :], vareps[:, :], TT, s_ve, s_rstd)

        @block.vector
        def _(dve):
            prime(dve, s_sub2, s_t2v, s_x1, s_x2)
            dve.wait_ge(s_w.sem, 16 * len(loads))
            dve.wait_ge(s_init.sem, 6)

            def layer_norm(b, k, src):
                for i in range(TT):
                    dve.bn_stats(stats[:, i, :], src[:, i, :]).then_inc(s_stat.sem, 1)
                s_stat.wait(dve, b, 2 * k + 2)
                dve.tensor_copy(held[:, 0:1], stats[:, 0, 0:1]).then_inc(s_held.sem, 1)
                for i in range(TT):
                    dve.bn_aggr(meanvar[:, i, :], stats[:, i, :]).then_inc(s_mv.sem, 1)
                s_mv.wait(dve, b, 2 * k + 2)
                dve.tensor_scalar(vareps[:, :], meanvar[:, :, 1], LN_EPS, None, ALU.add).then_inc(s_ve.sem, 1)
                s_rstd.wait(dve, b, k + 1)
                for i in range(TT):
                    dve.tensor_scalar(xn[:, i, :], src[:, i, :], meanvar[:, i, 0:1], rstd[:, i:i + 1],
                                      ALU.subtract, ALU.mult).then_inc(s_xn.sem, 1)

            def products(b, k, src, table, width, scale=None):
                s_rot.wait(dve, b, k + (k > 0))
                cos = table[:, 0:1, 0:width].to_broadcast([P, 2, width])
                sin = table[:, 1, 0:width]
                one = 1.0 if scale is None else scale
                dve.scalar_tensor_tensor(rot1[:, :, 0:width], src, one, cos, ALU.mult, ALU.mult)
                dve.scalar_tensor_tensor(rot2[:, 0, 0:width], src[:, 1, :], -one, sin, ALU.mult, ALU.mult)
                dve.scalar_tensor_tensor(rot2[:, 1, 0:width], src[:, 0, :], one, sin, ALU.mult, ALU.mult)\
                    .then_inc(s_mul.sem, 1)

            def group_products(b, g, n):
                s_task_ps.wait(dve, b, 4 * g + n + 1)
                two = bM.rearrange("p (a t) -> p a t", a=2)
                if n == 0:
                    products(b, 1 + 3 * g, two, rope_k, T)
                if n == 2:
                    products(b, 2 + 3 * g, two, rope_q, T)
                if n == 3:
                    s_copy.wait(dve, b, 3 * (g + 1))
                    products(b, 3 + 3 * g, bM[:, T + KEEP:T + 3 * KEEP].rearrange("p (a t) -> p a t", a=2),
                             rope_k, KEEP)

            def maxima(b, h):
                S = head_scores(h)
                s_s.wait(dve, b, h + 1)
                if h >= 2:
                    s_exp.wait(dve, b, 6 * (h - 1))
                m = nmax[:, h % 2, :]
                both = lambda at, n, apart: S[:, at:at + 2 * apart].rearrange("p (a k) -> p a k", k=apart)[:, :, 0:n]
                dve.tensor_reduce(m[:, 0:2], both(S1, T, T + KEEP), AX.X, ALU.max, negate=True)\
                    .then_inc(s_max.sem, 1)
                dve.tensor_reduce(m[:, 3:5], both(S0, P, P + KEEP), AX.X, ALU.max, negate=True)\
                    .then_inc(s_max.sem, 1)
                sel = S[:, S1 + T:S0 + P + KEEP].rearrange("p (a k) -> p a k", k=KEEP)
                dve.tensor_reduce(m[:, 2:6:3], sel[:, 0:8:7, :], AX.X, ALU.max, negate=True)\
                    .then_inc(s_max.sem, 1)

            def coefficients(b, h):
                s_exp.wait(dve, b, 6 * (h + 1))
                if h >= 2:
                    s_pn.wait(dve, b, 6 * (h - 1))
                dve.reciprocal(rinv[:, h % 2, :], rsum[:, h % 2, :]).then_inc(s_rinv.sem, 1)
                s_rinv.wait(dve, b, h + 1)
                dve.tensor_tensor(coef[:, h % 2, :].rearrange("p (a k) -> p a k", a=2),
                                  rinv[:, h % 2, :].rearrange("p (a k) -> p a k", a=2),
                                  gate[:, :].unsqueeze(1).to_broadcast([P, 2, 3]), ALU.mult)\
                    .then_inc(s_coef.sem, 1)

            def evacuate(b, h):
                s_pt_ps.wait(dve, b, h + 1)
                dve.tensor_copy(PT[:, h % GROUP, 0:2 * T], b4).then_inc(s_pta.sem, 1)

            with dve.Fori(0, B) as b:
                s_x.wait(dve, b, 16)
                layer_norm(b, 0, xin)
                s_lat.wait(dve, b, 1)
                for i in range(TT):
                    for n, (a, z) in enumerate(((0, QL), (QL, QL + KVL))):
                        if 2 * i + n >= 1:
                            s_ms.wait(dve, b, 2 * i + n)
                        dve.tensor_tensor_reduce(sq[:, 0, 0:z - a], lat[:, i, a:z], lat[:, i, a:z],
                                                 1.0 / (z - a), RMS_EPS, ALU.mult, ALU.add,
                                                 ms[:, i, n:n + 1]).then_inc(s_ms.sem, 1)
                s_srow_ps.wait(dve, b, 1)
                dve.tensor_copy(srow[:, :], b4[:, 0:T]).then_inc(s_srow.sem, 1)
                s_rlat.wait(dve, b, 1)
                for i in range(TT):
                    for n, (a, z) in enumerate(((0, QL), (QL, QL + KVL))):
                        dve.tensor_scalar(nlat[:, i, a:z], lat[:, i, a:z], rlat[:, i, n:n + 1], None,
                                          ALU.mult).then_inc(s_nlat.sem, 1)
                s_srow.wait(dve, b, 1)
                for i in range(TT):
                    dve.tensor_tensor_reduce(junk[:, i, 0:P], srow[:, i * P:(i + 1) * P], ident[:, :], 1.0,
                                             0.0, ALU.mult, ALU.add, scol[:, i:i + 1]).then_inc(s_scol.sem, 1)
                s_gate_ps.wait(dve, b, 1)
                dve.tensor_reduce(gmax[:, :], b5[:, 0:3], AX.X, ALU.max, negate=True).then_inc(s_gmax.sem, 1)
                s_scol.wait(dve, b, 2)
                for i in range(TT):
                    dve.tensor_scalar(junk[:, i, :], srow[:, :], scol[:, i:i + 1], None, ALU.is_equal)\
                        .then_inc(s_rankop.sem, 1)
                for i in range(TT):
                    s_rankop.wait(dve, b, i + 1)
                    dve.tensor_tensor_reduce(junk[:, i, :], junk[:, i, :], before[:, i, :], 1.0, 0.0,
                                             ALU.mult, ALU.add, tie[:, i:i + 1]).then_inc(s_rankop.sem, 1)
                for i in range(TT):
                    s_rankop.wait(dve, b, 3 + i)
                    dve.tensor_scalar(junk[:, i, :], srow[:, :], scol[:, i:i + 1], None, ALU.is_gt)\
                        .then_inc(s_rankop.sem, 1)
                for i in range(TT):
                    s_rankop.wait(dve, b, 5 + i)
                    dve.tensor_reduce(cnt[:, i:i + 1], junk[:, i, :], AX.X, ALU.add)\
                        .then_inc(s_rankop.sem, 1)
                for i in range(TT):
                    s_rankop.wait(dve, b, 7 + i)
                    dve.tensor_scalar(chosen[:, i:i + 1], cnt[:, i:i + 1], tie[:, i:i + 1], KEEP - 0.5,
                                      ALU.add, ALU.is_lt).then_inc(s_chosen.sem, 1)
                s_gexp.wait(dve, b, 1)
                dve.reciprocal(ginv[:, :], gsum[:, :]).then_inc(s_ginv.sem, 1)
                s_ginv.wait(dve, b, 1)
                dve.tensor_scalar(gate[:, :], gexp[:, :], ginv[:, 0:1], None, ALU.mult).then_inc(s_gate.sem, 1)
                s_kr_ps.wait(dve, b, 1)
                products(b, 0, ps[:, 2, :].rearrange("p (a t) -> p a t", a=2), rope_k, T, scale=1.0 / HEADS)
                s_rank_ps.wait(dve, b, 1)
                dve.tensor_copy(rank[:, :], b4[:, 0:2]).then_inc(s_rank.sem, 1)
                s_rank.wait(dve, b, 1)
                for i in range(TT):
                    dve.tensor_scalar(pick[:, i, :], iota64[:, :], rank[:, i:i + 1], chosen[:, i:i + 1],
                                      ALU.is_equal, ALU.mult).then_inc(s_pick.sem, 1)
                s_gate.wait(dve, b, 1)
                for g in range(2):
                    for n in (0, 2, 3):
                        group_products(b, g, n)
                for h in range(HEADS + LAG):
                    if h < HEADS:
                        maxima(b, h)
                    if 1 <= h <= HEADS:
                        coefficients(b, h - 1)
                    if h < 2 * GROUP and h % 4 != 1:
                        group_products(b, 2 + h // 4, h % 4)
                    if h >= LAG:
                        evacuate(b, h - LAG)
                s_v2_ps.wait(dve, b, 1)
                for w in range(2):
                    dve.tensor_tensor(Vz[:, :, w, w, :],
                                      ps[0:CTX, 3, 0:C].rearrange("p (a w d) -> p a w d", w=2, d=XD)[:, :, w, :],
                                      xrow[0:CTX, 0, :].rearrange("p (a w d) -> p a w d", w=2, d=XD)[:, :, w, :],
                                      ALU.add).then_inc(s_v2.sem, 1)
                s_proj.wait(dve, b, 1)
                for i in range(TT):
                    dve.tensor_tensor(x1[:, i, :], bM[:, i * C:(i + 1) * C], xin[:, i, :], ALU.add)\
                        .then_inc(s_x1.sem, 1)
                s_x1.wait(dve, b, 2)
                layer_norm(b, 1, x1)
                for i in range(TT):
                    s_s2.wait(dve, b, i + 1)
                    S = ps[:, 0:4, 0:4 * CTX].rearrange("p f (h k) -> p f h k", k=CTX)
                    dve.tensor_reduce(nmax2[:, :].rearrange("p (f h) -> p f h", f=4), S, AX.X, ALU.max,
                                      negate=True).then_inc(s_m2.sem, 1)
                    s_m2.wait(dve, b, i + 1)
                    if i == 0:
                        s_pt_ps.wait(dve, b, HEADS)
                    dve.tensor_tensor(P2[:, i, :, :].rearrange("p (f h) k -> p f h k", f=4), S,
                                      nmax2[:, :].rearrange("p (f h) -> p f h", f=4).unsqueeze(3)
                                      .to_broadcast([P, 4, 4, CTX]), ALU.add).then_inc(s_sub2.sem, 1)
                    if i:
                        s_sub2.wait(dve, b, i + 1)
                for i in range(TT):
                    s_e2.wait(dve, b, i + 1)
                    if i:
                        s_n2.wait(dve, b, i)
                    dve.tensor_reduce(rs2[:, :], P2[:, i, :, :], AX.X, ALU.add).then_inc(s_r2.sem, 1)
                    s_r2.wait(dve, b, 2 * i + 1)
                    dve.reciprocal(ri2[:, :], rs2[:, :]).then_inc(s_r2.sem, 1)
                for k in range(1, 8, 2):
                    s_t2_ps.wait(dve, b, k + 1)
                    i, n = k // 4, k % 4
                    dve.tensor_copy(PT2[0:CTX, 4 * n:4 * n + 4, i * P:(i + 1) * P],
                                    b5[0:CTX, :].rearrange("p (h t) -> p h t", h=4)).then_inc(s_t2v.sem, 1)
                s_y2.wait(dve, b, 1)
                s_out.wait(dve, b, 0)
                for i in range(TT):
                    s_x1b.wait(dve, b, i + 1)
                    dve.tensor_tensor(x2[:, i, :], bM[:, i * C:(i + 1) * C], x1b[:, i, :], ALU.add)\
                        .then_inc(s_x2.sem, 1)
                s_x2.wait(dve, b, 2)
                layer_norm(b, 2, x2)
                s_xn.wait(dve, b, 6)
                dve.tensor_reduce(hm[:, :], xn[:, :, :].rearrange("p a b -> p (a b)"), AX.X, ALU.max,
                                  apply_absolute_value=True).then_inc(s_hm.sem, 1)
                s_hm.wait(dve, b, 1)
                dve.tensor_tensor(hmax[:, :], hmax[:, :], hm[:, :], ALU.max).then_inc(s_hmax.sem, 1)
                s_xnT_ps.wait(dve, b, 3)


def phase2(nc, io, h_dram, x2_dram, u_dram, ident, hmax):
    with ExitStack() as ctx:
        def sb(name, shape, dt=F32):
            return ctx.enter_context(nc.sbuf_tensor(name, shape, dt))

        def signal(name, per=1, first=0):
            return Signal(ctx.enter_context(nc.semaphore("s_" + name)), per, first)

        def prime(eng, *signals):
            for s in signals:
                eng.sem_inc(s.sem, s.first)

        NB = INNER * C // P // BLK
        WC = INNER * C // P
        G = sb("G", [P, B, IT * T])
        wT = [sb("wgT", [P, CT, INNER]), sb("wuT", [P, CT, INNER]), sb("wdT", [P, IT, C])]
        wn = sb("wn", [P, WC])
        wq = sb("wq", [P, WC])
        wmax = sb("wmax", [P, NB])
        wscale = sb("wscale", [P, NB])
        winv = sb("winv", [P, NB])
        hin = sb("hin", [P, 2, CT * T])
        hq = sb("hq", [P, 2, CT * T])
        ubuf = sb("ubuf", [P, 2, IT * T])
        t1 = sb("t1", [P, IT * T])
        t2 = sb("t2", [P, IT * T])
        t3 = sb("t3", [P, IT * T])
        am = sb("am", [P, IT, 2])
        amc = sb("amc", [P, 2])
        held = sb("held2", [P, 1])
        run = sb("run", [P, 4])
        tot = sb("tot", [P, 5])
        sc = sb("sc", [P, 5])
        raw = sb("raw", [P, 5])
        inv = sb("inv", [P, 5])
        tmp = sb("tmp", [P, 5])
        xres = sb("xres", [P, 2, TT * C])
        yout = sb("yout", [P, 2, TT * C])
        ps = ctx.enter_context(nc.psum_tensor("ps2", [P, 8, 512], F32))
        GATE, UP, PROD, OUTQ, INP = range(5)

        s_wn = signal("w_loaded", 0)
        s_wop = signal("w_ops", 0)
        s_wt_ps = signal("wT_ps", 0)
        s_wt = signal("wT", 0)
        s_tot = signal("total_max", 0)
        s_sc = signal("scale_ops", 0)
        s_zero = signal("zeroed", 0)
        s_h = signal("h_loaded", 32)
        s_hr = signal("h_raised", 2, first=1)
        s_hq = signal("h_quantised", 2, first=1)
        s_gu_ps = signal("gu_ps", 2 * IT, first=1)
        s_gu = signal("gu_copied", 2 * IT, first=1)
        s_gum = signal("gu_max", 2 * IT, first=1)
        s_amc = signal("a_block_max", 2)
        s_run_a = signal("a_running", 2)
        s_ust = signal("u_stored", 32, first=1)
        s_gr = signal("g_raised", 1)
        s_gq = signal("g_quantised", 1)
        s_sig = signal("sigmoid", 1)
        s_sr = signal("sigmoid_raised", 1)
        s_sqz = signal("sigmoid_quantised", 1)
        s_gp = signal("g_product", 1, first=1)
        s_bm = signal("b_block_max", 1)
        s_run_b = signal("b_running", 1)
        s_u = signal("u_loaded", 16)
        s_ur = signal("u_raised", 1, first=1)
        s_uq = signal("u_quantised", 1)
        s_pr = signal("p_raised", 1)
        s_pq = signal("p_quantised", 1)
        s_op = signal("o_product", 1, first=1)
        s_cm = signal("c_block_max", 1)
        s_run_c = signal("c_running", 1)
        s_or = signal("o_raised", 2)
        s_oq = signal("o_quantised", 2)
        s_xr = signal("x_loaded2", 32)
        s_y_ps = signal("y_ps", 4, first=1)
        s_y = signal("y", 4, first=1)
        s_yst = signal("y_stored", 32, first=1)

        block = ctx.enter_context(nc.Block())
        names = ["ffn_gate", "ffn_up", "ffn_down"]

        def at_block(eng_block):
            return G[:, bass.ds(eng_block, 1), :].rearrange("p o c -> p (o c)")

        @block.sync
        def _(sp):
            prime(sp, s_ust, s_yst)
            for n, name in enumerate(names):
                if n:
                    sp.wait_ge(s_wop.sem, 8 * n)
                sp.dma_start(wn[:, :], io[name]).then_inc(s_wn.sem, 16)
            with sp.Fori(0, B // 2) as bb:
                for k in range(2):
                    s_hr.wait(sp, bb, 0)
                    sp.dma_start(hin[:, k, :], h_dram[bass.ds(bb * 2 + k, 1)].rearrange("o p c -> p (o c)"))\
                        .then_inc(s_h.sem, 16)
                for k in range(2):
                    s_gu.wait(sp, bb, IT * (k + 1))
                    sp.dma_start(u_dram[bass.ds(bb * 2 + k, 1)].rearrange("o p c -> p (o c)"), ubuf[:, k, :])\
                        .then_inc(s_ust.sem, 16)
            s_ust.wait_all(sp, B // 2)
            with sp.Fori(0, B) as c:
                s_ur.wait(sp, c, 0)
                sp.dma_start(ubuf[:, 0, :], u_dram[bass.ds(c, 1)].rearrange("o p c -> p (o c)"))\
                    .then_inc(s_u.sem, 16)
            with sp.Fori(0, B // 2) as bb:
                for k in range(2):
                    s_y.wait(sp, bb, 0)
                    sp.dma_start(xres[:, k, :], x2_dram[bass.ds(bb * 2 + k, 1)].rearrange("o p c -> p (o c)"))\
                        .then_inc(s_xr.sem, 16)
                for k in range(2):
                    s_y.wait(sp, bb, 2 * (k + 1))
                    sp.dma_start(io["out"][bass.ds(bb * 2 + k, 1)].rearrange("o (i p) c -> p (o i) c", p=P),
                                 yout[:, k, :].rearrange("p (i c) -> p i c", i=TT)).then_inc(s_yst.sem, 16)
            s_yst.wait_all(sp, B // 2)

        @block.gpsimd
        def _(pool):
            pool.memset(run[:, :], 0.0).then_inc(s_zero.sem, 1)
            red = bass.bass_isa.ReduceOp.max
            pool.partition_all_reduce(tot[:, INP:INP + 1], hmax[:, :], P, red).then_inc(s_tot.sem, 1)
            s_run_a.wait_all(pool, B // 2)
            pool.partition_all_reduce(tot[:, GATE:UP + 1], run[:, GATE:UP + 1], P, red).then_inc(s_tot.sem, 1)
            s_run_b.wait_all(pool, B)
            pool.partition_all_reduce(tot[:, PROD:PROD + 1], run[:, PROD:PROD + 1], P, red)\
                .then_inc(s_tot.sem, 1)
            s_run_c.wait_all(pool, B)
            pool.partition_all_reduce(tot[:, OUTQ:OUTQ + 1], run[:, OUTQ:OUTQ + 1], P, red)\
                .then_inc(s_tot.sem, 1)

        @block.tensor
        def _(pe):
            prime(pe, s_gu_ps, s_y_ps)
            for n in range(3):
                pe.wait_ge(s_wop.sem, 8 * (n + 1))
                rows, cols = ((IT, CT), (IT, CT), (CT, IT))[n]
                w = wq[:, :].rearrange("p (r c) -> p r c", r=rows)
                order = [(r, c) for c in range(cols) for r in range(rows)]
                for k, (r, c) in enumerate(order):
                    q = 12 * n + k
                    if q >= 8 and k % 4 == 0:
                        pe.wait_ge(s_wt.sem, q // 4 - 1)
                    m = pe.transpose(ps[:, (q // 4) % 2, (q % 4) * P:(q % 4 + 1) * P],
                                     w[:, r, c * P:(c + 1) * P], ident[:, :])
                    if k % 4 == 3:
                        m.then_inc(s_wt_ps.sem, 1)
            pe.wait_ge(s_wt.sem, 9)
            with pe.Fori(0, B // 2) as bb:
                for k in range(2):
                    s_hq.wait(pe, bb, k + 1)
                    for it in range(IT):
                        n = k * IT + it
                        if n >= 6:
                            s_gu.wait(pe, bb, n - 5)
                            s_gum.wait(pe, bb, n - 5)
                        elif n == 0:
                            s_gu.wait(pe, bb, 0)
                            s_gum.wait(pe, bb, 0)
                        for w in range(2):
                            for c in range(CT):
                                m = pe.matmul(ps[:, n % 6, w * T:(w + 1) * T],
                                              wT[w][:, c, it * P:(it + 1) * P],
                                              hq[:, k, c * T:(c + 1) * T], start=(c == 0), stop=(c == CT - 1))
                        m.then_inc(s_gu_ps.sem, 1)
            with pe.Fori(0, B // 2) as bb:
                for k in range(2):
                    s_oq.wait(pe, bb, k + 1)
                    for i in range(TT):
                        n = 2 * k + i
                        if n == 0:
                            s_y.wait(pe, bb, 0)
                        for it in range(IT):
                            m = pe.matmul(ps[:, n, 0:C], (t2, t3)[k][:, it * T + i * P:it * T + (i + 1) * P],
                                          wT[2][:, it, :], start=(it == 0), stop=(it == IT - 1))
                        m.then_inc(s_y_ps.sem, 1)

        def raised(act, out, src, stage, sig):
            act.activation(out, src, ACT.Copy, scale=inv[:, stage:stage + 1], bias=MAGIC).then_inc(sig.sem, 1)

        @block.scalar
        def _(act):
            prime(act, s_gu, s_hr, s_ur)
            for q in range(9):
                act.wait_ge(s_wt_ps.sem, q + 1)
                n, k = q // 3, q % 3
                flat = wT[n][:, :, :].rearrange("p a b -> p (a b)")
                act.activation(flat[:, k * 512:(k + 1) * 512], ps[:, q % 2, :], ACT.Copy)\
                    .then_inc(s_wt.sem, 1)
            act.wait_ge(s_sc.sem, 4)
            with act.Fori(0, B // 2) as bb:
                s_h.wait(act, bb, 32)
                for k in range(2):
                    s_hq.wait(act, bb, 0)
                    raised(act, t1[:, k * CT * T:(k + 1) * CT * T], hin[:, k, :], INP, s_hr)
                for k in range(2):
                    for it in range(IT):
                        n = k * IT + it
                        s_gu_ps.wait(act, bb, n + 1)
                        if it == 0:
                            s_ust.wait(act, bb, 0)
                        act.activation(at_block(bb * 2 + k)[:, it * T:(it + 1) * T], ps[:, n % 6, 0:T], ACT.Copy)
                        act.activation(ubuf[:, k, it * T:(it + 1) * T], ps[:, n % 6, T:2 * T], ACT.Copy)\
                            .then_inc(s_gu.sem, 1)
            act.wait_ge(s_sc.sem, 12)
            with act.Fori(0, B) as c:
                s_gp.wait(act, c, 0)
                raised(act, t1[:, :], at_block(c), GATE, s_gr)
                s_gq.wait(act, c, 1)
                act.activation(t2[:, :], t1[:, :], ACT.Sigmoid, scale=sc[:, GATE:GATE + 1]).then_inc(s_sig.sem, 1)
                s_sig.wait(act, c, 1)
                act.activation(t2[:, :], t2[:, :], ACT.Copy, scale=65536.0, bias=MAGIC).then_inc(s_sr.sem, 1)
            act.wait_ge(s_sc.sem, 18)
            with act.Fori(0, B) as c:
                s_op.wait(act, c, 0)
                s_u.wait(act, c, 16)
                raised(act, t1[:, :], ubuf[:, 0, :], UP, s_ur)
                raised(act, t2[:, :], at_block(c), PROD, s_pr)
            act.wait_ge(s_sc.sem, 24)
            with act.Fori(0, B // 2) as bb:
                for k in range(2):
                    s_y_ps.wait(act, bb, 0)
                    raised(act, (t2, t3)[k][:, :], at_block(bb * 2 + k), OUTQ, s_or)

        @block.vector
        def _(dve):
            prime(dve, s_gp, s_gum, s_hq, s_op, s_y)
            for n in range(3):
                k = 8 * n
                op = lambda ins: ins.then_inc(s_wop.sem, 1)
                wb = wn[:, :].rearrange("p (n e) -> p n e", e=BLK)
                qb = wq[:, :].rearrange("p (n e) -> p n e", e=BLK)
                dve.wait_ge(s_wn.sem, 16 * (n + 1))
                if n:
                    dve.wait_ge(s_wt_ps.sem, 3 * n)
                op(dve.tensor_reduce(wmax[:, :], wb, AX.X, ALU.max, apply_absolute_value=True))
                dve.wait_ge(s_wop.sem, k + 1)
                op(dve.tensor_scalar(wscale[:, :], wmax[:, :], 1.0 / 7.0, 1e-12, ALU.mult, ALU.max))
                dve.wait_ge(s_wop.sem, k + 2)
                op(dve.reciprocal(winv[:, :], wscale[:, :]))
                dve.wait_ge(s_wop.sem, k + 3)
                bc = lambda a: a[:, :].unsqueeze(2).to_broadcast([P, NB, BLK])
                op(dve.tensor_tensor(qb, wb, bc(winv), ALU.mult))
                dve.wait_ge(s_wop.sem, k + 4)
                op(dve.tensor_scalar(wq[:, :], wq[:, :], MAGIC, None, ALU.add))
                dve.wait_ge(s_wop.sem, k + 5)
                op(dve.tensor_scalar(wq[:, :], wq[:, :], MAGIC, 7.0, ALU.subtract, ALU.min))
                dve.wait_ge(s_wop.sem, k + 6)
                op(dve.tensor_scalar(wq[:, :], wq[:, :], -8.0, None, ALU.max))
                dve.wait_ge(s_wop.sem, k + 7)
                op(dve.tensor_tensor(qb, qb, bc(wscale), ALU.mult))

            def scales(first, stage, unit):
                n = first
                t, s, v = tot[:, stage:stage + 1], sc[:, stage:stage + 1], inv[:, stage:stage + 1]
                m = tmp[:, stage:stage + 1]
                if unit is None:
                    dve.tensor_scalar(m, t, 1.0, None, ALU.mult).then_inc(s_sc.sem, 1)
                else:
                    dve.tensor_scalar(m, t, unit, None, ALU.mult).then_inc(s_sc.sem, 1)
                dve.wait_ge(s_sc.sem, n + 1)
                dve.tensor_scalar(s, m, 1.0 / QMAX, 1e-12, ALU.mult, ALU.max).then_inc(s_sc.sem, 1)
                dve.wait_ge(s_sc.sem, n + 2)
                dve.reciprocal(v, s).then_inc(s_sc.sem, 1)
                dve.wait_ge(s_sc.sem, n + 3)
                if unit is None:
                    dve.tensor_scalar(v, v, 1.0, None, ALU.mult).then_inc(s_sc.sem, 1)
                else:
                    dve.tensor_scalar(v, v, unit, None, ALU.mult).then_inc(s_sc.sem, 1)
                return n + 4

            dve.wait_ge(s_zero.sem, 1)
            dve.wait_ge(s_tot.sem, 1)
            n = scales(0, INP, None)
            dve.wait_ge(s_sc.sem, n)
            with dve.Fori(0, B // 2) as bb:
                for k in range(2):
                    s_hr.wait(dve, bb, k + 1)
                    s_gu_ps.wait(dve, bb, 0)
                    dve.tensor_scalar(hq[:, k, :], t1[:, k * CT * T:(k + 1) * CT * T], MAGIC, QMAX,
                                      ALU.subtract, ALU.min).then_inc(s_hq.sem, 1)
                for k in range(2):
                    if k:
                        s_amc.wait(dve, bb, k)
                    for it in range(IT):
                        n_ = k * IT + it
                        s_gu_ps.wait(dve, bb, n_ + 1)
                        s_gu.wait(dve, bb, n_ + 1)
                        dve.tensor_reduce(am[:, it, :], ps[:, n_ % 6, :].rearrange("p (a t) -> p a t", a=2),
                                          AX.X, ALU.max, apply_absolute_value=True).then_inc(s_gum.sem, 1)
                    s_gum.wait(dve, bb, (k + 1) * IT)
                    dve.tensor_reduce(amc[:, :], am[:, :, :].rearrange("p i a -> p a i"), AX.X, ALU.max)\
                        .then_inc(s_amc.sem, 1)
                    s_amc.wait(dve, bb, k + 1)
                    dve.tensor_tensor(run[:, 0:2], run[:, 0:2], amc[:, :], ALU.max).then_inc(s_run_a.sem, 1)
                    s_run_a.wait(dve, bb, k + 1)
            dve.wait_ge(s_tot.sem, 2)
            n = scales(4, GATE, sc[:, INP:INP + 1])
            n = scales(n, UP, sc[:, INP:INP + 1])
            dve.wait_ge(s_sc.sem, n)
            with dve.Fori(0, B) as c:
                s_gr.wait(dve, c, 1)
                dve.tensor_scalar(t1[:, :], t1[:, :], MAGIC, QMAX, ALU.subtract, ALU.min).then_inc(s_gq.sem, 1)
                s_sr.wait(dve, c, 1)
                dve.tensor_scalar(t2[:, :], t2[:, :], MAGIC, 65535.0, ALU.subtract, ALU.min)\
                    .then_inc(s_sqz.sem, 1)
                s_sqz.wait(dve, c, 1)
                dve.tensor_tensor(at_block(c), t1[:, :], t2[:, :], ALU.mult).then_inc(s_gp.sem, 1)
                s_gp.wait(dve, c, 1)
                dve.tensor_copy(held[:, :], run[:, 0:1])
                dve.tensor_reduce(amc[:, 0:1], at_block(c), AX.X, ALU.max, apply_absolute_value=True)\
                    .then_inc(s_bm.sem, 1)
                s_bm.wait(dve, c, 1)
                dve.tensor_tensor(run[:, PROD:PROD + 1], run[:, PROD:PROD + 1], amc[:, 0:1], ALU.max)\
                    .then_inc(s_run_b.sem, 1)
                s_run_b.wait(dve, c, 1)
            dve.wait_ge(s_tot.sem, 3)
            dve.tensor_scalar(raw[:, PROD:PROD + 1], sc[:, GATE:GATE + 1], 1.0 / 65536.0, None, ALU.mult)\
                .then_inc(s_sc.sem, 1)
            dve.wait_ge(s_sc.sem, 13)
            n = scales(13, PROD, raw[:, PROD:PROD + 1])
            dve.wait_ge(s_sc.sem, n)
            dve.tensor_scalar(raw[:, OUTQ:OUTQ + 1], sc[:, PROD:PROD + 1], sc[:, UP:UP + 1], None, ALU.mult)\
                .then_inc(s_sc.sem, 1)
            with dve.Fori(0, B) as c:
                s_ur.wait(dve, c, 1)
                dve.tensor_scalar(t1[:, :], t1[:, :], MAGIC, QMAX, ALU.subtract, ALU.min).then_inc(s_uq.sem, 1)
                s_pr.wait(dve, c, 1)
                dve.tensor_scalar(t2[:, :], t2[:, :], MAGIC, QMAX, ALU.subtract, ALU.min).then_inc(s_pq.sem, 1)
                s_uq.wait(dve, c, 1)
                s_pq.wait(dve, c, 1)
                dve.tensor_tensor(at_block(c), t1[:, :], t2[:, :], ALU.mult).then_inc(s_op.sem, 1)
                s_op.wait(dve, c, 1)
                dve.tensor_copy(held[:, :], run[:, 0:1])
                dve.tensor_reduce(amc[:, 0:1], at_block(c), AX.X, ALU.max, apply_absolute_value=True)\
                    .then_inc(s_cm.sem, 1)
                s_cm.wait(dve, c, 1)
                dve.tensor_tensor(run[:, OUTQ:OUTQ + 1], run[:, OUTQ:OUTQ + 1], amc[:, 0:1], ALU.max)\
                    .then_inc(s_run_c.sem, 1)
                s_run_c.wait(dve, c, 1)
            dve.wait_ge(s_tot.sem, 4)
            dve.wait_ge(s_sc.sem, 18)
            n = scales(18, OUTQ, raw[:, OUTQ:OUTQ + 1])
            dve.wait_ge(s_sc.sem, n)
            dve.tensor_scalar(tmp[:, 0:2], sc[:, 0:2], 1.0, None, ALU.mult).then_inc(s_sc.sem, 1)
            dve.tensor_scalar(tmp[:, 2:4], sc[:, 0:2], 1.0, None, ALU.mult).then_inc(s_sc.sem, 1)
            with dve.Fori(0, B // 2) as bb:
                for k in range(2):
                    s_or.wait(dve, bb, k + 1)
                    t = (t2, t3)[k]
                    dve.tensor_scalar(t[:, :], t[:, :], MAGIC, QMAX, ALU.subtract, ALU.min)\
                        .then_inc(s_oq.sem, 1)
                s_xr.wait(dve, bb, 32)
                s_yst.wait(dve, bb, 0)
                for k in range(2):
                    for i in range(TT):
                        s_y_ps.wait(dve, bb, 2 * k + i + 1)
                        dve.scalar_tensor_tensor(yout[:, k, i * C:(i + 1) * C], ps[:, 2 * k + i, 0:C],
                                                 sc[:, OUTQ:OUTQ + 1], xres[:, k, i * C:(i + 1) * C],
                                                 ALU.mult, ALU.add).then_inc(s_y.sem, 1)



def _layouts(i):
    f = np.float32

    def rows(w):
        return w.reshape(w.shape[0] // P, P, -1).transpose(1, 0, 2)

    def below(w, first):
        out = np.zeros((P, w.shape[1]), f)
        out[first:first + w.shape[0]] = w
        return out

    def grouped(nope, rope):
        n = nope.shape[0]
        both = np.concatenate([nope.reshape(n, HEADS, 1, PART), rope.reshape(n, HEADS, 2, PART)], axis=2)
        return both.reshape(n, GROUPS, GROUP, PARTS, PART).transpose(0, 1, 3, 2, 4).reshape(n, -1)

    def split(w):
        w = w.reshape(w.shape[0], HEADS, DK)
        return grouped(w[:, :, :PART], w[:, :, PART:])

    a = {k: np.asarray(v) for k, v in i.items()}
    att = lambda n: a["L0_attn_" + n]
    xat = lambda n: a["L0_xattn_" + n]
    t = np.arange(T, dtype=f)
    freq = (1.0 / np.power(f(10000.0), np.arange(0, 2 * PART, 2, dtype=f) / f(2 * PART))).astype(f)
    angle = np.outer(t, freq).astype(f)
    cos, sin = np.cos(angle).T, np.sin(angle).T
    table = np.stack([np.tile(cos, (GROUP, 1)), np.tile(sin, (GROUP, 1))], 1).astype(f)
    p = np.arange(P)
    mask = np.where(p[None, :] > p[:, None], MASKED, 0.0).astype(f)
    kr = att("w_krope")
    bf = mybir.dt.np(BF16)
    return {
        "x": a["x"],
        "ctxT": a["ctx_1024"].transpose(0, 2, 1),
        "w_lat": rows(np.concatenate([att("w_cq"), att("w_ckv"), att("w_gate")[:, GATE_ORDER]], axis=1)),
        "w_imp": rows(np.tile(att("w_imp"), (1, P))),
        "w_win": rows(split(att("w_wink"))),
        "w_sel": rows(split(att("w_selk"))),
        "w_winv": rows(att("w_winv")),
        "w_selv": rows(att("w_selv")),
        "w_q": below(grouped(att("w_dq_nope"), att("w_dq_rope")), 0),
        "w_kn": below(att("w_dk_nope"), QL),
        "w_v1": below(att("w_dv"), QL),
        "w_kr": rows(np.concatenate([np.tile(kr[:, :PART], (1, GROUP)), np.tile(kr[:, PART:], (1, GROUP))], 1)),
        "w_proj": rows(att("w_proj")),
        "w_x": np.stack([rows(xat(n).T) for n in ("Wq", "Wk", "Wv", "Wo")], axis=1),
        "g_lat": np.concatenate([att("g_qnorm"), att("g_kvnorm")])[:, None],
        "rope_k": table,
        "rope_q": (table * f(DK ** -0.5)).astype(f),
        "maskb": np.concatenate([mask, mask], axis=1).astype(bf),
        "identb": np.eye(P).astype(bf),
        "before": np.stack([(np.arange(T)[None, :] < (p + n * P)[:, None]) for n in range(TT)], 1).astype(f),
        "uptri": np.concatenate([(p[:, None] < p[None, :]).astype(f), np.ones((P, P), f)], axis=1),
        "iota64": np.tile(np.arange(KEEP, dtype=f), (P, 1)),
        "own16": (p[:, None] // XD == np.arange(XH)[None, :]).astype(f),
        "meanw": np.full((P, P), 1.0 / T, f),
        "xb": np.stack([xat("bq").reshape(CT, P).T, xat("bk").reshape(CT, P).T], axis=1),
        "xrow": np.stack([np.tile(xat("bv"), (P, 1)), np.tile(xat("bo"), (P, 1))], axis=1),
        "ident": np.eye(P, dtype=f),
        "ffn_gate": rows(a["L0_ffn_w_gate"]).reshape(P, -1),
        "ffn_up": rows(a["L0_ffn_w_up"]).reshape(P, -1),
        "ffn_down": rows(a["L0_ffn_w_down"]).reshape(P, -1),
    }


def kernel(**inputs):
    import concourse.bacc as bacc
    from concourse.bass_utils import run_bass_kernel_spmd

    nc = bacc.Bacc("TRN2", target_bir_lowering=False, num_devices=1)
    arrays = {"in_" + k: np.ascontiguousarray(v) for k, v in _layouts(inputs).items()}
    io = {k[3:]: nc.dram_tensor(k, v.shape, mybir.dt.from_np(v.dtype), kind="ExternalInput").ap()
          for k, v in arrays.items()}
    io["out"] = nc.dram_tensor("out", (B, T, C), F32, kind="ExternalOutput").ap()
    build(nc, io)
    r = run_bass_kernel_spmd(nc, [arrays], core_ids=[0])
    return r.results[0]["out"]
```

```python
from contextlib import ExitStack

import numpy as np
import concourse.bass as bass
from concourse import mybir

ALU = mybir.AluOpType
ACT = mybir.ActivationFunctionType
AX = mybir.AxisListType
F32 = mybir.dt.float32
BF16 = mybir.dt.bfloat16

P = 128
B, T, C = 16, 256, 256
TT, CT = T // P, C // P
HEADS, GROUP = 16, 4
GROUPS = HEADS // GROUP
PART = 32
PARTS = 3
DK = PART * PARTS
VD = 32
KEEP = 64
QL, KVL = 96, 32
LC = QL + KVL + 3
CTX = 77
XD = C // HEADS
XH = P // XD
INNER = 768
IT = INNER // P
BLK = 32
MAGIC = 1.5 * 2.0 ** 23
QMAX = 32767.0
LN_EPS, RMS_EPS = 1e-5, 1e-6
MASKED = -1e30
WIN, BASE, SEL = 0, 1, 2
GATE_ORDER = [2, 0, 1]
QC, WC0, SC0, BC0 = 0, T, 2 * T, 2 * T + KEEP
HCOLS = 3 * T + KEEP
S1, S0 = 64, 640
SEG = {(1, WIN): (0, 256), (1, SEL): (256, 64), (1, BASE): (320, 256),
       (0, WIN): (576, 128), (0, SEL): (704, 64), (0, BASE): (768, 128)}
PCOLS = 896
GDMA = 16 * GROUP * PARTS
PBUF = 4
LAG = 3


class Signal:

    def __init__(self, sem, per, first=0):
        self.sem, self.per, self.first = sem, per, first

    def wait(self, eng, b, k):
        assert k + self.first > 0
        eng.wait_ge(self.sem, b * self.per + k + self.first)

    def wait_all(self, eng, passes):
        eng.wait_ge(self.sem, passes * self.per + self.first)


def build(nc, io):
    with ExitStack() as outer:
        x1_dram = nc.dram_tensor("x1_scratch", (B, P, TT * C), F32, kind="Internal").ap()
        h_dram = nc.dram_tensor("h_scratch", (B, P, CT * T), F32, kind="Internal").ap()
        x2_dram = nc.dram_tensor("x2_scratch", (B, P, TT * C), F32, kind="Internal").ap()
        u_dram = nc.dram_tensor("u_scratch", (B, P, IT * T), F32, kind="Internal").ap()
        ident = outer.enter_context(nc.sbuf_tensor("ident", [P, P], F32))
        hmax = outer.enter_context(nc.sbuf_tensor("hmax", [P, 1], F32))
        self_attention(nc, io, x1_dram, ident, hmax)
        cross_attention(nc, io, x1_dram, h_dram, x2_dram, ident, hmax)
        feed_forward(nc, io, h_dram, x2_dram, u_dram, ident, hmax)


def self_attention(nc, io, x1_dram, ident, hmax):
    with ExitStack() as ctx:
        def sb(name, shape, dt=F32):
            return ctx.enter_context(nc.sbuf_tensor(name, shape, dt))

        def signal(name, per=1, first=0):
            return Signal(ctx.enter_context(nc.semaphore("s_" + name)), per, first)

        def prime(eng, *signals):
            for s in signals:
                eng.sem_inc(s.sem, s.first)

        w_lat = sb("w_lat", [P, CT, LC])
        w_imp = sb("w_imp", [P, CT, P])
        w_win = sb("w_win", [P, CT, GROUPS * PARTS * P])
        w_sel = sb("w_sel", [P, CT, GROUPS * PARTS * P])
        w_winv = sb("w_winv", [P, CT, HEADS * VD])
        w_selv = sb("w_selv", [P, CT, HEADS * VD])
        w_q = sb("w_q", [P, GROUPS * PARTS * P])
        w_kn = sb("w_kn", [P, GROUPS * P])
        w_v1 = sb("w_v1", [P, HEADS * VD])
        w_kr = sb("w_kr", [P, CT, 2 * P])
        w_proj = sb("w_proj", [P, GROUPS, C])
        g_lat = sb("g_lat", [P, 1])
        rope_k = sb("rope_k", [P, 2, T])
        rope_q = sb("rope_q", [P, 2, T])
        maskb = sb("maskb", [P, 2 * P], BF16)
        identb = sb("identb", [P, P], BF16)
        before = sb("before", [P, TT, T])
        uptri = sb("uptri", [P, 2 * P])
        iota64 = sb("iota64", [P, KEEP])
        meanw = sb("meanw", [P, P])
        minus_half = sb("minus_half", [P, 4])
        xin = sb("xin", [P, TT, C])
        xres = sb("x_residual", [P, TT, C])
        stats = sb("stats", [P, TT, 6])
        meanvar = sb("meanvar", [P, TT, 2])
        vareps = sb("vareps", [P, TT])
        rstd = sb("rstd", [P, TT])
        xn = sb("xn", [P, TT, C])
        xnT = sb("xnT", [P, CT, T])
        lat = sb("lat", [P, TT, LC])
        ms = sb("ms", [P, TT, 2])
        rlat = sb("rlat", [P, TT, 2])
        held = sb("held", [P, 4])
        nlat = sb("nlat", [P, TT, P])
        nT = sb("nT", [P, T])
        srow = sb("srow", [P, T])
        scol = sb("scol", [P, TT])
        cnt = sb("cnt", [P, TT])
        tie = sb("tie", [P, TT])
        chosen = sb("chosen", [P, TT])
        rank = sb("rank", [P, TT])
        pick = sb("pick", [P, TT, KEEP])
        selT = sb("selT", [P, CT, KEEP])
        gmax = sb("gmax", [P, 1])
        gexp = sb("gexp", [P, 3])
        gsum = sb("gsum", [P, 1])
        ginv = sb("ginv", [P, 1])
        gate = sb("gate", [P, 3])
        V = sb("V", [P, 5, HEADS * VD])
        rot1 = sb("rot1", [P, 2, T])
        rot2 = sb("rot2", [P, 2, T])
        junk, sq = rot1, rot2
        st = sb("st", [P, 2, PARTS, HCOLS])
        QK = sb("QK", [DK, GROUPS, GROUP, HCOLS])
        nmax = sb("nmax", [P, 2, 6])
        rsum = sb("rsum", [P, 2, 6])
        rinv = sb("rinv", [P, 2, 6])
        coef = sb("coef", [P, 2, 6])
        Pr = sb("Pr", [P, PBUF, PCOLS])
        PT = sb("PT", [P, GROUP, 1024])
        OT = sb("OT", [P, GROUPS, T])
        x1 = sb("x1", [P, TT, C])

        ps = ctx.enter_context(nc.psum_tensor("ps", [P, 8, 512], F32))
        flat = ps[:, 0:4, :].rearrange("p a b -> p (a b)")
        b4, b5, bO, bM = ps[:, 4, :], ps[:, 5, :], ps[:, 6, :], ps[:, 7, :]

        loads = [
            (w_lat, "w_lat"), (w_imp, "w_imp"), (w_win, "w_win"), (w_sel, "w_sel"), (w_winv, "w_winv"),
            (w_selv, "w_selv"), (w_q, "w_q"), (w_kn, "w_kn"), (w_v1, "w_v1"), (w_kr, "w_kr"),
            (w_proj, "w_proj"), (g_lat, "g_lat"), (rope_k, "rope_k"), (rope_q, "rope_q"),
            (maskb, "maskb"), (identb, "identb"), (before, "before"), (uptri, "uptri"),
            (iota64, "iota64"), (meanw, "meanw"),
            (ident, "ident"),
        ]

        s_w = signal("weights", 0)
        s_init = signal("init", 0)
        s_x = signal("x_loaded", 16)
        s_xres = signal("residual_loaded", 16)
        s_stat = signal("ln_stats", 2)
        s_mv = signal("ln_meanvar", 2)
        s_ve = signal("ln_vareps", 1)
        s_rstd = signal("ln_rstd", 1)
        s_xn = signal("ln_done", 2, first=1)
        s_xnT_ps = signal("xnT_ps", 1)
        s_xnT = signal("xnT", 1)
        s_lat_ps = signal("latent_ps", 1)
        s_lat = signal("latent", 1)
        s_ms = signal("mean_square", 4)
        s_rlat = signal("latent_rms", 1)
        s_nlat = signal("latent_normed", 4)
        s_nT_ps = signal("nT_ps", 1)
        s_nT = signal("nT", 1)
        s_gate_ps = signal("gate_ps", 1)
        s_gmax = signal("gate_max", 1)
        s_gexp = signal("gate_exp", 1)
        s_gate = signal("gate", 2)
        s_srow_ps = signal("score_ps", 1)
        s_srow = signal("score_row", 1)
        s_rankop = signal("rank_ops", 10)
        s_chosen = signal("chosen", 2)
        s_rank_ps = signal("rank_ps", 1)
        s_rank = signal("rank", 1)
        s_pick = signal("pick", 2)
        s_selT_ps = signal("selT_ps", 1, first=1)
        s_selT = signal("selT", 1)
        s_v_ps = signal("value_ps", 5)
        s_v = signal("value", 5)
        s_kr_ps = signal("krope_ps", 1)
        s_task_ps = signal("task_ps", 16)
        s_mul = signal("rope_products", 1 + GROUPS * 3)
        s_rot = signal("rope_done", 2 + GROUPS * 3, first=1)
        s_copy = signal("nope_copied", GROUPS * 3)
        s_group = [signal("even_group", 2 * GDMA, first=1), signal("odd_group", 2 * GDMA, first=1)]
        s_s = signal("scores", HEADS)
        s_max = signal("score_max", HEADS * 3)
        s_exp = signal("exp", HEADS * 6)
        s_rinv = signal("sum_inverse", HEADS)
        s_coef = signal("coefficient", HEADS)
        s_pn = signal("probs_scaled", HEADS * 6)
        s_pt_ps = signal("probsT_ps", HEADS)
        s_pta = signal("probsT_a", HEADS)
        s_ptb = signal("probsT_b", HEADS)
        s_o_ps = signal("heads_ps", GROUPS)
        s_o = signal("heads_out", GROUPS)
        s_proj = signal("proj_ps", 1)
        s_x1 = signal("x1", 1, first=1)
        s_out = signal("stored", 16, first=1)

        ahead = {
            4: ([], ["stats"]),
            6: ([], ["norm"]),
            8: (["xnT"], ["lat"]),
            9: (["srow"], ["ms"]),
            10: (["gate"], ["nlat", "scol"]),
            11: (["nT"], ["ties"]),
            12: ([], ["larger"]),
            13: (["krope"], ["rank"]),
            14: ([(0, 0)], ["selT"]),
            15: ([(0, 1)], [(0, 2)]),
            16: ([(0, 3)], [(1, 0)]),
            17: ([(1, 1)], ["gate_done"]),
            18: ([(1, 2)], []),
            19: ([(1, 3)], []),
        }
        SLOTS = HEADS + LAG + 1

        def values_due(h):
            return (h - LAG) // GROUP - 1 if h > LAG and (h - LAG) % GROUP == 0 else None

        def steps(b, h, behind, nxt):
            out = []
            if not behind and h < 2 * GROUP:
                out.append((b, (2 + h // 4, h % 4)))
            if behind and h < 5:
                out.append((b, "value%d" % h))
            if nxt and h in ahead:
                out += [(b + 1, s) for s in ahead[h][behind]]
            return out

        first_row = [s for h in sorted(ahead) for s in ahead[h][0] + ahead[h][1]]

        def bank_read(eng, b, step):
            if step == "xnT":
                s_xnT.wait(eng, b, 1)
            elif step == "lat":
                s_lat.wait(eng, b, 1)
            elif step == "srow":
                s_srow.wait(eng, b, 1)
            elif step == "gate":
                s_gexp.wait(eng, b, 1)
            elif step == "nT":
                s_nT.wait(eng, b, 1)
            elif step == "krope":
                s_mul.wait(eng, b, 1)
            elif step == "rank":
                s_rank.wait(eng, b, 1)
            elif step == "selT":
                s_selT.wait(eng, b, 1)
            elif isinstance(step, str):
                s_v.wait(eng, b, int(step[5:]) + 1)
            else:
                g, n = step
                if n in (0, 2, 3):
                    s_mul.wait(eng, b, 1 + 3 * g + {0: 1, 2: 2, 3: 3}[n])
                if n in (1, 3):
                    s_copy.wait(eng, b, 3 * g + {1: 1, 3: 3}[n])

        block = ctx.enter_context(nc.Block())

        def head_scores(h):
            return flat[:, (h % 2) * 1024:(h % 2) * 1024 + 1024]

        halves = bM.rearrange("p (a t) -> p a t", a=2)

        @block.sync
        def _(sp):
            prime(sp, *s_group, s_out)
            for tile, name in loads:
                src = io[name]
                dims = len(tile.shape)
                dst = tile[:, :] if dims == 2 else tile[:, :, :] if dims == 3 else tile[:, :, :, :]
                sp.dma_start(dst, src).then_inc(s_w.sem, 16)

            def load(b, tile, sig):
                sp.dma_start(tile[:, :, :], io["x"][bass.ds(b, 1)].rearrange(
                    "o (i p) c -> p (o i) c", p=P)).then_inc(sig.sem, 16)

            def group(b, g):
                s_rot.wait(sp, b, 2 + 3 * (g + 1))
                for j in range(GROUP):
                    for part in range(PARTS):
                        sp.dma_start(QK[PART * part:PART * (part + 1), g, j, :],
                                     st[PART * j:PART * (j + 1), g % 2, part, :])\
                            .then_inc(s_group[g % 2].sem, 16)

            def row(b, nxt):
                if nxt:
                    s_xn.wait(sp, b + 1, 0)
                    load(b + 1, xin, s_x)
                s_x1.wait(sp, b, 0)
                load(b, xres, s_xres)
                for g in (2, 3):
                    group(b, g)
                if nxt:
                    for g in (0, 1):
                        group(b + 1, g)
                s_x1.wait(sp, b, 1)
                sp.dma_start(x1_dram[bass.ds(b, 1)].rearrange("o p c -> p (o c)"),
                             x1[:, :, :].rearrange("p a b -> p (a b)")).then_inc(s_out.sem, 16)

            load(0, xin, s_x)
            for g in (0, 1):
                group(0, g)
            with sp.Fori(0, B - 1) as b:
                row(b, True)
            row(B - 1, False)
            s_out.wait_all(sp, B)

        @block.tensor
        def _(pe):
            prime(pe, s_selT_ps)
            pe.wait_ge(s_w.sem, 16 * len(loads))
            pe.wait_ge(s_init.sem, 5)

            def normed_transposes(b):
                s_xn.wait(pe, b, 2)
                for i in range(TT):
                    for c in range(CT):
                        m = pe.transpose(halves[:, c, i * P:(i + 1) * P], xn[:, i, c * P:(c + 1) * P], ident[:, :])
                m.then_inc(s_xnT_ps.sem, 1)

            def latents(b):
                for i in range(TT):
                    for c in range(CT):
                        m = pe.matmul(bM[:, i * T:i * T + LC], xnT[:, c, i * P:(i + 1) * P], w_lat[:, c, :],
                                      start=(c == 0), stop=(c == CT - 1))
                m.then_inc(s_lat_ps.sem, 1)

            def importance(b):
                for c in range(CT):
                    m = pe.matmul(bM[:, 0:T], w_imp[:, c, :], xnT[:, c, :], start=(c == 0), stop=(c == CT - 1))
                m.then_inc(s_srow_ps.sem, 1)

            def gate_logits(b):
                for i in range(TT):
                    m = pe.matmul(bM[:, 0:3], meanw[:, :], lat[:, i, QL + KVL:LC], start=(i == 0),
                                  stop=(i == TT - 1))
                m.then_inc(s_gate_ps.sem, 1)

            def latent_transposes(b):
                s_nlat.wait(pe, b, 4)
                for i in range(TT):
                    m = pe.transpose(bM[:, i * P:(i + 1) * P], nlat[:, i, :], ident[:, :])
                m.then_inc(s_nT_ps.sem, 1)

            def shared_key(b):
                for part in range(2):
                    for c in range(CT):
                        m = pe.matmul(halves[:, part, :], w_kr[:, c, part * P:(part + 1) * P],
                                      xnT[:, c, :], start=(c == 0), stop=(c == CT - 1))
                m.then_inc(s_kr_ps.sem, 1)

            def ranks(b):
                s_chosen.wait(pe, b, 2)
                pe.matmul(bM[:, 0:1], uptri[:, 0:P], chosen[:, 0:1], start=True, stop=True)
                pe.matmul(bM[:, 1:2], uptri[:, P:2 * P], chosen[:, 0:1], start=True, stop=False)
                pe.matmul(bM[:, 1:2], uptri[:, 0:P], chosen[:, 1:2], start=False, stop=True)\
                    .then_inc(s_rank_ps.sem, 1)

            def selected(b):
                s_pick.wait(pe, b, 2)
                for c in range(CT):
                    for i in range(TT):
                        m = pe.matmul(bM[:, c * KEEP:(c + 1) * KEEP], xn[:, i, c * P:(c + 1) * P],
                                      pick[:, i, :], start=(i == 0), stop=(i == TT - 1))
                m.then_inc(s_selT_ps.sem, 1)

            def head_values(b, k):
                i = k % 2
                if k < 2:
                    for c in range(CT):
                        m = pe.matmul(bM, xnT[:, c, i * P:(i + 1) * P], w_winv[:, c, :], start=(c == 0),
                                      stop=(c == CT - 1))
                elif k < 4:
                    m = pe.matmul(bM, nT[:, i * P:(i + 1) * P], w_v1[:, :], start=True, stop=True)
                else:
                    for c in range(CT):
                        m = pe.matmul(bM[0:KEEP, :], selT[:, c, :], w_selv[:, c, :], start=(c == 0),
                                      stop=(c == CT - 1))
                m.then_inc(s_v_ps.sem, 1)

            def task(b, g, n):
                col = lambda part: slice((g * PARTS + part) * P, (g * PARTS + part + 1) * P)
                if n == 0:
                    for part in (1, 2):
                        for c in range(CT):
                            m = pe.matmul(halves[:, part - 1, :], w_win[:, c, col(part)], xnT[:, c, :],
                                          start=(c == 0), stop=(c == CT - 1))
                elif n == 1:
                    pe.matmul(halves[:, 0, :], w_kn[:, g * P:(g + 1) * P], nT[:, :], start=True, stop=True)
                    for c in range(CT):
                        m = pe.matmul(halves[:, 1, :], w_win[:, c, col(0)], xnT[:, c, :],
                                      start=(c == 0), stop=(c == CT - 1))
                elif n == 2:
                    for part in (1, 2):
                        m = pe.matmul(halves[:, part - 1, :], w_q[:, col(part)], nT[:, :], start=True, stop=True)
                else:
                    pe.matmul(halves[:, 0, :], w_q[:, col(0)], nT[:, :], start=True, stop=True)
                    for part in range(PARTS):
                        for c in range(CT):
                            m = pe.matmul(bM[:, T + KEEP * part:T + KEEP * (part + 1)], w_sel[:, c, col(part)],
                                          selT[:, c, :], start=(c == 0), stop=(c == CT - 1))
                m.then_inc(s_task_ps.sem, 1)

            makes = {"xnT": normed_transposes, "lat": latents, "srow": importance, "gate": gate_logits,
                     "nT": latent_transposes, "krope": shared_key, "rank": ranks, "selT": selected}

            def make(todo, before):
                for b, step in todo:
                    if isinstance(step, str) and step not in makes and not step.startswith("value"):
                        continue
                    if before:
                        bank_read(pe, *before)
                    if isinstance(step, tuple):
                        task(b, *step)
                    elif step in makes:
                        makes[step](b)
                    else:
                        head_values(b, int(step[5:]))
                    before = (b, step)
                return before

            def scores(b, h):
                g, j = h // GROUP, h % GROUP
                if j == 0:
                    s_group[g % 2].wait(pe, b, GDMA * (g // 2 + 1))
                if h >= 2:
                    s_exp.wait(pe, b, 6 * (h - 1))
                S = head_scores(h)
                qk = QK[:, g, j, :]
                q0, q1 = qk[:, QC:QC + P], qk[:, QC + P:QC + T]
                pe.matmul(S[:, 64:512], q1, qk[:, WC0:WC0 + 448], start=True, stop=False, skip_group_check=True)
                pe.matmul(S[:, 192:320], identb[:, :], maskb[:, 0:P], start=False, stop=True,
                          skip_group_check=True)
                pe.matmul(S[:, 512:640], q1, qk[:, WC0 + 448:HCOLS], start=True, stop=False,
                          skip_group_check=True)
                pe.matmul(S[:, 512:640], identb[:, :], maskb[:, 0:P], start=False, stop=False,
                          skip_group_check=True)
                pe.matmul(S[:, S0:S0 + P], q0, qk[:, WC0:WC0 + P], start=False, stop=False,
                          skip_group_check=True)
                pe.matmul(S[:, S0 + P:S0 + 2 * P + KEEP], q0, qk[:, SC0:SC0 + KEEP + P],
                          start=False, stop=False, skip_group_check=True)
                pe.matmul(S[:, S0:S0 + P], identb[:, :], maskb[:, 0:P], start=False, stop=False,
                          skip_group_check=True)
                m = pe.matmul(S[:, S0 + P + KEEP:S0 + 2 * P + KEEP], identb[:, :], maskb[:, 0:P], start=False,
                              stop=True, skip_group_check=True)
                m.then_inc(s_s.sem, 1)

            def transposes(b, h):
                s_pn.wait(pe, b, 6 * (h + 1))
                if h:
                    s_pta.wait(pe, b, h)
                    s_ptb.wait(pe, b, h)
                p = Pr[:, h % PBUF, :]
                w1, b1, e1 = SEG[1, WIN][0], SEG[1, BASE][0], SEG[1, SEL][0]
                w0, b0, e0 = SEG[0, WIN][0], SEG[0, BASE][0], SEG[0, SEL][0]
                for to, at in ((b4[:, 0:P], w0), (b4[:, P:2 * P], w1), (b4[:, 2 * P:3 * P], b0),
                               (b4[:, 3 * P:4 * P], b1), (b5[:, 0:P], w1 + P), (b5[:, P:2 * P], b1 + P)):
                    pe.transpose(to, p[:, at:at + P], ident[:, :])
                pe.transpose(b5[0:KEEP, 2 * P:3 * P], p[:, e0:e0 + KEEP], ident[:, :])
                pe.transpose(b5[0:KEEP, 3 * P:4 * P], p[:, e1:e1 + KEEP], ident[:, :]).then_inc(s_pt_ps.sem, 1)

            def values(b, g):
                s_pta.wait(pe, b, GROUP * (g + 1))
                s_ptb.wait(pe, b, GROUP * (g + 1))
                if g:
                    s_o.wait(pe, b, g)
                else:
                    s_v.wait(pe, b, 5)
                    s_x1.wait(pe, b, 0)
                for n, (tile, at, width, to) in enumerate((
                        (0, 0, T, 0), (2, T, T, 0), (4, 3 * T, T, 0), (1, 2 * T, P, P), (3, 2 * T + P, P, P))):
                    for j in range(GROUP):
                        h = g * GROUP + j
                        m = pe.matmul(bO[VD * j:VD * (j + 1), to:to + width], V[:, tile, VD * h:VD * (h + 1)],
                                      PT[:, j, at:at + width], start=(n == 0), stop=(n == 4),
                                      skip_group_check=True)
                m.then_inc(s_o_ps.sem, 1)

            def projection(b):
                s_o.wait(pe, b, GROUPS)
                for i in range(TT):
                    for g in range(GROUPS):
                        m = pe.matmul(bO[:, i * C:(i + 1) * C], OT[:, g, i * P:(i + 1) * P], w_proj[:, g, :],
                                      start=(g == 0), stop=(g == GROUPS - 1))
                m.then_inc(s_proj.sem, 1)

            def row(b, nxt):
                before = (b, (1, 3))
                for h in range(SLOTS):
                    before = make(steps(b, h, 0, nxt), before)
                    if h < HEADS:
                        scores(b, h)
                    before = make(steps(b, h, 1, nxt), before)
                    if values_due(h) is not None:
                        values(b, values_due(h))
                    if LAG <= h < HEADS + LAG:
                        transposes(b, h - LAG)
                projection(b)

            make([(0, s) for s in first_row], None)
            with pe.Fori(0, B - 1) as b:
                row(b, True)
            row(B - 1, False)

        @block.scalar
        def _(act):
            act.wait_ge(s_w.sem, 16 * len(loads))
            act.wait_ge(s_init.sem, 5)

            def copy(out, src, sig, scale=1.0):
                act.activation(out, src, ACT.Copy, scale=scale).then_inc(sig.sem, 1)

            def nope_copies(b, g, n):
                s_task_ps.wait(act, b, 4 * g + n + 1)
                gg = g % 2
                if n == 1:
                    s_group[gg].wait(act, b, GDMA * (g // 2))
                    act.activation(st[:, gg, 0, BC0:BC0 + T], halves[:, 0, :], ACT.Copy)
                    copy(st[:, gg, 0, WC0:WC0 + T], halves[:, 1, :], s_copy)
                if n == 3:
                    copy(st[:, gg, 0, QC:QC + T], halves[:, 0, :], s_copy, scale=DK ** -0.5)
                    copy(st[:, gg, 0, SC0:SC0 + KEEP], bM[:, T:T + KEEP], s_copy)

            def take(todo):
                for b, step in todo:
                    if step == "xnT":
                        s_xnT_ps.wait(act, b, 1)
                        copy(xnT[:, :, :].rearrange("p a b -> p (a b)"), bM, s_xnT)
                    elif step == "lat":
                        s_lat_ps.wait(act, b, 1)
                        copy(lat[:, :, :], halves[:, :, 0:LC], s_lat)
                    elif step == "nT":
                        s_nT_ps.wait(act, b, 1)
                        act.activation(nT[:, :], bM[:, 0:T], ACT.Copy, scale=g_lat[:, 0:1]).then_inc(s_nT.sem, 1)
                    elif step == "gate":
                        s_gmax.wait(act, b, 1)
                        act.activation(gexp[:, :], bM[:, 0:3], ACT.Exp, bias=gmax[:, 0:1],
                                       accum_out=gsum[:, 0:1]).then_inc(s_gexp.sem, 1)
                    elif step == "selT":
                        s_selT_ps.wait(act, b, 1)
                        copy(selT[:, :, :].rearrange("p a b -> p (a b)"), bM[:, 0:CT * KEEP], s_selT)
                    elif step in ("value0", "value1", "value2", "value3", "value4"):
                        k = int(step[5:])
                        s_v_ps.wait(act, b, k + 1)
                        rows = KEEP if k == 4 else P
                        copy(V[0:rows, k, :], bM[0:rows, :], s_v)
                    elif isinstance(step, tuple) and step[1] in (1, 3):
                        nope_copies(b, *step)

            def exps(b, h):
                S = head_scores(h)[:, 64:64 + PCOLS]
                s_max.wait(act, b, 3 * (h + 1))
                if h >= PBUF:
                    s_pt_ps.wait(act, b, h - PBUF + 1)
                if h >= 2:
                    s_coef.wait(act, b, h - 1)
                for i in (1, 0):
                    for a in (WIN, BASE, SEL):
                        at, width = SEG[i, a]
                        c = 3 * (1 - i) + a
                        act.activation(Pr[:, h % PBUF, at:at + width], S[:, at:at + width], ACT.Exp,
                                       bias=nmax[:, h % 2, c:c + 1], accum_out=rsum[:, h % 2, c:c + 1])\
                            .then_inc(s_exp.sem, 1)

            def evacuate(b, h):
                s_pt_ps.wait(act, b, h + 1)
                act.activation(PT[:, h % GROUP, 2 * T:3 * T], b5[:, 0:T], ACT.Copy)
                copy(PT[0:KEEP, h % GROUP, 3 * T:4 * T], b5[0:KEEP, T:2 * T], s_ptb)

            def row(b, nxt):
                for h in range(SLOTS):
                    take(steps(b, h, 0, nxt))
                    take(steps(b, h, 1, nxt))
                    if h < HEADS:
                        exps(b, h)
                    if values_due(h) is not None:
                        s_o_ps.wait(act, b, values_due(h) + 1)
                        copy(OT[:, values_due(h), :], bO[:, 0:T], s_o)
                    if LAG <= h < HEADS + LAG:
                        evacuate(b, h - LAG)

            take([(0, s) for s in first_row])
            with act.Fori(0, B - 1) as b:
                row(b, True)
            row(B - 1, False)

        @block.gpsimd
        def _(pool):
            prime(pool, s_rot)
            pool.memset(minus_half[:, :], -0.5).then_inc(s_init.sem, 1)
            pool.memset(PT[:, :, :], 0.0).then_inc(s_init.sem, 1)
            pool.memset(V[:, 4, :], 0.0).then_inc(s_init.sem, 1)
            pool.memset(hmax[:, :], 0.0).then_inc(s_init.sem, 1)
            pool.memset(rot1[:, :, :], 0.0).then_inc(s_init.sem, 1)
            pool.wait_ge(s_w.sem, 16 * len(loads))
            pool.wait_ge(s_init.sem, 5)

            def inverse_root(b, k, out, src, n, ready, done):
                ready.wait(pool, b, k)
                pool.tensor_tensor(out, src, minus_half[:, 0:n], ALU.pow).then_inc(done.sem, 1)

            def rotate(b, k, out, width):
                s_mul.wait(pool, b, k + 1)
                pool.tensor_tensor(out, rot1[:, :, 0:width], rot2[:, :, 0:width], ALU.add)\
                    .then_inc(s_rot.sem, 1)

            def take(todo):
                for b, step in todo:
                    if step == "stats":
                        inverse_root(b, 1, rstd[:, :], vareps[:, :], TT, s_ve, s_rstd)
                    elif step == "ms":
                        inverse_root(b, 4, rlat[:, :, :].rearrange("p a b -> p (a b)"),
                                     ms[:, :, :].rearrange("p a b -> p (a b)"), 4, s_ms, s_rlat)
                    elif step == "krope":
                        for gg in range(2):
                            s_group[gg].wait(pool, b, 0)
                            rotate(b, 0, st[:, gg, 1:3, BC0:BC0 + T], T)
                    elif isinstance(step, tuple) and step[1] != 1:
                        g, n = step
                        gg = g % 2
                        if n == 0 and g >= 2:
                            s_group[gg].wait(pool, b, GDMA * (g // 2))
                        at, width = {0: (WC0, T), 2: (QC, T), 3: (SC0, KEEP)}[n]
                        rotate(b, {0: 1, 2: 2, 3: 3}[n] + 3 * g, st[:, gg, 1:3, at:at + width], width)

            def scale(b, h):
                s_coef.wait(pool, b, h + 1)
                pool.tensor_tensor(held[:, 1 + h % 2:2 + h % 2], minus_half[:, 0:1], minus_half[:, 1:2], ALU.add)
                for i in (1, 0):
                    for a in (WIN, BASE, SEL):
                        at, width = SEG[i, a]
                        c = 3 * (1 - i) + a
                        p = Pr[:, h % PBUF, at:at + width]
                        pool.tensor_scalar(p, p, coef[:, h % 2, c:c + 1], 1.0, ALU.mult, ALU.mult)\
                            .then_inc(s_pn.sem, 1)

            def row(b, nxt):
                for h in range(SLOTS):
                    take(steps(b, h, 0, nxt))
                    if 1 <= h <= HEADS:
                        scale(b, h - 1)
                    take(steps(b, h, 1, nxt))

            take([(0, s) for s in first_row])
            with pool.Fori(0, B - 1) as b:
                row(b, True)
            row(B - 1, False)

        @block.vector
        def _(dve):
            prime(dve, s_x1, s_xn)
            dve.wait_ge(s_w.sem, 16 * len(loads))
            dve.wait_ge(s_init.sem, 5)
            latent_parts = [(i, n, a, z) for i in range(TT) for n, (a, z) in
                            enumerate(((0, QL), (QL, QL + KVL)))]

            def statistics(b):
                s_x.wait(dve, b, 16)
                for i in range(TT):
                    dve.bn_stats(stats[:, i, :], xin[:, i, :]).then_inc(s_stat.sem, 1)
                s_stat.wait(dve, b, 2)
                dve.tensor_copy(held[:, 0:1], stats[:, 0, 0:1])
                for i in range(TT):
                    dve.bn_aggr(meanvar[:, i, :], stats[:, i, :]).then_inc(s_mv.sem, 1)
                s_mv.wait(dve, b, 2)
                dve.tensor_scalar(vareps[:, :], meanvar[:, :, 1], LN_EPS, None, ALU.add).then_inc(s_ve.sem, 1)

            def norm(b):
                s_rstd.wait(dve, b, 1)
                s_selT_ps.wait(dve, b, 0)
                for i in range(TT):
                    dve.tensor_scalar(xn[:, i, :], xin[:, i, :], meanvar[:, i, 0:1], rstd[:, i:i + 1],
                                      ALU.subtract, ALU.mult).then_inc(s_xn.sem, 1)

            def mean_squares(b):
                s_lat.wait(dve, b, 1)
                s_rot.wait(dve, b, 0)
                for k, (i, n, a, z) in enumerate(latent_parts):
                    if k:
                        s_ms.wait(dve, b, k)
                    dve.tensor_tensor_reduce(sq[:, 0, 0:z - a], lat[:, i, a:z], lat[:, i, a:z],
                                             1.0 / (z - a), RMS_EPS, ALU.mult, ALU.add,
                                             ms[:, i, n:n + 1]).then_inc(s_ms.sem, 1)

            def normed_latents(b):
                s_rlat.wait(dve, b, 1)
                for i, n, a, z in latent_parts:
                    dve.tensor_scalar(nlat[:, i, a:z], lat[:, i, a:z], rlat[:, i, n:n + 1], None,
                                      ALU.mult).then_inc(s_nlat.sem, 1)

            def own_importance(b):
                s_srow.wait(dve, b, 1)
                for i in range(TT):
                    dve.tensor_tensor_reduce(junk[:, i, 0:P], srow[:, i * P:(i + 1) * P], ident[:, :], 1.0,
                                             0.0, ALU.mult, ALU.add, scol[:, i:i + 1]).then_inc(s_rankop.sem, 1)

            def ties(b):
                s_rankop.wait(dve, b, 2)
                for i in range(TT):
                    dve.tensor_scalar(junk[:, i, :], srow[:, :], scol[:, i:i + 1], None, ALU.is_equal)\
                        .then_inc(s_rankop.sem, 1)
                for i in range(TT):
                    s_rankop.wait(dve, b, 3 + i)
                    dve.tensor_tensor_reduce(junk[:, i, :], junk[:, i, :], before[:, i, :], 1.0, 0.0,
                                             ALU.mult, ALU.add, tie[:, i:i + 1]).then_inc(s_rankop.sem, 1)

            def larger(b):
                for i in range(TT):
                    s_rankop.wait(dve, b, 5 + i)
                    dve.tensor_scalar(junk[:, i, :], srow[:, :], scol[:, i:i + 1], None, ALU.is_gt)\
                        .then_inc(s_rankop.sem, 1)
                for i in range(TT):
                    s_rankop.wait(dve, b, 7 + i)
                    dve.tensor_reduce(cnt[:, i:i + 1], junk[:, i, :], AX.X, ALU.add)\
                        .then_inc(s_rankop.sem, 1)
                for i in range(TT):
                    s_rankop.wait(dve, b, 9 + i)
                    dve.tensor_scalar(chosen[:, i:i + 1], cnt[:, i:i + 1], tie[:, i:i + 1], KEEP - 0.5,
                                      ALU.add, ALU.is_lt).then_inc(s_chosen.sem, 1)

            def pick_columns(b):
                s_rank_ps.wait(dve, b, 1)
                dve.tensor_copy(rank[:, :], bM[:, 0:2]).then_inc(s_rank.sem, 1)
                s_rank.wait(dve, b, 1)
                for i in range(TT):
                    dve.tensor_scalar(pick[:, i, :], iota64[:, :], rank[:, i:i + 1], chosen[:, i:i + 1],
                                      ALU.is_equal, ALU.mult).then_inc(s_pick.sem, 1)

            def products(b, k, src, table, width, scale=None):
                s_rot.wait(dve, b, k + (k > 0))
                cos = table[:, 0:1, 0:width].to_broadcast([P, 2, width])
                sin = table[:, 1, 0:width]
                one = 1.0 if scale is None else scale
                dve.scalar_tensor_tensor(rot1[:, :, 0:width], src, one, cos, ALU.mult, ALU.mult)
                dve.scalar_tensor_tensor(rot2[:, 0, 0:width], src[:, 1, :], -one, sin, ALU.mult, ALU.mult)
                dve.scalar_tensor_tensor(rot2[:, 1, 0:width], src[:, 0, :], one, sin, ALU.mult, ALU.mult)\
                    .then_inc(s_mul.sem, 1)

            def group_products(b, g, n):
                s_task_ps.wait(dve, b, 4 * g + n + 1)
                if n == 0:
                    products(b, 1 + 3 * g, halves, rope_k, T)
                if n == 2:
                    products(b, 2 + 3 * g, halves, rope_q, T)
                if n == 3:
                    s_copy.wait(dve, b, 3 * (g + 1))
                    products(b, 3 + 3 * g, bM[:, T + KEEP:T + 3 * KEEP].rearrange("p (a t) -> p a t", a=2),
                             rope_k, KEEP)

            takes = {"stats": statistics, "norm": norm, "ms": mean_squares, "nlat": normed_latents,
                     "scol": own_importance, "ties": ties, "larger": larger, "rank": pick_columns}

            def take(todo):
                for b, step in todo:
                    if step in takes:
                        takes[step](b)
                    elif step == "srow":
                        s_srow_ps.wait(dve, b, 1)
                        dve.tensor_copy(srow[:, :], bM[:, 0:T]).then_inc(s_srow.sem, 1)
                    elif step == "gate":
                        s_gate_ps.wait(dve, b, 1)
                        dve.tensor_reduce(gmax[:, :], bM[:, 0:3], AX.X, ALU.max, negate=True)\
                            .then_inc(s_gmax.sem, 1)
                    elif step == "gate_done":
                        s_gexp.wait(dve, b, 1)
                        dve.reciprocal(ginv[:, :], gsum[:, :]).then_inc(s_gate.sem, 1)
                        s_gate.wait(dve, b, 1)
                        dve.tensor_scalar(gate[:, :], gexp[:, :], ginv[:, 0:1], None, ALU.mult)\
                            .then_inc(s_gate.sem, 1)
                    elif step == "krope":
                        s_kr_ps.wait(dve, b, 1)
                        products(b, 0, halves, rope_k, T, scale=1.0 / HEADS)
                    elif isinstance(step, tuple) and step[1] != 1:
                        group_products(b, *step)

            def maxima(b, h):
                S = head_scores(h)
                s_s.wait(dve, b, h + 1)
                if h >= 2:
                    s_exp.wait(dve, b, 6 * (h - 1))
                m = nmax[:, h % 2, :]
                both = lambda at, n, apart: S[:, at:at + 2 * apart].rearrange("p (a k) -> p a k", k=apart)[:, :, 0:n]
                dve.tensor_reduce(m[:, 0:2], both(S1, T, T + KEEP), AX.X, ALU.max, negate=True)\
                    .then_inc(s_max.sem, 1)
                dve.tensor_reduce(m[:, 3:5], both(S0, P, P + KEEP), AX.X, ALU.max, negate=True)\
                    .then_inc(s_max.sem, 1)
                sel = S[:, S1 + T:S0 + P + KEEP].rearrange("p (a k) -> p a k", k=KEEP)
                dve.tensor_reduce(m[:, 2:6:3], sel[:, 0:8:7, :], AX.X, ALU.max, negate=True)\
                    .then_inc(s_max.sem, 1)

            def coefficients(b, h):
                s_exp.wait(dve, b, 6 * (h + 1))
                if h >= 2:
                    s_pn.wait(dve, b, 6 * (h - 1))
                if h == 0:
                    s_gate.wait(dve, b, 2)
                dve.reciprocal(rinv[:, h % 2, :], rsum[:, h % 2, :]).then_inc(s_rinv.sem, 1)
                s_rinv.wait(dve, b, h + 1)
                dve.tensor_tensor(coef[:, h % 2, :].rearrange("p (a k) -> p a k", a=2),
                                  rinv[:, h % 2, :].rearrange("p (a k) -> p a k", a=2),
                                  gate[:, :].unsqueeze(1).to_broadcast([P, 2, 3]), ALU.mult)\
                    .then_inc(s_coef.sem, 1)

            def evacuate(b, h):
                s_pt_ps.wait(dve, b, h + 1)
                dve.tensor_copy(PT[:, h % GROUP, 0:2 * T], b4).then_inc(s_pta.sem, 1)

            def row(b, nxt):
                for h in range(SLOTS):
                    take(steps(b, h, 0, nxt))
                    if h < HEADS:
                        maxima(b, h)
                    take(steps(b, h, 1, nxt))
                    if 1 <= h <= HEADS:
                        coefficients(b, h - 1)
                    if LAG <= h < HEADS + LAG:
                        evacuate(b, h - LAG)
                s_proj.wait(dve, b, 1)
                s_xres.wait(dve, b, 16)
                s_out.wait(dve, b, 0)
                dve.tensor_tensor(x1[:, :, :].rearrange("p a b -> p (a b)"), bO,
                                  xres[:, :, :].rearrange("p a b -> p (a b)"), ALU.add).then_inc(s_x1.sem, 1)

            take([(0, s) for s in first_row])
            with dve.Fori(0, B - 1) as b:
                row(b, True)
            row(B - 1, False)


def cross_attention(nc, io, x1_dram, h_dram, x2_dram, ident, hmax):
    with ExitStack() as ctx:
        def sb(name, shape, dt=F32):
            return ctx.enter_context(nc.sbuf_tensor(name, shape, dt))

        def two(name, shape):
            return [sb(name + "_%d" % r, shape) for r in range(2)]

        def signals(name, per=1, first=0):
            return [Signal(ctx.enter_context(nc.semaphore("s_%s_%d" % (name, r))), per, first)
                    for r in range(2)]

        def prime(eng, *pairs):
            for pair in pairs:
                for s in pair:
                    eng.sem_inc(s.sem, s.first)

        w_x = sb("w_x", [P, 4, CT, C])
        own16 = sb("own16", [P, XH])
        xb = sb("xb", [P, 2, CT])
        xrow = sb("xrow", [P, 2, C])
        minus_half = sb("minus_half2", [P, TT])
        x1 = two("x1", [P, TT, C])
        x1b = two("x1b", [P, TT, C])
        ctxT = two("ctxT", [P, CT, CTX])
        stats = two("stats2", [P, 2, TT, 6])
        meanvar = two("meanvar2", [P, 2, TT, 2])
        vareps = two("vareps2", [P, 2, TT])
        rstd = two("rstd2", [P, 2, TT])
        held = two("held2", [P, 1])
        xn = two("xn2", [P, 2, TT, C])
        xnT = two("xnT2", [P, CT, T])
        kT2 = two("kT2", [P, CT, CTX])
        Kbd = two("Kbd", [P, CT, XH, CTX])
        Vz = two("Vz", [CTX, HEADS // 2, 2, 2, XD])
        q2 = two("q2", [P, CT, T])
        nmax2 = two("nmax2", [P, HEADS])
        P2 = two("P2", [P, TT, HEADS, CTX])
        rs2 = two("rs2", [P, TT, HEADS])
        ri2 = two("ri2", [P, TT, HEADS])
        PT2 = two("PT2", [P, HEADS, T])
        O2T = two("O2T", [P, CT, T])
        x2 = two("x2", [P, TT, C])
        hT = two("hT", [P, CT, T])
        hm = two("hm", [P, 1])
        ps = ctx.enter_context(nc.psum_tensor("ps_x", [P, 8, 512], F32))
        bank = lambda r, n: ps[:, 4 * r + n, :]

        loads = [(w_x, "w_x"), (own16, "own16"), (xb, "xb"), (xrow, "xrow")]
        s_w = ctx.enter_context(nc.semaphore("s_x_weights"))
        s_init = ctx.enter_context(nc.semaphore("s_x_init"))
        s_in = signals("x1_loaded", 32)
        s_ln = [signals("x_ln_ops_1", 5), signals("x_ln_ops_2", 5)]
        s_rstd = [signals("x_rstd_1", 1), signals("x_rstd_2", 1)]
        s_xn = [signals("x_normed_1", 2), signals("x_normed_2", 2)]
        s_x1b = signals("x1_biased", 1, first=1)
        s_kv_ps = signals("xkv_ps", 2, first=1)
        s_kv = signals("xkv", 2)
        s_kbd = signals("xk_blocks", 1)
        s_xnT_ps = [signals("xT_ps_1", 1, first=1), signals("xT_ps_2", 1, first=1)]
        s_xnT = [signals("xT_1", 1), signals("xT_2", 1, first=1)]
        s_q2_ps = signals("xq_ps", 1)
        s_q2 = signals("xq", 1)
        s_s2 = signals("xscores", 2)
        s_sub2 = signals("xshifted", 4)
        s_e2 = signals("xexp", 2)
        s_r2 = signals("xsum", 4)
        s_n2 = signals("xprobs", 2)
        s_t2_ps = signals("xprobsT_ps", 8)
        s_t2 = signals("xprobsT", 8, first=1)
        s_o2_ps = signals("xheads_ps", 1)
        s_o2 = signals("xheads_out", 1, first=1)
        s_y2_ps = signals("xproj_ps", 1)
        s_x2 = signals("x2", 1, first=1)
        s_hm = signals("h_max", 1)
        s_hmax = Signal(ctx.enter_context(nc.semaphore("s_h_running_max")), 2, first=1)
        s_out = signals("x_stored", 32, first=1)

        PAIRS = B // 2
        STAGES = 10

        def rows(eng, early, first, second):
            def period(old, new, nxt):
                for k in range(STAGES):
                    for row, stages in ((old, second), (new, first), (nxt, early)):
                        if row:
                            for step in stages.get(k, []):
                                step(*row)

            period(None, None, (0, 0))
            period(None, (0, 0), (0, 1))
            with eng.Fori(0, PAIRS - 1) as b:
                period((b, 0), (b, 1), (b + 1, 0))
                period((b, 1), (b + 1, 0), (b + 1, 1))
            period((PAIRS - 1, 0), (PAIRS - 1, 1), None)
            period((PAIRS - 1, 1), None, None)

        def tile(step, i):
            return lambda b, r: step(b, r, i)

        block = ctx.enter_context(nc.Block())

        @block.sync
        def _(sp):
            prime(sp, s_out)
            for tile, name in loads:
                dims = len(tile.shape)
                dst = tile[:, :] if dims == 2 else tile[:, :, :] if dims == 3 else tile[:, :, :, :]
                sp.dma_start(dst, io[name]).then_inc(s_w, 16)

            def load(b, r):
                s_x1b[r].wait(sp, b, 0)
                sp.dma_start(x1[r][:, :, :].rearrange("p a b -> p (a b)"),
                             x1_dram[bass.ds(2 * b + r, 1)].rearrange("o p c -> p (o c)"))\
                    .then_inc(s_in[r].sem, 16)
                s_kv_ps[r].wait(sp, b, 0)
                sp.dma_start(ctxT[r][:, :, :], io["ctxT"][bass.ds(2 * b + r, 1)].rearrange(
                    "o (i p) c -> p (o i) c", p=P)).then_inc(s_in[r].sem, 16)

            def store(b, r):
                s_x2[r].wait(sp, b, 1)
                sp.dma_start(x2_dram[bass.ds(2 * b + r, 1)].rearrange("o p c -> p (o c)"),
                             x2[r][:, :, :].rearrange("p a b -> p (a b)")).then_inc(s_out[r].sem, 16)
                s_xnT[1][r].wait(sp, b, 1)
                sp.dma_start(h_dram[bass.ds(2 * b + r, 1)].rearrange("o p c -> p (o c)"),
                             hT[r][:, :, :].rearrange("p a b -> p (a b)")).then_inc(s_out[r].sem, 16)

            for r in range(2):
                load(0, r)
            with sp.Fori(0, PAIRS - 1) as b:
                for r in range(2):
                    load(b + 1, r)
                    store(b, r)
            for r in range(2):
                store(PAIRS - 1, r)
            for r in range(2):
                s_out[r].wait_all(sp, PAIRS)

        @block.tensor
        def _(pe):
            prime(pe, s_kv_ps, *s_xnT_ps)
            pe.wait_ge(s_w, 16 * len(loads))

            def context(b, r):
                s_in[r].wait(pe, b, 32)
                s_t2[r].wait(pe, b, 0)
                for f in range(CT):
                    for c in range(CT):
                        m = pe.matmul(bank(r, 0)[:, f * P:f * P + CTX], w_x[:, 1, c, f * P:(f + 1) * P],
                                      ctxT[r][:, c, :], start=(c == 0), stop=(c == CT - 1))
                m.then_inc(s_kv_ps[r].sem, 1)
                for c in range(CT):
                    m = pe.matmul(bank(r, 1)[0:CTX, 0:C], ctxT[r][:, c, :], w_x[:, 2, c, :],
                                  start=(c == 0), stop=(c == CT - 1))
                m.then_inc(s_kv_ps[r].sem, 1)

            def transposes(b, r, k):
                s_xn[k][r].wait(pe, b, 2)
                if k == 0:
                    s_o2[r].wait(pe, b, 0)
                for i in range(TT):
                    for c in range(CT):
                        m = pe.transpose(bank(r, 2)[:, c * T + i * P:c * T + (i + 1) * P],
                                         xn[r][:, k, i, c * P:(c + 1) * P], ident[:, :])
                m.then_inc(s_xnT_ps[k][r].sem, 1)

            def queries(b, r):
                s_xnT[0][r].wait(pe, b, 1)
                s_x2[r].wait(pe, b, 0)
                for f in range(CT):
                    for c in range(CT):
                        m = pe.matmul(bank(r, 3)[:, f * T:(f + 1) * T], w_x[:, 0, c, f * P:(f + 1) * P],
                                      xnT[r][:, c, :], start=(c == 0), stop=(c == CT - 1))
                m.then_inc(s_q2_ps[r].sem, 1)

            def scores(b, r, i):
                if i:
                    s_sub2[r].wait(pe, b, 2 * i)
                else:
                    s_q2[r].wait(pe, b, 1)
                    s_kbd[r].wait(pe, b, 1)
                    s_kv[r].wait(pe, b, 2)
                    s_xnT[1][r].wait(pe, b, 0)
                for f in range(CT):
                    for n in range(2):
                        m = pe.matmul(bank(r, 2 * f + n)[:, 0:4 * CTX], q2[r][:, f, i * P:(i + 1) * P],
                                      Kbd[r][:, f, 4 * n:4 * n + 4, :].rearrange("p a b -> p (a b)"),
                                      start=True, stop=True)
                m.then_inc(s_s2[r].sem, 1)

            def probs_transposes(b, r, i):
                s_n2[r].wait(pe, b, i + 1)
                s_sub2[r].wait(pe, b, 4)
                for n in range(4):
                    k = 4 * i + n
                    if k >= 2:
                        s_t2[r].wait(pe, b, k - 1)
                    for m4 in range(4):
                        m = pe.transpose(bank(r, n % 2)[0:CTX, m4 * P:(m4 + 1) * P],
                                         P2[r][:, i, 4 * n + m4, :], ident[:, :])
                    m.then_inc(s_t2_ps[r].sem, 1)

            def values(b, r):
                s_t2[r].wait(pe, b, 8)
                for w in range(2):
                    for pair in range(HEADS // 2):
                        j, f = pair % 4, pair // 4
                        m = pe.matmul(bank(r, 2)[32 * j:32 * (j + 1), f * T:(f + 1) * T],
                                      Vz[r][:, pair, w, :, :].rearrange("p a b -> p (a b)"),
                                      PT2[r][0:CTX, 2 * pair + w, :], start=(w == 0 and f == 0), stop=(w == 1),
                                      skip_group_check=True)
                m.then_inc(s_o2_ps[r].sem, 1)

            def output(b, r):
                s_o2[r].wait(pe, b, 1)
                for i in range(TT):
                    for f in range(CT):
                        m = pe.matmul(bank(r, 3)[:, i * C:(i + 1) * C], O2T[r][:, f, i * P:(i + 1) * P],
                                      w_x[:, 3, f, :], start=(f == 0), stop=(f == CT - 1))
                m.then_inc(s_y2_ps[r].sem, 1)

            rows(pe, {6: [context], 7: [tile(transposes, 0), queries]},
                 {0: [tile(scores, 0)], 4: [tile(scores, 1)]},
                 {3: [tile(probs_transposes, 0)], 5: [tile(probs_transposes, 1)], 6: [values], 7: [output],
                  8: [tile(transposes, 1)]})

        @block.scalar
        def _(act):
            prime(act, s_t2, s_o2, s_xnT[1])

            def copy(out, src, sig):
                act.activation(out, src, ACT.Copy).then_inc(sig.sem, 1)

            def normed(b, r, k):
                s_xnT_ps[k][r].wait(act, b, 1)
                if k:
                    s_out[r].wait(act, b, 0)
                copy((hT if k else xnT)[r][:, :, :].rearrange("p a b -> p (a b)"), bank(r, 2), s_xnT[k][r])

            def exps(b, r, i):
                s_sub2[r].wait(act, b, 2 * i + 2)
                p = P2[r][:, i, :, :].rearrange("p h k -> p (h k)")
                act.activation(p, p, ACT.Exp).then_inc(s_e2[r].sem, 1)

            def evacuate(b, r, i):
                for n in range(4):
                    s_t2_ps[r].wait(act, b, 4 * i + n + 1)
                    copy(PT2[r][0:CTX, 4 * n:4 * n + 4, i * P:(i + 1) * P],
                         bank(r, n % 2)[0:CTX, :].rearrange("p (h t) -> p h t", h=4), s_t2[r])

            def heads_out(b, r):
                s_o2_ps[r].wait(act, b, 1)
                copy(O2T[r][:, :, :].rearrange("p a b -> p (a b)"), bank(r, 2), s_o2[r])

            rows(act, {7: [tile(normed, 0)]},
                 {3: [tile(exps, 0)], 5: [tile(exps, 1)]},
                 {3: [tile(evacuate, 0)], 5: [tile(evacuate, 1)], 6: [heads_out], 8: [tile(normed, 1)]})

        @block.gpsimd
        def _(pool):
            prime(pool, s_x1b)
            for r in range(2):
                pool.memset(Vz[r][:, :, :, :, :], 0.0).then_inc(s_init, 1)
            pool.memset(minus_half[:, :], -0.5).then_inc(s_init, 1)
            pool.wait_ge(s_w, 16 * len(loads))
            pool.wait_ge(s_init, 3)

            def inverse_root(b, r, k):
                s_ln[k][r].wait(pool, b, 5)
                pool.tensor_tensor(rstd[r][:, k, :], vareps[r][:, k, :], minus_half[:, :], ALU.pow)\
                    .then_inc(s_rstd[k][r].sem, 1)

            def biased(b, r):
                s_in[r].wait(pool, b, 32)
                s_x2[r].wait(pool, b, 0)
                s_xn[0][r].wait(pool, b, 2)
                pool.tensor_tensor(x1b[r][:, :, :], x1[r][:, :, :],
                                   xrow[:, 1:2, :].to_broadcast([P, TT, C]), ALU.add)\
                    .then_inc(s_x1b[r].sem, 1)

            def blocks(b, r):
                s_kv[r].wait(pool, b, 1)
                for f in range(CT):
                    m = pool.tensor_tensor(Kbd[r][:, f, :, :], kT2[r][:, f:f + 1, :].to_broadcast([P, XH, CTX]),
                                           own16[:, :].unsqueeze(2).to_broadcast([P, XH, CTX]), ALU.mult)
                m.then_inc(s_kbd[r].sem, 1)

            def normalise(b, r, i):
                s_r2[r].wait(pool, b, 2 * i + 2)
                pool.tensor_tensor(P2[r][:, i, :, :], P2[r][:, i, :, :],
                                   ri2[r][:, i, :].unsqueeze(2).to_broadcast([P, HEADS, CTX]), ALU.mult)\
                    .then_inc(s_n2[r].sem, 1)

            rows(pool, {4: [tile(inverse_root, 0)], 6: [blocks], 9: [biased]},
                 {6: [tile(normalise, 0)], 8: [tile(normalise, 1)]},
                 {7: [tile(inverse_root, 1)]})

        @block.vector
        def _(dve):
            prime(dve, s_x2)
            dve.sem_inc(s_hmax.sem, s_hmax.first)
            dve.wait_ge(s_w, 16 * len(loads))
            dve.wait_ge(s_init, 3)

            def statistics(b, r, k):
                src = (x2 if k else x1)[r]
                (s_x2 if k else s_in)[r].wait(dve, b, 1 if k else 32)
                for i in range(TT):
                    dve.bn_stats(stats[r][:, k, i, :], src[:, i, :]).then_inc(s_ln[k][r].sem, 1)
                s_ln[k][r].wait(dve, b, 2)
                dve.tensor_copy(held[r][:, 0:1], stats[r][:, k, 0, 0:1])
                for i in range(TT):
                    dve.bn_aggr(meanvar[r][:, k, i, :], stats[r][:, k, i, :]).then_inc(s_ln[k][r].sem, 1)
                s_ln[k][r].wait(dve, b, 4)
                dve.tensor_scalar(vareps[r][:, k, :], meanvar[r][:, k, :, 1], LN_EPS, None, ALU.add)\
                    .then_inc(s_ln[k][r].sem, 1)

            def norm(b, r, k):
                src = (x2 if k else x1)[r]
                s_rstd[k][r].wait(dve, b, 1)
                s_xnT_ps[k][r].wait(dve, b, 0)
                for i in range(TT):
                    dve.tensor_scalar(xn[r][:, k, i, :], src[:, i, :], meanvar[r][:, k, i, 0:1], rstd[r][:, k, i:i + 1],
                                      ALU.subtract, ALU.mult).then_inc(s_xn[k][r].sem, 1)

            def context(b, r):
                s_kv_ps[r].wait(dve, b, 1)
                for f in range(CT):
                    m = dve.tensor_scalar(kT2[r][:, f, :], bank(r, 0)[:, f * P:f * P + CTX], xb[:, 1, f:f + 1],
                                          None, ALU.add)
                m.then_inc(s_kv[r].sem, 1)
                s_kv_ps[r].wait(dve, b, 2)
                for w in range(2):
                    m = dve.tensor_tensor(
                        Vz[r][:, :, w, w, :],
                        bank(r, 1)[0:CTX, 0:C].rearrange("p (a w d) -> p a w d", w=2, d=XD)[:, :, w, :],
                        xrow[0:CTX, 0, :].rearrange("p (a w d) -> p a w d", w=2, d=XD)[:, :, w, :], ALU.add)
                m.then_inc(s_kv[r].sem, 1)

            def queries(b, r):
                s_q2_ps[r].wait(dve, b, 1)
                for f in range(CT):
                    m = dve.tensor_scalar(q2[r][:, f, :], bank(r, 3)[:, f * T:(f + 1) * T], xb[:, 0, f:f + 1],
                                          XD ** -0.5, ALU.add, ALU.mult)
                m.then_inc(s_q2[r].sem, 1)

            def shift(b, r, i):
                s_s2[r].wait(dve, b, i + 1)
                S = ps[:, 4 * r:4 * r + 4, 0:4 * CTX].rearrange("p f (h k) -> p f h k", k=CTX)
                dve.tensor_reduce(nmax2[r][:, :].rearrange("p (f h) -> p f h", f=4), S, AX.X, ALU.max,
                                  negate=True).then_inc(s_sub2[r].sem, 1)
                s_sub2[r].wait(dve, b, 2 * i + 1)
                dve.tensor_tensor(P2[r][:, i, :, :].rearrange("p (f h) k -> p f h k", f=4), S,
                                  nmax2[r][:, :].rearrange("p (f h) -> p f h", f=4).unsqueeze(3)
                                  .to_broadcast([P, 4, 4, CTX]), ALU.add).then_inc(s_sub2[r].sem, 1)

            def sums(b, r, i):
                s_e2[r].wait(dve, b, i + 1)
                dve.tensor_reduce(rs2[r][:, i, :], P2[r][:, i, :, :], AX.X, ALU.add).then_inc(s_r2[r].sem, 1)
                s_r2[r].wait(dve, b, 2 * i + 1)
                dve.reciprocal(ri2[r][:, i, :], rs2[r][:, i, :]).then_inc(s_r2[r].sem, 1)

            def residual(b, r):
                s_y2_ps[r].wait(dve, b, 1)
                s_x1b[r].wait(dve, b, 1)
                s_out[r].wait(dve, b, 0)
                dve.tensor_tensor(x2[r][:, :, :].rearrange("p a b -> p (a b)"), bank(r, 3),
                                  x1b[r][:, :, :].rearrange("p a b -> p (a b)"), ALU.add)\
                    .then_inc(s_x2[r].sem, 1)

            def largest(b, r):
                s_xn[1][r].wait(dve, b, 2)
                dve.tensor_reduce(hm[r][:, :], xn[r][:, 1, :, :].rearrange("p a b -> p (a b)"), AX.X, ALU.max,
                                  apply_absolute_value=True).then_inc(s_hm[r].sem, 1)
                s_hm[r].wait(dve, b, 1)
                s_hmax.wait(dve, b, r)
                dve.tensor_tensor(hmax[:, :], hmax[:, :], hm[r][:, :], ALU.max).then_inc(s_hmax.sem, 1)

            rows(dve, {4: [tile(statistics, 0)], 6: [tile(norm, 0), context], 8: [queries]},
                 {3: [tile(shift, 0)], 5: [tile(shift, 1)], 6: [tile(sums, 0), tile(sums, 1)]},
                 {7: [residual, tile(statistics, 1)], 8: [tile(norm, 1)], 9: [largest]})


def feed_forward(nc, io, h_dram, x2_dram, u_dram, ident, hmax):
    with ExitStack() as ctx:
        def sb(name, shape, dt=F32):
            return ctx.enter_context(nc.sbuf_tensor(name, shape, dt))

        def signal(name, per=1, first=0):
            return Signal(ctx.enter_context(nc.semaphore("s_" + name)), per, first)

        def prime(eng, *signals):
            for s in signals:
                eng.sem_inc(s.sem, s.first)

        NB = INNER * C // P // BLK
        WC = INNER * C // P
        G = sb("G", [P, B, IT * T])
        wT = [sb("wgT", [P, CT, INNER]), sb("wuT", [P, CT, INNER]), sb("wdT", [P, IT, C])]
        wn = sb("wn", [P, WC])
        wq = sb("wq", [P, WC])
        wmax = sb("wmax", [P, NB])
        wscale = sb("wscale", [P, NB])
        winv = sb("winv", [P, NB])
        hin = sb("hin", [P, 2, CT * T])
        hq = sb("hq", [P, 2, CT * T])
        ubuf = sb("ubuf", [P, 2, IT * T])
        t1 = sb("t1", [P, IT * T])
        t2 = sb("t2", [P, IT * T])
        t3 = sb("t3", [P, IT * T])
        am = sb("am", [P, IT, 2])
        amc = sb("amc", [P, 2])
        held = sb("held3", [P, 1])
        run = sb("run", [P, 4])
        tot = sb("tot", [P, 5])
        sc = sb("sc", [P, 5])
        raw = sb("raw", [P, 5])
        inv = sb("inv", [P, 5])
        tmp = sb("tmp", [P, 5])
        xres = sb("xres", [P, 2, TT * C])
        yout = sb("yout", [P, 2, TT * C])
        ps = ctx.enter_context(nc.psum_tensor("ps2", [P, 8, 512], F32))
        GATE, UP, PROD, OUTQ, INP = range(5)

        s_wn = signal("w_loaded", 0)
        s_wop = signal("w_ops", 0)
        s_wt_ps = signal("wT_ps", 0)
        s_wt = signal("wT", 0)
        s_tot = signal("total_max", 0)
        s_sc = signal("scale_ops", 0)
        s_zero = signal("zeroed", 0)
        s_h = signal("h_loaded", 32)
        s_hr = signal("h_raised", 2, first=1)
        s_hq = signal("h_quantised", 2, first=1)
        s_gu_ps = signal("gu_ps", 2 * IT, first=1)
        s_gu = signal("gu_copied", 2 * IT, first=1)
        s_gum = signal("gu_max", 2 * IT, first=1)
        s_amc = signal("a_block_max", 2)
        s_run_a = signal("a_running", 2)
        s_ust = signal("u_stored", 32, first=1)
        s_gr = signal("g_raised", 1)
        s_gq = signal("g_quantised", 1)
        s_sig = signal("sigmoid", 1)
        s_sr = signal("sigmoid_raised", 1)
        s_sqz = signal("sigmoid_quantised", 1)
        s_gp = signal("g_product", 1, first=1)
        s_bm = signal("b_block_max", 1)
        s_run_b = signal("b_running", 1)
        s_u = signal("u_loaded", 16)
        s_ur = signal("u_raised", 1, first=1)
        s_uq = signal("u_quantised", 1)
        s_pr = signal("p_raised", 1)
        s_pq = signal("p_quantised", 1)
        s_op = signal("o_product", 1, first=1)
        s_cm = signal("c_block_max", 1)
        s_run_c = signal("c_running", 1)
        s_or = signal("o_raised", 2)
        s_oq = signal("o_quantised", 2)
        s_xr = signal("x_loaded2", 32)
        s_y_ps = signal("y_ps", 4, first=1)
        s_y = signal("y", 4, first=1)
        s_yst = signal("y_stored", 32, first=1)

        block = ctx.enter_context(nc.Block())
        names = ["ffn_gate", "ffn_up", "ffn_down"]

        def at_block(eng_block):
            return G[:, bass.ds(eng_block, 1), :].rearrange("p o c -> p (o c)")

        @block.sync
        def _(sp):
            prime(sp, s_ust, s_yst)
            for n, name in enumerate(names):
                if n:
                    sp.wait_ge(s_wop.sem, 8 * n)
                sp.dma_start(wn[:, :], io[name]).then_inc(s_wn.sem, 16)
            with sp.Fori(0, B // 2) as bb:
                for k in range(2):
                    s_hr.wait(sp, bb, 0)
                    sp.dma_start(hin[:, k, :], h_dram[bass.ds(bb * 2 + k, 1)].rearrange("o p c -> p (o c)"))\
                        .then_inc(s_h.sem, 16)
                for k in range(2):
                    s_gu.wait(sp, bb, IT * (k + 1))
                    sp.dma_start(u_dram[bass.ds(bb * 2 + k, 1)].rearrange("o p c -> p (o c)"), ubuf[:, k, :])\
                        .then_inc(s_ust.sem, 16)
            s_ust.wait_all(sp, B // 2)
            with sp.Fori(0, B) as c:
                s_ur.wait(sp, c, 0)
                sp.dma_start(ubuf[:, 0, :], u_dram[bass.ds(c, 1)].rearrange("o p c -> p (o c)"))\
                    .then_inc(s_u.sem, 16)
            with sp.Fori(0, B // 2) as bb:
                for k in range(2):
                    s_y.wait(sp, bb, 0)
                    sp.dma_start(xres[:, k, :], x2_dram[bass.ds(bb * 2 + k, 1)].rearrange("o p c -> p (o c)"))\
                        .then_inc(s_xr.sem, 16)
                for k in range(2):
                    s_y.wait(sp, bb, 2 * (k + 1))
                    sp.dma_start(io["out"][bass.ds(bb * 2 + k, 1)].rearrange("o (i p) c -> p (o i) c", p=P),
                                 yout[:, k, :].rearrange("p (i c) -> p i c", i=TT)).then_inc(s_yst.sem, 16)
            s_yst.wait_all(sp, B // 2)

        @block.gpsimd
        def _(pool):
            pool.memset(run[:, :], 0.0).then_inc(s_zero.sem, 1)
            red = bass.bass_isa.ReduceOp.max
            pool.partition_all_reduce(tot[:, INP:INP + 1], hmax[:, :], P, red).then_inc(s_tot.sem, 1)
            s_run_a.wait_all(pool, B // 2)
            pool.partition_all_reduce(tot[:, GATE:UP + 1], run[:, GATE:UP + 1], P, red).then_inc(s_tot.sem, 1)
            s_run_b.wait_all(pool, B)
            pool.partition_all_reduce(tot[:, PROD:PROD + 1], run[:, PROD:PROD + 1], P, red)\
                .then_inc(s_tot.sem, 1)
            s_run_c.wait_all(pool, B)
            pool.partition_all_reduce(tot[:, OUTQ:OUTQ + 1], run[:, OUTQ:OUTQ + 1], P, red)\
                .then_inc(s_tot.sem, 1)

        @block.tensor
        def _(pe):
            prime(pe, s_gu_ps, s_y_ps)
            for n in range(3):
                pe.wait_ge(s_wop.sem, 8 * (n + 1))
                rows, cols = ((IT, CT), (IT, CT), (CT, IT))[n]
                w = wq[:, :].rearrange("p (r c) -> p r c", r=rows)
                order = [(r, c) for c in range(cols) for r in range(rows)]
                for k, (r, c) in enumerate(order):
                    q = 12 * n + k
                    if q >= 8 and k % 4 == 0:
                        pe.wait_ge(s_wt.sem, q // 4 - 1)
                    m = pe.transpose(ps[:, (q // 4) % 2, (q % 4) * P:(q % 4 + 1) * P],
                                     w[:, r, c * P:(c + 1) * P], ident[:, :])
                    if k % 4 == 3:
                        m.then_inc(s_wt_ps.sem, 1)
            pe.wait_ge(s_wt.sem, 9)
            with pe.Fori(0, B // 2) as bb:
                for k in range(2):
                    s_hq.wait(pe, bb, k + 1)
                    for it in range(IT):
                        n = k * IT + it
                        if n >= 6:
                            s_gu.wait(pe, bb, n - 5)
                            s_gum.wait(pe, bb, n - 5)
                        elif n == 0:
                            s_gu.wait(pe, bb, 0)
                            s_gum.wait(pe, bb, 0)
                        for w in range(2):
                            for c in range(CT):
                                m = pe.matmul(ps[:, n % 6, w * T:(w + 1) * T],
                                              wT[w][:, c, it * P:(it + 1) * P],
                                              hq[:, k, c * T:(c + 1) * T], start=(c == 0), stop=(c == CT - 1))
                        m.then_inc(s_gu_ps.sem, 1)
            with pe.Fori(0, B // 2) as bb:
                for k in range(2):
                    s_oq.wait(pe, bb, k + 1)
                    for i in range(TT):
                        n = 2 * k + i
                        if n == 0:
                            s_y.wait(pe, bb, 0)
                        for it in range(IT):
                            m = pe.matmul(ps[:, n, 0:C], (t2, t3)[k][:, it * T + i * P:it * T + (i + 1) * P],
                                          wT[2][:, it, :], start=(it == 0), stop=(it == IT - 1))
                        m.then_inc(s_y_ps.sem, 1)

        def raised(act, out, src, stage, sig):
            act.activation(out, src, ACT.Copy, scale=inv[:, stage:stage + 1], bias=MAGIC).then_inc(sig.sem, 1)

        @block.scalar
        def _(act):
            prime(act, s_gu, s_hr, s_ur)
            for q in range(9):
                act.wait_ge(s_wt_ps.sem, q + 1)
                n, k = q // 3, q % 3
                flat = wT[n][:, :, :].rearrange("p a b -> p (a b)")
                act.activation(flat[:, k * 512:(k + 1) * 512], ps[:, q % 2, :], ACT.Copy)\
                    .then_inc(s_wt.sem, 1)
            act.wait_ge(s_sc.sem, 4)
            with act.Fori(0, B // 2) as bb:
                s_h.wait(act, bb, 32)
                for k in range(2):
                    s_hq.wait(act, bb, 0)
                    raised(act, t1[:, k * CT * T:(k + 1) * CT * T], hin[:, k, :], INP, s_hr)
                for k in range(2):
                    for it in range(IT):
                        n = k * IT + it
                        s_gu_ps.wait(act, bb, n + 1)
                        if it == 0:
                            s_ust.wait(act, bb, 0)
                        act.activation(at_block(bb * 2 + k)[:, it * T:(it + 1) * T], ps[:, n % 6, 0:T], ACT.Copy)
                        act.activation(ubuf[:, k, it * T:(it + 1) * T], ps[:, n % 6, T:2 * T], ACT.Copy)\
                            .then_inc(s_gu.sem, 1)
            act.wait_ge(s_sc.sem, 12)
            with act.Fori(0, B) as c:
                s_gp.wait(act, c, 0)
                raised(act, t1[:, :], at_block(c), GATE, s_gr)
                s_gq.wait(act, c, 1)
                act.activation(t2[:, :], t1[:, :], ACT.Sigmoid, scale=sc[:, GATE:GATE + 1]).then_inc(s_sig.sem, 1)
                s_sig.wait(act, c, 1)
                act.activation(t2[:, :], t2[:, :], ACT.Copy, scale=65536.0, bias=MAGIC).then_inc(s_sr.sem, 1)
            act.wait_ge(s_sc.sem, 18)
            with act.Fori(0, B) as c:
                s_op.wait(act, c, 0)
                s_u.wait(act, c, 16)
                raised(act, t1[:, :], ubuf[:, 0, :], UP, s_ur)
                raised(act, t2[:, :], at_block(c), PROD, s_pr)
            act.wait_ge(s_sc.sem, 24)
            with act.Fori(0, B // 2) as bb:
                for k in range(2):
                    s_y_ps.wait(act, bb, 0)
                    raised(act, (t2, t3)[k][:, :], at_block(bb * 2 + k), OUTQ, s_or)

        @block.vector
        def _(dve):
            prime(dve, s_gp, s_gum, s_hq, s_op, s_y)
            for n in range(3):
                k = 8 * n
                op = lambda ins: ins.then_inc(s_wop.sem, 1)
                wb = wn[:, :].rearrange("p (n e) -> p n e", e=BLK)
                qb = wq[:, :].rearrange("p (n e) -> p n e", e=BLK)
                dve.wait_ge(s_wn.sem, 16 * (n + 1))
                if n:
                    dve.wait_ge(s_wt_ps.sem, 3 * n)
                op(dve.tensor_reduce(wmax[:, :], wb, AX.X, ALU.max, apply_absolute_value=True))
                dve.wait_ge(s_wop.sem, k + 1)
                op(dve.tensor_scalar(wscale[:, :], wmax[:, :], 1.0 / 7.0, 1e-12, ALU.mult, ALU.max))
                dve.wait_ge(s_wop.sem, k + 2)
                op(dve.reciprocal(winv[:, :], wscale[:, :]))
                dve.wait_ge(s_wop.sem, k + 3)
                bc = lambda a: a[:, :].unsqueeze(2).to_broadcast([P, NB, BLK])
                op(dve.tensor_tensor(qb, wb, bc(winv), ALU.mult))
                dve.wait_ge(s_wop.sem, k + 4)
                op(dve.tensor_scalar(wq[:, :], wq[:, :], MAGIC, None, ALU.add))
                dve.wait_ge(s_wop.sem, k + 5)
                op(dve.tensor_scalar(wq[:, :], wq[:, :], MAGIC, 7.0, ALU.subtract, ALU.min))
                dve.wait_ge(s_wop.sem, k + 6)
                op(dve.tensor_scalar(wq[:, :], wq[:, :], -8.0, None, ALU.max))
                dve.wait_ge(s_wop.sem, k + 7)
                op(dve.tensor_tensor(qb, qb, bc(wscale), ALU.mult))

            def scales(first, stage, unit):
                n = first
                t, s, v = tot[:, stage:stage + 1], sc[:, stage:stage + 1], inv[:, stage:stage + 1]
                m = tmp[:, stage:stage + 1]
                if unit is None:
                    dve.tensor_scalar(m, t, 1.0, None, ALU.mult).then_inc(s_sc.sem, 1)
                else:
                    dve.tensor_scalar(m, t, unit, None, ALU.mult).then_inc(s_sc.sem, 1)
                dve.wait_ge(s_sc.sem, n + 1)
                dve.tensor_scalar(s, m, 1.0 / QMAX, 1e-12, ALU.mult, ALU.max).then_inc(s_sc.sem, 1)
                dve.wait_ge(s_sc.sem, n + 2)
                dve.reciprocal(v, s).then_inc(s_sc.sem, 1)
                dve.wait_ge(s_sc.sem, n + 3)
                if unit is None:
                    dve.tensor_scalar(v, v, 1.0, None, ALU.mult).then_inc(s_sc.sem, 1)
                else:
                    dve.tensor_scalar(v, v, unit, None, ALU.mult).then_inc(s_sc.sem, 1)
                return n + 4

            dve.wait_ge(s_zero.sem, 1)
            dve.wait_ge(s_tot.sem, 1)
            n = scales(0, INP, None)
            dve.wait_ge(s_sc.sem, n)
            with dve.Fori(0, B // 2) as bb:
                for k in range(2):
                    s_hr.wait(dve, bb, k + 1)
                    s_gu_ps.wait(dve, bb, 0)
                    dve.tensor_scalar(hq[:, k, :], t1[:, k * CT * T:(k + 1) * CT * T], MAGIC, QMAX,
                                      ALU.subtract, ALU.min).then_inc(s_hq.sem, 1)
                for k in range(2):
                    if k:
                        s_amc.wait(dve, bb, k)
                    for it in range(IT):
                        n_ = k * IT + it
                        s_gu_ps.wait(dve, bb, n_ + 1)
                        s_gu.wait(dve, bb, n_ + 1)
                        dve.tensor_reduce(am[:, it, :], ps[:, n_ % 6, :].rearrange("p (a t) -> p a t", a=2),
                                          AX.X, ALU.max, apply_absolute_value=True).then_inc(s_gum.sem, 1)
                    s_gum.wait(dve, bb, (k + 1) * IT)
                    dve.tensor_reduce(amc[:, :], am[:, :, :].rearrange("p i a -> p a i"), AX.X, ALU.max)\
                        .then_inc(s_amc.sem, 1)
                    s_amc.wait(dve, bb, k + 1)
                    dve.tensor_tensor(run[:, 0:2], run[:, 0:2], amc[:, :], ALU.max).then_inc(s_run_a.sem, 1)
                    s_run_a.wait(dve, bb, k + 1)
            dve.wait_ge(s_tot.sem, 2)
            n = scales(4, GATE, sc[:, INP:INP + 1])
            n = scales(n, UP, sc[:, INP:INP + 1])
            dve.wait_ge(s_sc.sem, n)
            with dve.Fori(0, B) as c:
                s_gr.wait(dve, c, 1)
                dve.tensor_scalar(t1[:, :], t1[:, :], MAGIC, QMAX, ALU.subtract, ALU.min).then_inc(s_gq.sem, 1)
                s_sr.wait(dve, c, 1)
                dve.tensor_scalar(t2[:, :], t2[:, :], MAGIC, 65535.0, ALU.subtract, ALU.min)\
                    .then_inc(s_sqz.sem, 1)
                s_sqz.wait(dve, c, 1)
                dve.tensor_tensor(at_block(c), t1[:, :], t2[:, :], ALU.mult).then_inc(s_gp.sem, 1)
                s_gp.wait(dve, c, 1)
                dve.tensor_copy(held[:, :], run[:, 0:1])
                dve.tensor_reduce(amc[:, 0:1], at_block(c), AX.X, ALU.max, apply_absolute_value=True)\
                    .then_inc(s_bm.sem, 1)
                s_bm.wait(dve, c, 1)
                dve.tensor_tensor(run[:, PROD:PROD + 1], run[:, PROD:PROD + 1], amc[:, 0:1], ALU.max)\
                    .then_inc(s_run_b.sem, 1)
                s_run_b.wait(dve, c, 1)
            dve.wait_ge(s_tot.sem, 3)
            dve.tensor_scalar(raw[:, PROD:PROD + 1], sc[:, GATE:GATE + 1], 1.0 / 65536.0, None, ALU.mult)\
                .then_inc(s_sc.sem, 1)
            dve.wait_ge(s_sc.sem, 13)
            n = scales(13, PROD, raw[:, PROD:PROD + 1])
            dve.wait_ge(s_sc.sem, n)
            dve.tensor_scalar(raw[:, OUTQ:OUTQ + 1], sc[:, PROD:PROD + 1], sc[:, UP:UP + 1], None, ALU.mult)\
                .then_inc(s_sc.sem, 1)
            with dve.Fori(0, B) as c:
                s_ur.wait(dve, c, 1)
                dve.tensor_scalar(t1[:, :], t1[:, :], MAGIC, QMAX, ALU.subtract, ALU.min).then_inc(s_uq.sem, 1)
                s_pr.wait(dve, c, 1)
                dve.tensor_scalar(t2[:, :], t2[:, :], MAGIC, QMAX, ALU.subtract, ALU.min).then_inc(s_pq.sem, 1)
                s_uq.wait(dve, c, 1)
                s_pq.wait(dve, c, 1)
                dve.tensor_tensor(at_block(c), t1[:, :], t2[:, :], ALU.mult).then_inc(s_op.sem, 1)
                s_op.wait(dve, c, 1)
                dve.tensor_copy(held[:, :], run[:, 0:1])
                dve.tensor_reduce(amc[:, 0:1], at_block(c), AX.X, ALU.max, apply_absolute_value=True)\
                    .then_inc(s_cm.sem, 1)
                s_cm.wait(dve, c, 1)
                dve.tensor_tensor(run[:, OUTQ:OUTQ + 1], run[:, OUTQ:OUTQ + 1], amc[:, 0:1], ALU.max)\
                    .then_inc(s_run_c.sem, 1)
                s_run_c.wait(dve, c, 1)
            dve.wait_ge(s_tot.sem, 4)
            dve.wait_ge(s_sc.sem, 18)
            n = scales(18, OUTQ, raw[:, OUTQ:OUTQ + 1])
            dve.wait_ge(s_sc.sem, n)
            dve.tensor_scalar(tmp[:, 0:2], sc[:, 0:2], 1.0, None, ALU.mult).then_inc(s_sc.sem, 1)
            dve.tensor_scalar(tmp[:, 2:4], sc[:, 0:2], 1.0, None, ALU.mult).then_inc(s_sc.sem, 1)
            with dve.Fori(0, B // 2) as bb:
                for k in range(2):
                    s_or.wait(dve, bb, k + 1)
                    t = (t2, t3)[k]
                    dve.tensor_scalar(t[:, :], t[:, :], MAGIC, QMAX, ALU.subtract, ALU.min)\
                        .then_inc(s_oq.sem, 1)
                s_xr.wait(dve, bb, 32)
                s_yst.wait(dve, bb, 0)
                for k in range(2):
                    for i in range(TT):
                        s_y_ps.wait(dve, bb, 2 * k + i + 1)
                        dve.scalar_tensor_tensor(yout[:, k, i * C:(i + 1) * C], ps[:, 2 * k + i, 0:C],
                                                 sc[:, OUTQ:OUTQ + 1], xres[:, k, i * C:(i + 1) * C],
                                                 ALU.mult, ALU.add).then_inc(s_y.sem, 1)



def _layouts(i):
    f = np.float32

    def rows(w):
        return w.reshape(w.shape[0] // P, P, -1).transpose(1, 0, 2)

    def below(w, first):
        out = np.zeros((P, w.shape[1]), f)
        out[first:first + w.shape[0]] = w
        return out

    def grouped(nope, rope):
        n = nope.shape[0]
        both = np.concatenate([nope.reshape(n, HEADS, 1, PART), rope.reshape(n, HEADS, 2, PART)], axis=2)
        return both.reshape(n, GROUPS, GROUP, PARTS, PART).transpose(0, 1, 3, 2, 4).reshape(n, -1)

    def split(w):
        w = w.reshape(w.shape[0], HEADS, DK)
        return grouped(w[:, :, :PART], w[:, :, PART:])

    a = {k: np.asarray(v) for k, v in i.items()}
    att = lambda n: a["L0_attn_" + n]
    xat = lambda n: a["L0_xattn_" + n]
    t = np.arange(T, dtype=f)
    freq = (1.0 / np.power(f(10000.0), np.arange(0, 2 * PART, 2, dtype=f) / f(2 * PART))).astype(f)
    angle = np.outer(t, freq).astype(f)
    cos, sin = np.cos(angle).T, np.sin(angle).T
    table = np.stack([np.tile(cos, (GROUP, 1)), np.tile(sin, (GROUP, 1))], 1).astype(f)
    p = np.arange(P)
    mask = np.where(p[None, :] > p[:, None], MASKED, 0.0).astype(f)
    kr = att("w_krope")
    bf = mybir.dt.np(BF16)
    return {
        "x": a["x"],
        "ctxT": a["ctx_1024"].transpose(0, 2, 1),
        "w_lat": rows(np.concatenate([att("w_cq"), att("w_ckv"), att("w_gate")[:, GATE_ORDER]], axis=1)),
        "w_imp": rows(np.tile(att("w_imp"), (1, P))),
        "w_win": rows(split(att("w_wink"))),
        "w_sel": rows(split(att("w_selk"))),
        "w_winv": rows(att("w_winv")),
        "w_selv": rows(att("w_selv")),
        "w_q": below(grouped(att("w_dq_nope"), att("w_dq_rope")), 0),
        "w_kn": below(att("w_dk_nope"), QL),
        "w_v1": below(att("w_dv"), QL),
        "w_kr": rows(np.concatenate([np.tile(kr[:, :PART], (1, GROUP)), np.tile(kr[:, PART:], (1, GROUP))], 1)),
        "w_proj": rows(att("w_proj")),
        "w_x": np.stack([rows(xat(n).T) for n in ("Wq", "Wk", "Wv", "Wo")], axis=1),
        "g_lat": np.concatenate([att("g_qnorm"), att("g_kvnorm")])[:, None],
        "rope_k": table,
        "rope_q": (table * f(DK ** -0.5)).astype(f),
        "maskb": np.concatenate([mask, mask], axis=1).astype(bf),
        "identb": np.eye(P).astype(bf),
        "before": np.stack([(np.arange(T)[None, :] < (p + n * P)[:, None]) for n in range(TT)], 1).astype(f),
        "uptri": np.concatenate([(p[:, None] < p[None, :]).astype(f), np.ones((P, P), f)], axis=1),
        "iota64": np.tile(np.arange(KEEP, dtype=f), (P, 1)),
        "own16": (p[:, None] // XD == np.arange(XH)[None, :]).astype(f),
        "meanw": np.full((P, P), 1.0 / T, f),
        "xb": np.stack([xat("bq").reshape(CT, P).T, xat("bk").reshape(CT, P).T], axis=1),
        "xrow": np.stack([np.tile(xat("bv"), (P, 1)), np.tile(xat("bo"), (P, 1))], axis=1),
        "ident": np.eye(P, dtype=f),
        "ffn_gate": rows(a["L0_ffn_w_gate"]).reshape(P, -1),
        "ffn_up": rows(a["L0_ffn_w_up"]).reshape(P, -1),
        "ffn_down": rows(a["L0_ffn_w_down"]).reshape(P, -1),
    }


def kernel(**inputs):
    import concourse.bacc as bacc
    from concourse.bass_utils import run_bass_kernel_spmd

    nc = bacc.Bacc("TRN2", target_bir_lowering=False, num_devices=1)
    arrays = {"in_" + k: np.ascontiguousarray(v) for k, v in _layouts(inputs).items()}
    io = {k[3:]: nc.dram_tensor(k, v.shape, mybir.dt.from_np(v.dtype), kind="ExternalInput").ap()
          for k, v in arrays.items()}
    io["out"] = nc.dram_tensor("out", (B, T, C), F32, kind="ExternalOutput").ap()
    build(nc, io)
    r = run_bass_kernel_spmd(nc, [arrays], core_ids=[0])
    return r.results[0]["out"]
```

```python
from contextlib import ExitStack

import numpy as np
import concourse.bass as bass
from concourse import mybir

ALU = mybir.AluOpType
ACT = mybir.ActivationFunctionType
AX = mybir.AxisListType
F32 = mybir.dt.float32
BF16 = mybir.dt.bfloat16
FP16 = mybir.dt.float16

P = 128
ALL = slice(None)
B, T, C = 16, 256, 256
TT, CT = T // P, C // P
HEADS, GROUP = 16, 4
GROUPS = HEADS // GROUP
PART = 32
PARTS = 3
DK = PART * PARTS
VD = 32
KEEP = 64
QL, KVL = 96, 32
LC = QL + KVL + 3
CTX = 77
XD = C // HEADS
XH = P // XD
INNER = 768
IT = INNER // P
BLK = 32
MAGIC = 1.5 * 2.0 ** 23
QMAX = 32767.0
LN_EPS, RMS_EPS = 1e-5, 1e-6
MASKED = -1e30
WSCALE = 256.0
WIN, BASE, SEL = 0, 1, 2
GATE_ORDER = [2, 0, 1]
QC, WC0, SC0, BC0 = 0, T, 2 * T, 2 * T + KEEP
HCOLS = 3 * T + KEEP
S1, S0 = 64, 640
SEG = {(1, WIN): (0, 256), (1, SEL): (256, 64), (1, BASE): (320, 256),
       (0, WIN): (576, 128), (0, SEL): (704, 64), (0, BASE): (768, 128)}
PCOLS = 896
GDMA = 16 * GROUP * PARTS
PBUF = 4
LAG = 3


class Signal:

    def __init__(self, sem, per, first=0):
        self.sem, self.per, self.first = sem, per, first

    def wait(self, eng, b, k, from_pass=0):
        least = b if isinstance(b, int) else from_pass
        assert least * self.per + k + self.first > 0
        eng.wait_ge(self.sem, b * self.per + k + self.first)

    def wait_all(self, eng, passes):
        eng.wait_ge(self.sem, passes * self.per + self.first)


def build(nc, io):
    with ExitStack() as outer:
        x1_dram = nc.dram_tensor("x1_scratch", (B, P, TT * C), F32, kind="Internal").ap()
        h_dram = nc.dram_tensor("h_scratch", (B, P, CT * T), F32, kind="Internal").ap()
        x2_dram = nc.dram_tensor("x2_scratch", (B, P, TT * C), F32, kind="Internal").ap()
        u_dram = nc.dram_tensor("u_scratch", (B, P, IT * T), F32, kind="Internal").ap()
        ident = outer.enter_context(nc.sbuf_tensor("ident", [P, P], F32))
        hmax = outer.enter_context(nc.sbuf_tensor("hmax", [P, 1], F32))
        self_attention(nc, io, x1_dram, ident, hmax)
        cross_attention(nc, io, x1_dram, h_dram, x2_dram, ident, hmax)
        feed_forward(nc, io, h_dram, x2_dram, u_dram, ident, hmax)


def self_attention(nc, io, x1_dram, ident, hmax):
    with ExitStack() as ctx:
        def sb(name, shape, dt=F32):
            return ctx.enter_context(nc.sbuf_tensor(name, shape, dt))

        def signal(name, per=1, first=0):
            return Signal(ctx.enter_context(nc.semaphore("s_" + name)), per, first)

        def prime(eng, *signals):
            for s in signals:
                eng.sem_inc(s.sem, s.first)

        w_lat = sb("w_lat", [P, CT, LC])
        w_imp = sb("w_imp", [P, CT, P])
        def halved(name, shape):
            return [sb("%s_%s" % (name, n), shape, FP16) for n in ("upper", "lower")]

        w_win = halved("w_win", [P, CT, GROUPS * PARTS * P])
        w_sel = halved("w_sel", [P, CT, GROUPS * PARTS * P])
        w_winv = halved("w_winv", [P, CT, HEADS * VD])
        w_selv = halved("w_selv", [P, CT, HEADS * VD])
        w_q = halved("w_q", [P, GROUPS * PARTS * P])
        w_kn = halved("w_kn", [P, GROUPS * P])
        w_v1 = halved("w_v1", [P, HEADS * VD])
        w_kr = halved("w_kr", [P, CT, 2 * P])
        w_proj = sb("w_proj", [P, GROUPS, C])
        g_lat = sb("g_lat", [P, 1])
        rope_k = sb("rope_k", [P, 2, T])
        rope_q = sb("rope_q", [P, 2, T])
        maskb = sb("maskb", [P, 2 * P], BF16)
        identb = sb("identb", [P, P], BF16)
        before = sb("before", [P, TT, T])
        uptri = sb("uptri", [P, 2 * P])
        iota64 = sb("iota64", [P, KEEP])
        meanw = sb("meanw", [P, P])
        minus_half = sb("minus_half", [P, 4])
        xin = sb("xin", [P, TT, C])
        xres = sb("x_residual", [P, TT, C])
        stats = sb("stats", [P, TT, 6])
        meanvar = sb("meanvar", [P, TT, 2])
        vareps = sb("vareps", [P, TT])
        rstd = sb("rstd", [P, TT])
        xn = sb("xn", [P, TT, C])
        xnT = sb("xnT", [P, CT, T])
        xnT2 = halved("xnT", [P, CT, T])
        lat = sb("lat", [P, TT, LC])
        ms = sb("ms", [P, TT, 2])
        rlat = sb("rlat", [P, TT, 2])
        held = sb("held", [P, 4])
        nlat = sb("nlat", [P, TT, P])
        nT = sb("nT", [P, T])
        nT2 = halved("nT", [P, T])
        srow = sb("srow", [P, T])
        scol = sb("scol", [P, TT])
        cnt = sb("cnt", [P, TT])
        tie = sb("tie", [P, TT])
        chosen = sb("chosen", [P, TT])
        rank = sb("rank", [P, TT])
        pick = sb("pick", [P, TT, KEEP])
        selT = sb("selT", [P, CT, KEEP])
        selT2 = halved("selT", [P, CT, KEEP])
        gmax = sb("gmax", [P, 1])
        gexp = sb("gexp", [P, 3])
        gsum = sb("gsum", [P, 1])
        ginv = sb("ginv", [P, 1])
        gate = sb("gate", [P, 3])
        V = sb("V", [P, 5, HEADS * VD])
        rot1 = sb("rot1", [P, 2, 2, T])
        rot2 = sb("rot2", [P, 2, 2, T])
        junk, sq = rot1[:, 0], rot2[:, 0]
        st = sb("st", [P, 2, PARTS, HCOLS])
        QK = sb("QK", [DK, GROUPS, GROUP, HCOLS])
        nmax = sb("nmax", [P, 2, 6])
        rsum = sb("rsum", [P, 2, 6])
        rinv = sb("rinv", [P, 2, 6])
        coef = sb("coef", [P, 2, 6])
        Pr = sb("Pr", [P, PBUF, PCOLS])
        PT = sb("PT", [P, GROUP, 1024])
        OT = sb("OT", [P, GROUPS, T])
        x1 = sb("x1", [P, TT, C])

        ps = ctx.enter_context(nc.psum_tensor("ps", [P, 8, 512], F32))
        flat = ps[:, 0:4, :].rearrange("p a b -> p (a b)")
        b4, b5, bO, bM = ps[:, 4, :], ps[:, 5, :], ps[:, 6, :], ps[:, 7, :]

        loads = [
            (w_lat, "w_lat"), (w_imp, "w_imp"), (w_proj, "w_proj"), (g_lat, "g_lat"), (rope_k, "rope_k"), (rope_q, "rope_q"),
            (maskb, "maskb"), (identb, "identb"), (before, "before"), (uptri, "uptri"),
            (iota64, "iota64"), (meanw, "meanw"),
            (ident, "ident"),
        ]

        rooms = {"Pr": Pr[:, :, :].rearrange("p a b -> p (a b)"), "PT": PT[:, :, :].rearrange("p a b -> p (a b)"),
                 "st0": st[:, 0, :, :].rearrange("p a b -> p (a b)"),
                 "st1": st[:, 1, :, :].rearrange("p a b -> p (a b)")}
        to_halve = []
        taken = {}
        for tile, name, room in ((w_win, "w_win", "Pr"), (w_sel, "w_sel", "PT"), (w_kr, "w_kr", "PT"),
                                 (w_v1, "w_v1", "PT"), (w_winv, "w_winv", "st0"), (w_selv, "w_selv", "st0"),
                                 (w_q, "w_q", "st1"), (w_kn, "w_kn", "st1")):
            flat_ = [t[:, :] if len(t.shape) == 2 else t[:, :, :].rearrange("p a b -> p (a b)") for t in tile]
            size, at = flat_[0].shape[1], taken.get(room, 0)
            to_halve.append((name, flat_, rooms[room][:, at:at + size]))
            taken[room] = at + size

        s_w = signal("weights", 0)
        s_raw = signal("raw_weights", 0)
        s_upper = signal("upper_weights", 0)
        s_lower = signal("lower_weights", 0)
        s_init = signal("init", 0)
        s_x = signal("x_loaded", 16)
        s_xres = signal("residual_loaded", 16)
        s_ln = signal("ln_ops", 5)
        s_rstd = signal("ln_rstd", 1)
        s_xn = signal("ln_done", 2, first=1)
        s_xnT_ps = signal("xnT_ps", 1)
        s_xnT = signal("xnT", 2)
        s_low = signal("lower_halves", 3)
        s_lat_ps = signal("latent_ps", 1)
        s_lat = signal("latent", 1)
        s_ms = signal("mean_square", 4)
        s_rlat = signal("latent_rms", 1)
        s_nlat = signal("latent_normed", 4)
        s_nT_ps = signal("nT_ps", 1)
        s_nT = signal("nT", 2)
        s_gate_ps = signal("gate_ps", 1)
        s_gexp = signal("gate_exp", 1)
        s_gate = signal("gate", 3)
        s_srow_ps = signal("score_ps", 1)
        s_srow = signal("score_row", 1)
        s_rankop = signal("rank_ops", 15)
        s_rank_ps = signal("rank_ps", 1)
        s_selT_ps = signal("selT_ps", 1, first=1)
        s_selT = signal("selT", 2)
        s_v_ps = signal("value_ps", 5)
        s_v = signal("value", 5)
        s_kr_ps = signal("krope_ps", 1)
        s_task_ps = signal("task_ps", 16)
        s_mul = signal("rope_products", 1 + GROUPS * 3)
        s_rot = signal("rope_done", 2 + GROUPS * 3, first=1)
        s_copy = signal("nope_copied", GROUPS * 3)
        s_group = [signal("even_group", 2 * GDMA, first=1), signal("odd_group", 2 * GDMA, first=1)]
        s_s = signal("scores", HEADS)
        s_max = signal("score_max", HEADS * 3)
        s_exp = signal("exp", HEADS * 6)
        s_coef = signal("coefficient", 2 * HEADS)
        s_pn = signal("probs_scaled", HEADS * 6)
        s_pt_ps = signal("probsT_ps", HEADS)
        s_pta = signal("probsT_a", HEADS)
        s_ptb = signal("probsT_b", HEADS)
        s_o_ps = signal("heads_ps", GROUPS)
        s_o = signal("heads_out", GROUPS)
        s_proj = signal("proj_ps", 1)
        s_x1 = signal("x1", 1, first=1)
        s_out = signal("stored", 16, first=1)

        ahead = {
            4: ([], ["stats"]),
            6: ([], ["norm"]),
            8: (["xnT"], ["lat"]),
            9: (["srow"], ["ms"]),
            10: (["gate"], ["nlat", "scol"]),
            11: (["nT"], ["ties"]),
            12: (["larger"], []),
            13: (["krope"], ["rank"]),
            14: ([(0, 0)], ["selT"]),
            15: ([(0, 1)], [(0, 2)]),
            16: ([(0, 3)], [(1, 0)]),
            17: ([(1, 1)], [(1, 2), "gate_done"]),
            18: ([(1, 3)], []),
        }
        SLOTS = HEADS + LAG + 1

        def values_due(h):
            return (h - LAG) // GROUP - 1 if h > LAG and (h - LAG) % GROUP == 0 else None

        def steps(b, h, behind, nxt):
            out = []
            if not behind and h < 2 * GROUP:
                out.append((b, (2 + h // 4, h % 4)))
            if behind:
                out += [(b, "value%d" % k) for k in {0: [0], 1: [1], 2: [2, 3], 4: [4]}.get(h, [])]
            if nxt and h in ahead:
                out += [(b + 1, s) for s in ahead[h][behind]]
            return out

        first_row = [s for h in sorted(ahead) for s in ahead[h][0] + ahead[h][1]]

        def bank_read(eng, b, step):
            if step == "xnT":
                s_xnT.wait(eng, b, 2)
            elif step == "lat":
                s_lat.wait(eng, b, 1)
            elif step == "srow":
                s_srow.wait(eng, b, 1)
            elif step == "gate":
                s_gexp.wait(eng, b, 1)
            elif step == "nT":
                s_nT.wait(eng, b, 2)
            elif step == "krope":
                s_mul.wait(eng, b, 1)
            elif step == "rank":
                s_rankop.wait(eng, b, 13)
            elif step == "selT":
                s_selT.wait(eng, b, 2)
            elif isinstance(step, str):
                s_v.wait(eng, b, int(step[5:]) + 1)
            else:
                g, n = step
                if n in (0, 2, 3):
                    s_mul.wait(eng, b, 1 + 3 * g + {0: 1, 2: 2, 3: 3}[n])
                if n in (1, 3):
                    s_copy.wait(eng, b, 3 * g + {1: 1, 3: 3}[n])

        block = ctx.enter_context(nc.Block())

        def head_scores(h):
            return flat[:, (h % 2) * 1024:(h % 2) * 1024 + 1024]

        OTHER_BANKS = {(1, 0): 0, (1, 1): 1, (1, 3): 0, "value0": 4, "value1": 5, "value2": 4,
                       "value3": 5}

        def in_halves(bank):
            return bank.rearrange("p (a t) -> p a t", a=2)

        def step_bank(step):
            return ps[:, OTHER_BANKS.get(step, 7), :]

        halves = in_halves(bM)

        def cut(upper_lower, *index):
            return [t[index] for t in upper_lower]

        @block.sync
        def _(sp):
            prime(sp, *s_group, s_out)
            for name, _, room in to_halve:
                src = io[name]
                sp.dma_start(room, src if len(src.shape) == 2 else src.rearrange("p a b -> p (a b)"))\
                    .then_inc(s_raw.sem, 16)
            for tile, name in loads:
                src = io[name]
                dims = len(tile.shape)
                dst = tile[:, :] if dims == 2 else tile[:, :, :] if dims == 3 else tile[:, :, :, :]
                sp.dma_start(dst, src).then_inc(s_w.sem, 16)

            def load(b, tile, sig):
                sp.dma_start(tile[:, :, :], io["x"][bass.ds(b, 1)].rearrange(
                    "o (i p) c -> p (o i) c", p=P)).then_inc(sig.sem, 16)

            def group(b, g):
                s_rot.wait(sp, b, 2 + 3 * (g + 1))
                for j in range(GROUP):
                    for part in range(PARTS):
                        sp.dma_start(QK[PART * part:PART * (part + 1), g, j, :],
                                     st[PART * j:PART * (j + 1), g % 2, part, :])\
                            .then_inc(s_group[g % 2].sem, 16)

            def row(b, nxt):
                if nxt:
                    s_xn.wait(sp, b + 1, 0)
                    load(b + 1, xin, s_x)
                s_x1.wait(sp, b, 0)
                load(b, xres, s_xres)
                for g in (2, 3):
                    group(b, g)
                if nxt:
                    for g in (0, 1):
                        group(b + 1, g)
                s_x1.wait(sp, b, 1)
                sp.dma_start(x1_dram[bass.ds(b, 1)].rearrange("o p c -> p (o c)"),
                             x1[:, :, :].rearrange("p a b -> p (a b)")).then_inc(s_out.sem, 16)

            load(0, xin, s_x)
            for g in (0, 1):
                group(0, g)
            with sp.Fori(0, B - 1) as b:
                row(b, True)
            row(B - 1, False)
            s_out.wait_all(sp, B)

        @block.tensor
        def _(pe):
            prime(pe, s_selT_ps)
            pe.wait_ge(s_w.sem, 16 * len(loads))
            pe.wait_ge(s_init.sem, 4)

            def product(out, left, right, start=True, stop=True):
                pe.matmul(out, left[0], right[0], start=start, stop=False)
                pe.matmul(out, left[0], right[1], start=False, stop=False)
                return pe.matmul(out, left[1], right[0], start=False, stop=stop)

            def normed_transposes(b):
                s_xn.wait(pe, b, 2)
                for i in range(TT):
                    for c in range(CT):
                        m = pe.transpose(halves[:, c, i * P:(i + 1) * P], xn[:, i, c * P:(c + 1) * P], ident[:, :])
                m.then_inc(s_xnT_ps.sem, 1)

            def latents(b):
                for i in range(TT):
                    for c in range(CT):
                        m = pe.matmul(bM[:, i * T:i * T + LC], xnT[:, c, i * P:(i + 1) * P], w_lat[:, c, :],
                                      start=(c == 0), stop=(c == CT - 1))
                m.then_inc(s_lat_ps.sem, 1)

            def importance(b):
                for c in range(CT):
                    m = pe.matmul(bM[:, 0:T], w_imp[:, c, :], xnT[:, c, :], start=(c == 0), stop=(c == CT - 1))
                m.then_inc(s_srow_ps.sem, 1)

            def gate_logits(b):
                for i in range(TT):
                    m = pe.matmul(bM[:, 0:3], meanw[:, :], lat[:, i, QL + KVL:LC], start=(i == 0),
                                  stop=(i == TT - 1))
                m.then_inc(s_gate_ps.sem, 1)

            def latent_transposes(b):
                s_nlat.wait(pe, b, 4)
                for i in range(TT):
                    m = pe.transpose(bM[:, i * P:(i + 1) * P], nlat[:, i, :], ident[:, :])
                m.then_inc(s_nT_ps.sem, 1)

            def shared_key(b):
                s_low.wait(pe, b, 1)
                for part in range(2):
                    for c in range(CT):
                        m = product(halves[:, part, :], cut(w_kr, ALL, c, slice(part * P, (part + 1) * P)),
                                    cut(xnT2, ALL, c, ALL), start=(c == 0), stop=(c == CT - 1))
                m.then_inc(s_kr_ps.sem, 1)

            def ranks(b):
                s_rankop.wait(pe, b, 12)
                pe.matmul(bM[:, 0:1], uptri[:, 0:P], chosen[:, 0:1], start=True, stop=True)
                pe.matmul(bM[:, 1:2], uptri[:, P:2 * P], chosen[:, 0:1], start=True, stop=False)
                pe.matmul(bM[:, 1:2], uptri[:, 0:P], chosen[:, 1:2], start=False, stop=True)\
                    .then_inc(s_rank_ps.sem, 1)

            def selected(b):
                s_rankop.wait(pe, b, 15)
                for c in range(CT):
                    for i in range(TT):
                        m = pe.matmul(bM[:, c * KEEP:(c + 1) * KEEP], xn[:, i, c * P:(c + 1) * P],
                                      pick[:, i, :], start=(i == 0), stop=(i == TT - 1))
                m.then_inc(s_selT_ps.sem, 1)

            def head_values(b, k):
                tile = slice((k % 2) * P, (k % 2 + 1) * P)
                bank = step_bank("value%d" % k)
                if k < 2:
                    for c in range(CT):
                        m = product(bank, cut(xnT2, ALL, c, tile), cut(w_winv, ALL, c, ALL), start=(c == 0),
                                    stop=(c == CT - 1))
                elif k < 4:
                    m = product(bank, cut(nT2, ALL, tile), cut(w_v1, ALL, ALL))
                else:
                    for c in range(CT):
                        m = product(bank[0:KEEP, :], cut(selT2, ALL, c, ALL), cut(w_selv, ALL, c, ALL),
                                    start=(c == 0), stop=(c == CT - 1))
                m.then_inc(s_v_ps.sem, 1)

            def task(b, g, n):
                bank = step_bank((g, n))
                halves = in_halves(bank)
                col = lambda part: slice((g * PARTS + part) * P, (g * PARTS + part + 1) * P)
                if n == 0:
                    for part in (1, 2):
                        for c in range(CT):
                            m = product(halves[:, part - 1, :], cut(w_win, ALL, c, col(part)),
                                        cut(xnT2, ALL, c, ALL), start=(c == 0), stop=(c == CT - 1))
                elif n == 1:
                    s_low.wait(pe, b, 2)
                    product(halves[:, 0, :], cut(w_kn, ALL, slice(g * P, (g + 1) * P)), cut(nT2, ALL, ALL))
                    for c in range(CT):
                        m = product(halves[:, 1, :], cut(w_win, ALL, c, col(0)), cut(xnT2, ALL, c, ALL),
                                    start=(c == 0), stop=(c == CT - 1))
                elif n == 2:
                    for part in (1, 2):
                        m = product(halves[:, part - 1, :], cut(w_q, ALL, col(part)), cut(nT2, ALL, ALL))
                else:
                    product(halves[:, 0, :], cut(w_q, ALL, col(0)), cut(nT2, ALL, ALL))
                    s_low.wait(pe, b, 3)
                    for part in range(PARTS):
                        for c in range(CT):
                            m = product(bank[:, T + KEEP * part:T + KEEP * (part + 1)],
                                        cut(w_sel, ALL, c, col(part)), cut(selT2, ALL, c, ALL),
                                        start=(c == 0), stop=(c == CT - 1))
                m.then_inc(s_task_ps.sem, 1)

            makes = {"xnT": normed_transposes, "lat": latents, "srow": importance, "gate": gate_logits,
                     "nT": latent_transposes, "krope": shared_key, "rank": ranks, "selT": selected}

            def make(todo, before, heads=None):
                for b, step in todo:
                    if isinstance(step, str) and step not in makes and not step.startswith("value"):
                        continue
                    bank = OTHER_BANKS.get(step)
                    if bank in before:
                        bank_read(pe, *before[bank])
                    elif bank in (0, 1) and heads is not None:
                        s_exp.wait(pe, heads, 6 * (HEADS - 1))
                    if isinstance(step, tuple):
                        task(b, *step)
                    elif step in makes:
                        makes[step](b)
                    else:
                        head_values(b, int(step[5:]))
                    before[bank] = (b, step)

            def scores(b, h):
                g, j = h // GROUP, h % GROUP
                if j == 0:
                    s_group[g % 2].wait(pe, b, GDMA * (g // 2 + 1))
                if h == 0:
                    bank_read(pe, b, (1, 1))
                    bank_read(pe, b, (1, 3))
                if h >= 2:
                    s_exp.wait(pe, b, 6 * (h - 1))
                S = head_scores(h)
                qk = QK[:, g, j, :]
                q0, q1 = qk[:, QC:QC + P], qk[:, QC + P:QC + T]
                pe.matmul(S[:, 64:512], q1, qk[:, WC0:WC0 + 448], start=True, stop=False, skip_group_check=True)
                pe.matmul(S[:, 192:320], identb[:, :], maskb[:, 0:P], start=False, stop=True,
                          skip_group_check=True)
                pe.matmul(S[:, 512:640], q1, qk[:, WC0 + 448:HCOLS], start=True, stop=False,
                          skip_group_check=True)
                pe.matmul(S[:, 512:640], identb[:, :], maskb[:, 0:P], start=False, stop=False,
                          skip_group_check=True)
                pe.matmul(S[:, S0:S0 + P], q0, qk[:, WC0:WC0 + P], start=False, stop=False,
                          skip_group_check=True)
                pe.matmul(S[:, S0 + P:S0 + 2 * P + KEEP], q0, qk[:, SC0:SC0 + KEEP + P],
                          start=False, stop=False, skip_group_check=True)
                pe.matmul(S[:, S0:S0 + P], identb[:, :], maskb[:, 0:P], start=False, stop=False,
                          skip_group_check=True)
                m = pe.matmul(S[:, S0 + P + KEEP:S0 + 2 * P + KEEP], identb[:, :], maskb[:, 0:P], start=False,
                              stop=True, skip_group_check=True)
                m.then_inc(s_s.sem, 1)

            def transposes(b, h):
                s_pn.wait(pe, b, 6 * (h + 1))
                if h:
                    s_pta.wait(pe, b, h)
                    s_ptb.wait(pe, b, h)
                else:
                    s_v.wait(pe, b, 4)
                p = Pr[:, h % PBUF, :]
                w1, b1, e1 = SEG[1, WIN][0], SEG[1, BASE][0], SEG[1, SEL][0]
                w0, b0, e0 = SEG[0, WIN][0], SEG[0, BASE][0], SEG[0, SEL][0]
                for to, at in ((b4[:, 0:P], w0), (b4[:, P:2 * P], w1), (b4[:, 2 * P:3 * P], b0),
                               (b4[:, 3 * P:4 * P], b1), (b5[:, 0:P], w1 + P), (b5[:, P:2 * P], b1 + P)):
                    pe.transpose(to, p[:, at:at + P], ident[:, :])
                pe.transpose(b5[0:KEEP, 2 * P:3 * P], p[:, e0:e0 + KEEP], ident[:, :])
                pe.transpose(b5[0:KEEP, 3 * P:4 * P], p[:, e1:e1 + KEEP], ident[:, :]).then_inc(s_pt_ps.sem, 1)

            def values(b, g):
                s_pta.wait(pe, b, GROUP * (g + 1))
                s_ptb.wait(pe, b, GROUP * (g + 1))
                if g:
                    s_o.wait(pe, b, g)
                else:
                    s_v.wait(pe, b, 5)
                    s_x1.wait(pe, b, 0)
                for n, (tile, at, width, to) in enumerate((
                        (0, 0, T, 0), (2, T, T, 0), (4, 3 * T, T, 0), (1, 2 * T, P, P), (3, 2 * T + P, P, P))):
                    for j in range(GROUP):
                        h = g * GROUP + j
                        m = pe.matmul(bO[VD * j:VD * (j + 1), to:to + width], V[:, tile, VD * h:VD * (h + 1)],
                                      PT[:, j, at:at + width], start=(n == 0), stop=(n == 4),
                                      skip_group_check=True)
                m.then_inc(s_o_ps.sem, 1)

            def projection(b):
                s_o.wait(pe, b, GROUPS)
                for i in range(TT):
                    for g in range(GROUPS):
                        m = pe.matmul(bO[:, i * C:(i + 1) * C], OT[:, g, i * P:(i + 1) * P], w_proj[:, g, :],
                                      start=(g == 0), stop=(g == GROUPS - 1))
                m.then_inc(s_proj.sem, 1)

            def row(b, nxt):
                before = {None: (b, (1, 2))}
                for h in range(SLOTS):
                    make(steps(b, h, 0, nxt), before, b)
                    if h < HEADS:
                        scores(b, h)
                    make(steps(b, h, 1, nxt), before, b)
                    if values_due(h) is not None:
                        values(b, values_due(h))
                    if LAG <= h < HEADS + LAG:
                        transposes(b, h - LAG)
                projection(b)

            make([(0, s) for s in first_row], {})
            with pe.Fori(0, B - 1) as b:
                row(b, True)
            row(B - 1, False)

        @block.scalar
        def _(act):
            act.wait_ge(s_w.sem, 16 * len(loads))
            act.wait_ge(s_init.sem, 4)
            act.wait_ge(s_raw.sem, 16 * len(to_halve))
            for _, tile, room in to_halve:
                act.activation(tile[0], room, ACT.Copy, scale=WSCALE).then_inc(s_upper.sem, 1)
            act.wait_ge(s_lower.sem, len(to_halve) + 1)

            def copy(out, src, sig, scale=1.0):
                act.activation(out, src, ACT.Copy, scale=scale).then_inc(sig.sem, 1)

            def nope_copies(b, g, n):
                s_task_ps.wait(act, b, 4 * g + n + 1)
                gg = g % 2
                bank = step_bank((g, n))
                halves = in_halves(bank)
                if n == 1:
                    s_group[gg].wait(act, b, GDMA * (g // 2))
                    act.activation(st[:, gg, 0, BC0:BC0 + T], halves[:, 0, :], ACT.Copy, scale=1.0 / WSCALE)
                    copy(st[:, gg, 0, WC0:WC0 + T], halves[:, 1, :], s_copy, scale=1.0 / WSCALE)
                if n == 3:
                    copy(st[:, gg, 0, QC:QC + T], halves[:, 0, :], s_copy, scale=DK ** -0.5 / WSCALE)
                    copy(st[:, gg, 0, SC0:SC0 + KEEP], bank[:, T:T + KEEP], s_copy, scale=1.0 / WSCALE)

            def take(todo):
                for b, step in todo:
                    if step == "xnT":
                        s_xnT_ps.wait(act, b, 1)
                        copy(xnT[:, :, :].rearrange("p a b -> p (a b)"), bM, s_xnT)
                        copy(xnT2[0][:, :, :].rearrange("p a b -> p (a b)"), bM, s_xnT)
                    elif step == "lat":
                        s_lat_ps.wait(act, b, 1)
                        copy(lat[:, :, :], halves[:, :, 0:LC], s_lat)
                    elif step == "nT":
                        s_nT_ps.wait(act, b, 1)
                        for out in (nT, nT2[0]):
                            copy(out[:, :], bM[:, 0:T], s_nT, scale=g_lat[:, 0:1])
                    elif step == "gate":
                        s_gate.wait(act, b, 1)
                        act.activation(gexp[:, :], bM[:, 0:3], ACT.Exp, bias=gmax[:, 0:1],
                                       accum_out=gsum[:, 0:1]).then_inc(s_gexp.sem, 1)
                    elif step == "selT":
                        s_selT_ps.wait(act, b, 1)
                        for out in (selT, selT2[0]):
                            copy(out[:, :, :].rearrange("p a b -> p (a b)"), bM[:, 0:CT * KEEP], s_selT)
                    elif step in ("value0", "value1", "value2", "value3", "value4"):
                        k = int(step[5:])
                        s_v_ps.wait(act, b, k + 1)
                        rows = KEEP if k == 4 else P
                        copy(V[0:rows, k, :], step_bank(step)[0:rows, :], s_v, scale=1.0 / WSCALE)
                    elif isinstance(step, tuple) and step[1] in (1, 3):
                        nope_copies(b, *step)

            def exps(b, h):
                S = head_scores(h)[:, 64:64 + PCOLS]
                s_max.wait(act, b, 3 * (h + 1))
                if h >= PBUF:
                    s_pt_ps.wait(act, b, h - PBUF + 1)
                if h >= 2:
                    s_coef.wait(act, b, 2 * (h - 1))
                for i in (1, 0):
                    for a in (WIN, BASE, SEL):
                        at, width = SEG[i, a]
                        c = 3 * (1 - i) + a
                        act.activation(Pr[:, h % PBUF, at:at + width], S[:, at:at + width], ACT.Exp,
                                       bias=nmax[:, h % 2, c:c + 1], accum_out=rsum[:, h % 2, c:c + 1])\
                            .then_inc(s_exp.sem, 1)

            def evacuate(b, h):
                s_pt_ps.wait(act, b, h + 1)
                act.activation(PT[:, h % GROUP, 2 * T:3 * T], b5[:, 0:T], ACT.Copy)
                copy(PT[0:KEEP, h % GROUP, 3 * T:4 * T], b5[0:KEEP, T:2 * T], s_ptb)

            def row(b, nxt):
                for h in range(SLOTS):
                    take(steps(b, h, 0, nxt))
                    take(steps(b, h, 1, nxt))
                    if h < HEADS:
                        exps(b, h)
                    if values_due(h) is not None:
                        s_o_ps.wait(act, b, values_due(h) + 1)
                        copy(OT[:, values_due(h), :], bO[:, 0:T], s_o)
                    if LAG <= h < HEADS + LAG:
                        evacuate(b, h - LAG)

            take([(0, s) for s in first_row])
            with act.Fori(0, B - 1) as b:
                row(b, True)
            row(B - 1, False)

        @block.gpsimd
        def _(pool):
            prime(pool, s_rot)
            pool.memset(minus_half[:, :], -0.5).then_inc(s_init.sem, 1)
            pool.memset(V[:, 4, :], 0.0).then_inc(s_init.sem, 1)
            pool.memset(hmax[:, :], 0.0).then_inc(s_init.sem, 1)
            pool.memset(rot1[:, :, :, :], 0.0).then_inc(s_init.sem, 1)
            pool.wait_ge(s_w.sem, 16 * len(loads))
            pool.wait_ge(s_init.sem, 4)

            def inverse_root(b, k, out, src, n, ready, done):
                ready.wait(pool, b, k)
                pool.tensor_tensor(out, src, minus_half[:, 0:n], ALU.pow).then_inc(done.sem, 1)

            def rotate(b, k, out, width):
                s_mul.wait(pool, b, k + 1)
                pool.tensor_tensor(out, rot1[:, k % 2, :, 0:width], rot2[:, k % 2, :, 0:width], ALU.add)\
                    .then_inc(s_rot.sem, 1)

            def take(todo):
                for b, step in todo:
                    if step == "stats":
                        inverse_root(b, 5, rstd[:, :], vareps[:, :], TT, s_ln, s_rstd)
                    elif step == "ms":
                        inverse_root(b, 4, rlat[:, :, :].rearrange("p a b -> p (a b)"),
                                     ms[:, :, :].rearrange("p a b -> p (a b)"), 4, s_ms, s_rlat)
                    elif step == "krope":
                        for gg in range(2):
                            s_group[gg].wait(pool, b, 0)
                            rotate(b, 0, st[:, gg, 1:3, BC0:BC0 + T], T)
                    elif isinstance(step, tuple) and step[1] != 1:
                        g, n = step
                        gg = g % 2
                        if n == 0 and g >= 2:
                            s_group[gg].wait(pool, b, GDMA * (g // 2))
                        at, width = {0: (WC0, T), 2: (QC, T), 3: (SC0, KEEP)}[n]
                        rotate(b, {0: 1, 2: 2, 3: 3}[n] + 3 * g, st[:, gg, 1:3, at:at + width], width)

            def scale(b, h):
                s_coef.wait(pool, b, 2 * (h + 1))
                pool.tensor_tensor(held[:, 1 + h % 2:2 + h % 2], minus_half[:, 0:1], minus_half[:, 1:2], ALU.add)
                for i in (1, 0):
                    for a in (WIN, BASE, SEL):
                        at, width = SEG[i, a]
                        c = 3 * (1 - i) + a
                        p = Pr[:, h % PBUF, at:at + width]
                        pool.tensor_scalar(p, p, coef[:, h % 2, c:c + 1], 1.0, ALU.mult, ALU.mult)\
                            .then_inc(s_pn.sem, 1)

            def row(b, nxt):
                for h in range(SLOTS):
                    take(steps(b, h, 0, nxt))
                    if 1 <= h <= HEADS:
                        scale(b, h - 1)
                    take(steps(b, h, 1, nxt))

            take([(0, s) for s in first_row])
            with pool.Fori(0, B - 1) as b:
                row(b, True)
            row(B - 1, False)

        @block.vector
        def _(dve):
            prime(dve, s_x1, s_xn)
            dve.wait_ge(s_w.sem, 16 * len(loads))
            dve.wait_ge(s_init.sem, 4)
            for n, (_, tile, room) in enumerate(to_halve):
                dve.wait_ge(s_upper.sem, n + 1)
                dve.scalar_tensor_tensor(tile[1], room, WSCALE, tile[0], ALU.mult, ALU.subtract)\
                    .then_inc(s_lower.sem, 1)
            dve.wait_ge(s_lower.sem, len(to_halve))
            dve.memset(PT[:, :, :], 0.0).then_inc(s_lower.sem, 1)
            latent_parts = [(i, n, a, z) for i in range(TT) for n, (a, z) in
                            enumerate(((0, QL), (QL, QL + KVL)))]

            def statistics(b):
                s_x.wait(dve, b, 16)
                for i in range(TT):
                    dve.bn_stats(stats[:, i, :], xin[:, i, :]).then_inc(s_ln.sem, 1)
                s_ln.wait(dve, b, 2)
                dve.tensor_copy(held[:, 0:1], stats[:, 0, 0:1])
                for i in range(TT):
                    dve.bn_aggr(meanvar[:, i, :], stats[:, i, :]).then_inc(s_ln.sem, 1)
                s_ln.wait(dve, b, 4)
                dve.tensor_scalar(vareps[:, :], meanvar[:, :, 1], LN_EPS, None, ALU.add).then_inc(s_ln.sem, 1)

            def norm(b):
                s_rstd.wait(dve, b, 1)
                s_selT_ps.wait(dve, b, 0)
                for i in range(TT):
                    dve.tensor_scalar(xn[:, i, :], xin[:, i, :], meanvar[:, i, 0:1], rstd[:, i:i + 1],
                                      ALU.subtract, ALU.mult).then_inc(s_xn.sem, 1)

            def mean_squares(b):
                s_lat.wait(dve, b, 1)
                s_rot.wait(dve, b, 0)
                for k, (i, n, a, z) in enumerate(latent_parts):
                    if k:
                        s_ms.wait(dve, b, k)
                    dve.tensor_tensor_reduce(sq[:, 0, 0:z - a], lat[:, i, a:z], lat[:, i, a:z],
                                             1.0 / (z - a), RMS_EPS, ALU.mult, ALU.add,
                                             ms[:, i, n:n + 1]).then_inc(s_ms.sem, 1)

            def normed_latents(b):
                s_rlat.wait(dve, b, 1)
                for i, n, a, z in latent_parts:
                    dve.tensor_scalar(nlat[:, i, a:z], lat[:, i, a:z], rlat[:, i, n:n + 1], None,
                                      ALU.mult).then_inc(s_nlat.sem, 1)

            def own_importance(b):
                s_srow.wait(dve, b, 1)
                for i in range(TT):
                    dve.tensor_tensor_reduce(junk[:, i, 0:P], srow[:, i * P:(i + 1) * P], ident[:, :], 1.0,
                                             0.0, ALU.mult, ALU.add, scol[:, i:i + 1]).then_inc(s_rankop.sem, 1)

            def ties(b):
                s_rankop.wait(dve, b, 2)
                for i in range(TT):
                    dve.tensor_scalar(junk[:, i, :], srow[:, :], scol[:, i:i + 1], None, ALU.is_equal)\
                        .then_inc(s_rankop.sem, 1)
                for i in range(TT):
                    s_rankop.wait(dve, b, 3 + i)
                    dve.tensor_tensor_reduce(junk[:, i, :], junk[:, i, :], before[:, i, :], 1.0, 0.0,
                                             ALU.mult, ALU.add, tie[:, i:i + 1]).then_inc(s_rankop.sem, 1)

            def larger(b):
                for i in range(TT):
                    s_rankop.wait(dve, b, 5 + i)
                    dve.tensor_scalar(junk[:, i, :], srow[:, :], scol[:, i:i + 1], None, ALU.is_gt)\
                        .then_inc(s_rankop.sem, 1)
                for i in range(TT):
                    s_rankop.wait(dve, b, 7 + i)
                    dve.tensor_reduce(cnt[:, i:i + 1], junk[:, i, :], AX.X, ALU.add)\
                        .then_inc(s_rankop.sem, 1)
                for i in range(TT):
                    s_rankop.wait(dve, b, 9 + i)
                    dve.tensor_scalar(chosen[:, i:i + 1], cnt[:, i:i + 1], tie[:, i:i + 1], KEEP - 0.5,
                                      ALU.add, ALU.is_lt).then_inc(s_rankop.sem, 1)

            def pick_columns(b):
                s_rank_ps.wait(dve, b, 1)
                dve.tensor_copy(rank[:, :], bM[:, 0:2]).then_inc(s_rankop.sem, 1)
                s_rankop.wait(dve, b, 13)
                for i in range(TT):
                    dve.tensor_scalar(pick[:, i, :], iota64[:, :], rank[:, i:i + 1], chosen[:, i:i + 1],
                                      ALU.is_equal, ALU.mult).then_inc(s_rankop.sem, 1)

            def lower(b, ready, whole, upper_lower):
                ready.wait(dve, b, 2)
                dve.tensor_tensor(upper_lower[1], whole, upper_lower[0], ALU.subtract).then_inc(s_low.sem, 1)

            def products(b, k, src, table, width, scale=None):
                s_rot.wait(dve, b, k if k > 1 else 0)
                cos = table[:, 0:1, 0:width].to_broadcast([P, 2, width])
                sin = table[:, 1, 0:width]
                one = (1.0 if scale is None else scale) / WSCALE
                dve.scalar_tensor_tensor(rot1[:, k % 2, :, 0:width], src, one, cos, ALU.mult, ALU.mult)
                dve.scalar_tensor_tensor(rot2[:, k % 2, 0, 0:width], src[:, 1, :], -one, sin, ALU.mult, ALU.mult)
                dve.scalar_tensor_tensor(rot2[:, k % 2, 1, 0:width], src[:, 0, :], one, sin, ALU.mult, ALU.mult)\
                    .then_inc(s_mul.sem, 1)

            def group_products(b, g, n):
                s_task_ps.wait(dve, b, 4 * g + n + 1)
                bank = step_bank((g, n))
                halves = in_halves(bank)
                if n == 0:
                    products(b, 1 + 3 * g, halves, rope_k, T)
                if n == 2:
                    products(b, 2 + 3 * g, halves, rope_q, T)
                if n == 3:
                    s_copy.wait(dve, b, 3 * (g + 1))
                    products(b, 3 + 3 * g, bank[:, T + KEEP:T + 3 * KEEP].rearrange("p (a t) -> p a t", a=2),
                             rope_k, KEEP)

            takes = {"stats": statistics, "norm": norm, "ms": mean_squares, "nlat": normed_latents,
                     "scol": own_importance, "ties": ties, "larger": larger, "rank": pick_columns}

            def take(todo):
                for b, step in todo:
                    if step in takes:
                        takes[step](b)
                    elif step == "xnT":
                        lower(b, s_xnT, xnT[:, :, :], cut(xnT2, ALL, ALL, ALL))
                    elif step == "nT":
                        lower(b, s_nT, nT[:, :], cut(nT2, ALL, ALL))
                    elif step == "selT":
                        lower(b, s_selT, selT[:, :, :], cut(selT2, ALL, ALL, ALL))
                    elif step == "srow":
                        s_srow_ps.wait(dve, b, 1)
                        dve.tensor_copy(srow[:, :], bM[:, 0:T]).then_inc(s_srow.sem, 1)
                    elif step == "gate":
                        s_gate_ps.wait(dve, b, 1)
                        dve.tensor_reduce(gmax[:, :], bM[:, 0:3], AX.X, ALU.max, negate=True)\
                            .then_inc(s_gate.sem, 1)
                    elif step == "gate_done":
                        s_gexp.wait(dve, b, 1)
                        dve.reciprocal(ginv[:, :], gsum[:, :]).then_inc(s_gate.sem, 1)
                        s_gate.wait(dve, b, 2)
                        dve.tensor_scalar(gate[:, :], gexp[:, :], ginv[:, 0:1], None, ALU.mult)\
                            .then_inc(s_gate.sem, 1)
                    elif step == "krope":
                        s_kr_ps.wait(dve, b, 1)
                        products(b, 0, halves, rope_k, T, scale=1.0 / HEADS)
                    elif isinstance(step, tuple) and step[1] != 1:
                        group_products(b, *step)

            def maxima(b, h):
                S = head_scores(h)
                s_s.wait(dve, b, h + 1)
                if h >= 2:
                    s_exp.wait(dve, b, 6 * (h - 1))
                m = nmax[:, h % 2, :]
                both = lambda at, n, apart: S[:, at:at + 2 * apart].rearrange("p (a k) -> p a k", k=apart)[:, :, 0:n]
                dve.tensor_reduce(m[:, 0:2], both(S1, T, T + KEEP), AX.X, ALU.max, negate=True)\
                    .then_inc(s_max.sem, 1)
                dve.tensor_reduce(m[:, 3:5], both(S0, P, P + KEEP), AX.X, ALU.max, negate=True)\
                    .then_inc(s_max.sem, 1)
                sel = S[:, S1 + T:S0 + P + KEEP].rearrange("p (a k) -> p a k", k=KEEP)
                dve.tensor_reduce(m[:, 2:6:3], sel[:, 0:8:7, :], AX.X, ALU.max, negate=True)\
                    .then_inc(s_max.sem, 1)

            def coefficients(b, h):
                s_exp.wait(dve, b, 6 * (h + 1))
                if h >= 2:
                    s_pn.wait(dve, b, 6 * (h - 1))
                if h == 0:
                    s_gate.wait(dve, b, 3)
                dve.reciprocal(rinv[:, h % 2, :], rsum[:, h % 2, :]).then_inc(s_coef.sem, 1)
                s_coef.wait(dve, b, 2 * h + 1)
                dve.tensor_tensor(coef[:, h % 2, :].rearrange("p (a k) -> p a k", a=2),
                                  rinv[:, h % 2, :].rearrange("p (a k) -> p a k", a=2),
                                  gate[:, :].unsqueeze(1).to_broadcast([P, 2, 3]), ALU.mult)\
                    .then_inc(s_coef.sem, 1)

            def evacuate(b, h):
                s_pt_ps.wait(dve, b, h + 1)
                dve.tensor_copy(PT[:, h % GROUP, 0:2 * T], b4).then_inc(s_pta.sem, 1)

            def row(b, nxt):
                for h in range(SLOTS):
                    take(steps(b, h, 0, nxt))
                    if h < HEADS:
                        maxima(b, h)
                    if 1 <= h <= HEADS:
                        coefficients(b, h - 1)
                    take(steps(b, h, 1, nxt))
                    if LAG <= h < HEADS + LAG:
                        evacuate(b, h - LAG)
                s_proj.wait(dve, b, 1)
                s_xres.wait(dve, b, 16)
                s_out.wait(dve, b, 0)
                dve.tensor_tensor(x1[:, :, :].rearrange("p a b -> p (a b)"), bO,
                                  xres[:, :, :].rearrange("p a b -> p (a b)"), ALU.add).then_inc(s_x1.sem, 1)

            take([(0, s) for s in first_row])
            with dve.Fori(0, B - 1) as b:
                row(b, True)
            row(B - 1, False)


def cross_attention(nc, io, x1_dram, h_dram, x2_dram, ident, hmax):
    with ExitStack() as ctx:
        def sb(name, shape, dt=F32):
            return ctx.enter_context(nc.sbuf_tensor(name, shape, dt))

        def two(name, shape):
            return [sb(name + "_%d" % r, shape) for r in range(2)]

        def signals(name, per=1, first=0):
            return [Signal(ctx.enter_context(nc.semaphore("s_%s_%d" % (name, r))), per, first)
                    for r in range(2)]

        def prime(eng, *pairs):
            for pair in pairs:
                for s in pair:
                    eng.sem_inc(s.sem, s.first)

        w_x = sb("w_x", [P, 4, CT, C])
        own16 = sb("own16", [P, XH])
        xb = sb("xb", [P, 2, CT])
        xrow = sb("xrow", [P, 2, C])
        minus_half = sb("minus_half2", [P, TT])
        x1 = two("x1", [P, TT, C])
        x1b = two("x1b", [P, TT, C])
        ctxT = two("ctxT", [P, CT, CTX])
        stats = two("stats2", [P, 2, TT, 6])
        meanvar = two("meanvar2", [P, 2, TT, 2])
        vareps = two("vareps2", [P, 2, TT])
        rstd = two("rstd2", [P, 2, TT])
        held = two("held2", [P, 1])
        xn = two("xn2", [P, 2, TT, C])
        xnT = two("xnT2", [P, CT, T])
        kT2 = two("kT2", [P, CT, CTX])
        Kbd = two("Kbd", [P, CT, XH, CTX])
        Vz = two("Vz", [CTX, HEADS // 2, 2, 2, XD])
        q2 = two("q2", [P, CT, T])
        nmax2 = two("nmax2", [P, HEADS])
        P2 = two("P2", [P, TT, HEADS, CTX])
        rs2 = two("rs2", [P, TT, HEADS])
        ri2 = two("ri2", [P, TT, HEADS])
        PT2 = two("PT2", [P, HEADS, T])
        O2T = two("O2T", [P, CT, T])
        x2 = two("x2", [P, TT, C])
        hT = two("hT", [P, CT, T])
        hm = two("hm", [P, 1])
        ps = ctx.enter_context(nc.psum_tensor("ps_x", [P, 8, 512], F32))
        bank = lambda r, n: ps[:, 4 * r + n, :]

        loads = [(w_x, "w_x"), (own16, "own16"), (xb, "xb"), (xrow, "xrow")]
        s_w = ctx.enter_context(nc.semaphore("s_x_weights"))
        s_init = ctx.enter_context(nc.semaphore("s_x_init"))
        s_in = signals("x1_loaded", 32)
        s_ln = [signals("x_ln_ops_1", 5), signals("x_ln_ops_2", 5)]
        s_rstd = [signals("x_rstd_1", 1), signals("x_rstd_2", 1)]
        s_xn = [signals("x_normed_1", 2), signals("x_normed_2", 2)]
        s_x1b = signals("x1_biased", 1, first=1)
        s_kv_ps = signals("xkv_ps", 2, first=1)
        s_kv = signals("xkv", 2)
        s_kbd = signals("xk_blocks", 1)
        s_xnT_ps = [signals("xT_ps_1", 1, first=1), signals("xT_ps_2", 1, first=1)]
        s_xnT = [signals("xT_1", 1), signals("xT_2", 1, first=1)]
        s_q2_ps = signals("xq_ps", 1)
        s_q2 = signals("xq", 1)
        s_s2 = signals("xscores", 2)
        s_sub2 = signals("xshifted", 4)
        s_e2 = signals("xexp", 2)
        s_r2 = signals("xsum", 4)
        s_n2 = signals("xprobs", 2)
        s_t2_ps = signals("xprobsT_ps", 8)
        s_t2 = signals("xprobsT", 8, first=1)
        s_o2_ps = signals("xheads_ps", 1)
        s_o2 = signals("xheads_out", 1, first=1)
        s_y2_ps = signals("xproj_ps", 1)
        s_x2 = signals("x2", 1, first=1)
        s_hm = signals("h_max", 1)
        s_hmax = Signal(ctx.enter_context(nc.semaphore("s_h_running_max")), 2, first=1)
        s_out = signals("x_stored", 32, first=1)

        PAIRS = B // 2
        STAGES = 10

        def rows(eng, early, first, second):
            def period(old, new, nxt):
                for k in range(STAGES):
                    for row, stages in ((old, second), (new, first), (nxt, early)):
                        if row:
                            for step in stages.get(k, []):
                                step(*row)

            period(None, None, (0, 0))
            period(None, (0, 0), (0, 1))
            with eng.Fori(0, PAIRS - 1) as b:
                period((b, 0), (b, 1), (b + 1, 0))
                period((b, 1), (b + 1, 0), (b + 1, 1))
            period((PAIRS - 1, 0), (PAIRS - 1, 1), None)
            period((PAIRS - 1, 1), None, None)

        def tile(step, i):
            return lambda b, r: step(b, r, i)

        block = ctx.enter_context(nc.Block())

        @block.sync
        def _(sp):
            prime(sp, s_out)
            for tile, name in loads:
                dims = len(tile.shape)
                dst = tile[:, :] if dims == 2 else tile[:, :, :] if dims == 3 else tile[:, :, :, :]
                sp.dma_start(dst, io[name]).then_inc(s_w, 16)

            def load(b, r):
                s_x1b[r].wait(sp, b, 0)
                sp.dma_start(x1[r][:, :, :].rearrange("p a b -> p (a b)"),
                             x1_dram[bass.ds(2 * b + r, 1)].rearrange("o p c -> p (o c)"))\
                    .then_inc(s_in[r].sem, 16)
                s_kv_ps[r].wait(sp, b, 0)
                sp.dma_start(ctxT[r][:, :, :], io["ctxT"][bass.ds(2 * b + r, 1)].rearrange(
                    "o (i p) c -> p (o i) c", p=P)).then_inc(s_in[r].sem, 16)

            def store(b, r):
                s_x2[r].wait(sp, b, 1)
                sp.dma_start(x2_dram[bass.ds(2 * b + r, 1)].rearrange("o p c -> p (o c)"),
                             x2[r][:, :, :].rearrange("p a b -> p (a b)")).then_inc(s_out[r].sem, 16)
                s_xnT[1][r].wait(sp, b, 1)
                sp.dma_start(h_dram[bass.ds(2 * b + r, 1)].rearrange("o p c -> p (o c)"),
                             hT[r][:, :, :].rearrange("p a b -> p (a b)")).then_inc(s_out[r].sem, 16)

            for r in range(2):
                load(0, r)
            with sp.Fori(0, PAIRS - 1) as b:
                for r in range(2):
                    load(b + 1, r)
                    store(b, r)
            for r in range(2):
                store(PAIRS - 1, r)
            for r in range(2):
                s_out[r].wait_all(sp, PAIRS)

        @block.tensor
        def _(pe):
            prime(pe, s_kv_ps, *s_xnT_ps)
            pe.wait_ge(s_w, 16 * len(loads))

            def context(b, r):
                s_in[r].wait(pe, b, 32)
                s_t2[r].wait(pe, b, 0)
                for f in range(CT):
                    for c in range(CT):
                        m = pe.matmul(bank(r, 0)[:, f * P:f * P + CTX], w_x[:, 1, c, f * P:(f + 1) * P],
                                      ctxT[r][:, c, :], start=(c == 0), stop=(c == CT - 1))
                m.then_inc(s_kv_ps[r].sem, 1)
                for c in range(CT):
                    m = pe.matmul(bank(r, 1)[0:CTX, 0:C], ctxT[r][:, c, :], w_x[:, 2, c, :],
                                  start=(c == 0), stop=(c == CT - 1))
                m.then_inc(s_kv_ps[r].sem, 1)

            def transposes(b, r, k):
                s_xn[k][r].wait(pe, b, 2)
                if k == 0:
                    s_o2[r].wait(pe, b, 0)
                for i in range(TT):
                    for c in range(CT):
                        m = pe.transpose(bank(r, 2)[:, c * T + i * P:c * T + (i + 1) * P],
                                         xn[r][:, k, i, c * P:(c + 1) * P], ident[:, :])
                m.then_inc(s_xnT_ps[k][r].sem, 1)

            def queries(b, r):
                s_xnT[0][r].wait(pe, b, 1)
                s_x2[r].wait(pe, b, 0)
                for f in range(CT):
                    for c in range(CT):
                        m = pe.matmul(bank(r, 3)[:, f * T:(f + 1) * T], w_x[:, 0, c, f * P:(f + 1) * P],
                                      xnT[r][:, c, :], start=(c == 0), stop=(c == CT - 1))
                m.then_inc(s_q2_ps[r].sem, 1)

            def scores(b, r, i):
                if i:
                    s_sub2[r].wait(pe, b, 2 * i)
                else:
                    s_q2[r].wait(pe, b, 1)
                    s_kbd[r].wait(pe, b, 1)
                    s_kv[r].wait(pe, b, 2)
                    s_xnT[1][r].wait(pe, b, 0)
                for f in range(CT):
                    for n in range(2):
                        m = pe.matmul(bank(r, 2 * f + n)[:, 0:4 * CTX], q2[r][:, f, i * P:(i + 1) * P],
                                      Kbd[r][:, f, 4 * n:4 * n + 4, :].rearrange("p a b -> p (a b)"),
                                      start=True, stop=True)
                m.then_inc(s_s2[r].sem, 1)

            def probs_transposes(b, r, i):
                s_n2[r].wait(pe, b, i + 1)
                s_sub2[r].wait(pe, b, 4)
                for n in range(4):
                    k = 4 * i + n
                    if k >= 2:
                        s_t2[r].wait(pe, b, k - 1)
                    for m4 in range(4):
                        m = pe.transpose(bank(r, n % 2)[0:CTX, m4 * P:(m4 + 1) * P],
                                         P2[r][:, i, 4 * n + m4, :], ident[:, :])
                    m.then_inc(s_t2_ps[r].sem, 1)

            def values(b, r):
                s_t2[r].wait(pe, b, 8)
                for w in range(2):
                    for pair in range(HEADS // 2):
                        j, f = pair % 4, pair // 4
                        m = pe.matmul(bank(r, 2)[32 * j:32 * (j + 1), f * T:(f + 1) * T],
                                      Vz[r][:, pair, w, :, :].rearrange("p a b -> p (a b)"),
                                      PT2[r][0:CTX, 2 * pair + w, :], start=(w == 0 and f == 0), stop=(w == 1),
                                      skip_group_check=True)
                m.then_inc(s_o2_ps[r].sem, 1)

            def output(b, r):
                s_o2[r].wait(pe, b, 1)
                for i in range(TT):
                    for f in range(CT):
                        m = pe.matmul(bank(r, 3)[:, i * C:(i + 1) * C], O2T[r][:, f, i * P:(i + 1) * P],
                                      w_x[:, 3, f, :], start=(f == 0), stop=(f == CT - 1))
                m.then_inc(s_y2_ps[r].sem, 1)

            rows(pe, {6: [context], 7: [tile(transposes, 0), queries]},
                 {0: [tile(scores, 0)], 4: [tile(scores, 1)]},
                 {3: [tile(probs_transposes, 0)], 5: [tile(probs_transposes, 1)], 6: [values], 7: [output],
                  8: [tile(transposes, 1)]})

        @block.scalar
        def _(act):
            prime(act, s_t2, s_o2, s_xnT[1])

            def copy(out, src, sig):
                act.activation(out, src, ACT.Copy).then_inc(sig.sem, 1)

            def normed(b, r, k):
                s_xnT_ps[k][r].wait(act, b, 1)
                if k:
                    s_out[r].wait(act, b, 0)
                copy((hT if k else xnT)[r][:, :, :].rearrange("p a b -> p (a b)"), bank(r, 2), s_xnT[k][r])

            def exps(b, r, i):
                s_sub2[r].wait(act, b, 2 * i + 2)
                p = P2[r][:, i, :, :].rearrange("p h k -> p (h k)")
                act.activation(p, p, ACT.Exp).then_inc(s_e2[r].sem, 1)

            def evacuate(b, r, i):
                for n in range(4):
                    s_t2_ps[r].wait(act, b, 4 * i + n + 1)
                    copy(PT2[r][0:CTX, 4 * n:4 * n + 4, i * P:(i + 1) * P],
                         bank(r, n % 2)[0:CTX, :].rearrange("p (h t) -> p h t", h=4), s_t2[r])

            def heads_out(b, r):
                s_o2_ps[r].wait(act, b, 1)
                copy(O2T[r][:, :, :].rearrange("p a b -> p (a b)"), bank(r, 2), s_o2[r])

            rows(act, {7: [tile(normed, 0)]},
                 {3: [tile(exps, 0)], 5: [tile(exps, 1)]},
                 {3: [tile(evacuate, 0)], 5: [tile(evacuate, 1)], 6: [heads_out], 8: [tile(normed, 1)]})

        @block.gpsimd
        def _(pool):
            prime(pool, s_x1b)
            for r in range(2):
                pool.memset(Vz[r][:, :, :, :, :], 0.0).then_inc(s_init, 1)
            pool.memset(minus_half[:, :], -0.5).then_inc(s_init, 1)
            pool.wait_ge(s_w, 16 * len(loads))
            pool.wait_ge(s_init, 3)

            def inverse_root(b, r, k):
                s_ln[k][r].wait(pool, b, 5)
                pool.tensor_tensor(rstd[r][:, k, :], vareps[r][:, k, :], minus_half[:, :], ALU.pow)\
                    .then_inc(s_rstd[k][r].sem, 1)

            def biased(b, r):
                s_in[r].wait(pool, b, 32)
                s_x2[r].wait(pool, b, 0)
                s_xn[0][r].wait(pool, b, 2)
                pool.tensor_tensor(x1b[r][:, :, :], x1[r][:, :, :],
                                   xrow[:, 1:2, :].to_broadcast([P, TT, C]), ALU.add)\
                    .then_inc(s_x1b[r].sem, 1)

            def blocks(b, r):
                s_kv[r].wait(pool, b, 1)
                for f in range(CT):
                    m = pool.tensor_tensor(Kbd[r][:, f, :, :], kT2[r][:, f:f + 1, :].to_broadcast([P, XH, CTX]),
                                           own16[:, :].unsqueeze(2).to_broadcast([P, XH, CTX]), ALU.mult)
                m.then_inc(s_kbd[r].sem, 1)

            def normalise(b, r, i):
                s_r2[r].wait(pool, b, 2 * i + 2)
                pool.tensor_tensor(P2[r][:, i, :, :], P2[r][:, i, :, :],
                                   ri2[r][:, i, :].unsqueeze(2).to_broadcast([P, HEADS, CTX]), ALU.mult)\
                    .then_inc(s_n2[r].sem, 1)

            rows(pool, {4: [tile(inverse_root, 0)], 6: [blocks], 9: [biased]},
                 {6: [tile(normalise, 0)], 8: [tile(normalise, 1)]},
                 {7: [tile(inverse_root, 1)]})

        @block.vector
        def _(dve):
            prime(dve, s_x2)
            dve.sem_inc(s_hmax.sem, s_hmax.first)
            dve.wait_ge(s_w, 16 * len(loads))
            dve.wait_ge(s_init, 3)

            def statistics(b, r, k):
                src = (x2 if k else x1)[r]
                (s_x2 if k else s_in)[r].wait(dve, b, 1 if k else 32)
                for i in range(TT):
                    dve.bn_stats(stats[r][:, k, i, :], src[:, i, :]).then_inc(s_ln[k][r].sem, 1)
                s_ln[k][r].wait(dve, b, 2)
                dve.tensor_copy(held[r][:, 0:1], stats[r][:, k, 0, 0:1])
                for i in range(TT):
                    dve.bn_aggr(meanvar[r][:, k, i, :], stats[r][:, k, i, :]).then_inc(s_ln[k][r].sem, 1)
                s_ln[k][r].wait(dve, b, 4)
                dve.tensor_scalar(vareps[r][:, k, :], meanvar[r][:, k, :, 1], LN_EPS, None, ALU.add)\
                    .then_inc(s_ln[k][r].sem, 1)

            def norm(b, r, k):
                src = (x2 if k else x1)[r]
                s_rstd[k][r].wait(dve, b, 1)
                s_xnT_ps[k][r].wait(dve, b, 0)
                for i in range(TT):
                    dve.tensor_scalar(xn[r][:, k, i, :], src[:, i, :], meanvar[r][:, k, i, 0:1], rstd[r][:, k, i:i + 1],
                                      ALU.subtract, ALU.mult).then_inc(s_xn[k][r].sem, 1)

            def context(b, r):
                s_kv_ps[r].wait(dve, b, 1)
                for f in range(CT):
                    m = dve.tensor_scalar(kT2[r][:, f, :], bank(r, 0)[:, f * P:f * P + CTX], xb[:, 1, f:f + 1],
                                          None, ALU.add)
                m.then_inc(s_kv[r].sem, 1)
                s_kv_ps[r].wait(dve, b, 2)
                for w in range(2):
                    m = dve.tensor_tensor(
                        Vz[r][:, :, w, w, :],
                        bank(r, 1)[0:CTX, 0:C].rearrange("p (a w d) -> p a w d", w=2, d=XD)[:, :, w, :],
                        xrow[0:CTX, 0, :].rearrange("p (a w d) -> p a w d", w=2, d=XD)[:, :, w, :], ALU.add)
                m.then_inc(s_kv[r].sem, 1)

            def queries(b, r):
                s_q2_ps[r].wait(dve, b, 1)
                for f in range(CT):
                    m = dve.tensor_scalar(q2[r][:, f, :], bank(r, 3)[:, f * T:(f + 1) * T], xb[:, 0, f:f + 1],
                                          XD ** -0.5, ALU.add, ALU.mult)
                m.then_inc(s_q2[r].sem, 1)

            def shift(b, r, i):
                s_s2[r].wait(dve, b, i + 1)
                S = ps[:, 4 * r:4 * r + 4, 0:4 * CTX].rearrange("p f (h k) -> p f h k", k=CTX)
                dve.tensor_reduce(nmax2[r][:, :].rearrange("p (f h) -> p f h", f=4), S, AX.X, ALU.max,
                                  negate=True).then_inc(s_sub2[r].sem, 1)
                s_sub2[r].wait(dve, b, 2 * i + 1)
                dve.tensor_tensor(P2[r][:, i, :, :].rearrange("p (f h) k -> p f h k", f=4), S,
                                  nmax2[r][:, :].rearrange("p (f h) -> p f h", f=4).unsqueeze(3)
                                  .to_broadcast([P, 4, 4, CTX]), ALU.add).then_inc(s_sub2[r].sem, 1)

            def sums(b, r, i):
                s_e2[r].wait(dve, b, i + 1)
                dve.tensor_reduce(rs2[r][:, i, :], P2[r][:, i, :, :], AX.X, ALU.add).then_inc(s_r2[r].sem, 1)
                s_r2[r].wait(dve, b, 2 * i + 1)
                dve.reciprocal(ri2[r][:, i, :], rs2[r][:, i, :]).then_inc(s_r2[r].sem, 1)

            def residual(b, r):
                s_y2_ps[r].wait(dve, b, 1)
                s_x1b[r].wait(dve, b, 1)
                s_out[r].wait(dve, b, 0)
                dve.tensor_tensor(x2[r][:, :, :].rearrange("p a b -> p (a b)"), bank(r, 3),
                                  x1b[r][:, :, :].rearrange("p a b -> p (a b)"), ALU.add)\
                    .then_inc(s_x2[r].sem, 1)

            def largest(b, r):
                s_xn[1][r].wait(dve, b, 2)
                dve.tensor_reduce(hm[r][:, :], xn[r][:, 1, :, :].rearrange("p a b -> p (a b)"), AX.X, ALU.max,
                                  apply_absolute_value=True).then_inc(s_hm[r].sem, 1)
                s_hm[r].wait(dve, b, 1)
                s_hmax.wait(dve, b, r)
                dve.tensor_tensor(hmax[:, :], hmax[:, :], hm[r][:, :], ALU.max).then_inc(s_hmax.sem, 1)

            rows(dve, {4: [tile(statistics, 0)], 6: [tile(norm, 0), context], 8: [queries]},
                 {3: [tile(shift, 0)], 5: [tile(shift, 1)], 6: [tile(sums, 0), tile(sums, 1)]},
                 {7: [residual, tile(statistics, 1)], 8: [tile(norm, 1)], 9: [largest]})


def feed_forward(nc, io, h_dram, x2_dram, u_dram, ident, hmax):
    with ExitStack() as ctx:
        def sb(name, shape, dt=F32):
            return ctx.enter_context(nc.sbuf_tensor(name, shape, dt))

        def signal(name, per=1, first=0):
            return Signal(ctx.enter_context(nc.semaphore("s_" + name)), per, first)

        def prime(eng, *signals):
            for s in signals:
                eng.sem_inc(s.sem, s.first)

        NB = INNER * C // P // BLK
        WC = INNER * C // P
        G = sb("G", [P, B, IT * T])
        wT = [[sb("%s_%s" % (name, n), shape, FP16) for n in ("upper", "lower")] for name, shape in
              (("wgT", [P, CT, INNER]), ("wuT", [P, CT, INNER]), ("wdT", [P, IT, C]))]
        hq2 = [sb("hq_" + n, [P, 2, CT * T], FP16) for n in ("upper", "lower")]
        oq2 = [sb("oq_" + n, [P, 2, IT * T], FP16) for n in ("upper", "lower")]
        wn = sb("wn", [P, WC])
        wq = sb("wq", [P, WC])
        wmax = sb("wmax", [P, NB])
        wscale = sb("wscale", [P, NB])
        winv = sb("winv", [P, NB])
        hin = sb("hin", [P, 2, CT * T])
        hq = sb("hq", [P, 2, CT * T])
        ubuf = sb("ubuf", [P, 2, IT * T])
        t1 = sb("t1", [P, IT * T])
        t2 = sb("t2", [P, IT * T])
        t3 = sb("t3", [P, IT * T])
        am = sb("am", [P, IT, 2])
        amc = sb("amc", [P, 2])
        held = sb("held3", [P, 5])
        magic = sb("magic", [P, 2])
        run = sb("run", [P, 4])
        tot = sb("tot", [P, 5])
        sc = sb("sc", [P, 5])
        raw = sb("raw", [P, 5])
        inv = sb("inv", [P, 5])
        tmp = sb("tmp", [P, 5])
        xres = sb("xres", [P, 2, TT * C])
        yout = sb("yout", [P, 2, TT * C])
        ps = ctx.enter_context(nc.psum_tensor("ps2", [P, 8, 512], F32))
        GATE, UP, PROD, OUTQ, INP = range(5)

        QUARTERS = 4
        HB = IT * T // 2
        BODIES = 2 * B // QUARTERS

        s_wn = signal("w_loaded", 0)
        s_wop = signal("w_ops", 0)
        s_wt_ps = signal("wT_ps", 0)
        s_wt = signal("wT", 0)
        s_wl = signal("wT_lower", 0)
        s_tot = signal("total_max", 0)
        s_sc = signal("scale_ops", 0)
        s_zero = signal("zeroed", 0)
        s_h = [signal("h_loaded_even", 16), signal("h_loaded_odd", 16)]
        s_hr = signal("h_raised", 2, first=2)
        s_hq = signal("h_quantised", 2, first=2)
        s_hh = signal("h_upper", 2)
        s_hl = signal("h_lower", 2)
        s_gu_ps = signal("gu_ps", 2 * IT, first=2 * IT)
        s_gu = signal("gu_copied", 2 * IT, first=2 * IT)
        s_gum = signal("gu_max", 2 * IT, first=2 * IT)
        s_run_a = signal("a_running", 4)
        s_ust = [signal("u_stored_even", 16, first=1), signal("u_stored_odd", 16, first=1)]
        s_gr = signal("g_raised", QUARTERS)
        s_gq = signal("g_quantised", QUARTERS)
        s_sig = signal("sigmoid", QUARTERS)
        s_sr = signal("sigmoid_raised", QUARTERS)
        s_sqz = signal("sigmoid_quantised", QUARTERS)
        s_gp = signal("g_product", QUARTERS, first=QUARTERS)
        s_run_b = signal("b_running", 2 * QUARTERS)
        s_u = [signal("u_loaded_even", 16), signal("u_loaded_odd", 16)]
        s_ur = signal("u_raised", QUARTERS, first=QUARTERS)
        s_pr = signal("p_raised", QUARTERS)
        s_cq = signal("c_quantised", 2 * QUARTERS)
        s_op = signal("o_product", QUARTERS, first=QUARTERS)
        s_run_c = signal("c_running", 2 * QUARTERS)
        s_or = signal("o_raised", 2)
        s_oq = signal("o_quantised", 4, first=4)
        s_oh = signal("o_upper", 2)
        s_xr = [signal("x_loaded_even", 16), signal("x_loaded_odd", 16)]
        s_y_ps = signal("y_ps", 4, first=4)
        s_y = signal("y", 4, first=4)
        s_yst = [signal("y_stored_even", 16, first=1), signal("y_stored_odd", 16, first=1)]

        block = ctx.enter_context(nc.Block())
        names = ["ffn_gate", "ffn_up", "ffn_down"]

        def at_block(eng_block):
            return G[:, bass.ds(eng_block, 1), :].rearrange("p o c -> p (o c)")

        def at_half(bb, j):
            return at_block(bb * 2 + j // 2)[:, (j % 2) * HB:(j % 2 + 1) * HB]

        def buffers(a, b):
            return [t[:, n * HB:(n + 1) * HB] for t in (a, b) for n in range(2)]

        first4 = buffers(t1, t3)
        second4 = buffers(t2, wq)

        def staggered(eng, stages, size=QUARTERS, bodies=BODIES):
            last = max(lag for lag, _ in stages)
            for j in range(size):
                for lag, step in stages:
                    if j >= lag:
                        step(0, j - lag)
            with eng.Fori(1, bodies) as bb:
                for j in range(size):
                    for lag, step in stages:
                        step(bb, j - lag)
            for j in range(size, size + last):
                for lag, step in stages:
                    if j - lag < size:
                        step(bodies - 1, j - lag)

        def by_blocks(eng, stages):
            staggered(eng, stages, 2, B // 2)

        def lag_pass(bb, j):
            return (bb, j) if j >= 0 else (bb - 1, j + 2)

        @block.sync
        def _(sp):
            prime(sp, *s_ust, *s_yst)
            for n, name in enumerate(names):
                if n:
                    sp.wait_ge(s_wop.sem, 7 * n)
                sp.dma_start(wn[:, :], io[name]).then_inc(s_wn.sem, 16)

            def load_h(bb, j):
                s_hr.wait(sp, bb, j + 1 - 2, 1)
                sp.dma_start(hin[:, j % 2, :], h_dram[bass.ds(bb * 2 + j, 1)].rearrange("o p c -> p (o c)"))\
                    .then_inc(s_h[j % 2].sem, 16)

            def store_u(bb, j):
                s_gu.wait(sp, bb, IT * (j + 1), 1)
                sp.dma_start(u_dram[bass.ds(bb * 2 + j, 1)].rearrange("o p c -> p (o c)"), ubuf[:, j % 2, :])\
                    .then_inc(s_ust[j % 2].sem, 16)

            by_blocks(sp, [(0, load_h), (2, store_u)])
            for k in range(2):
                s_ust[k].wait_all(sp, B // 2)
            with sp.Fori(0, B // 2) as bb:
                for k in range(2):
                    s_ur.wait(sp, bb, 2 * k - 2)
                    sp.dma_start(ubuf[:, k, :], u_dram[bass.ds(bb * 2 + k, 1)].rearrange("o p c -> p (o c)"))\
                        .then_inc(s_u[k].sem, 16)

            def load_x(bb, j):
                s_y.wait(sp, bb, 2 * (j + 1 - 2), 1)
                sp.dma_start(xres[:, j % 2, :], x2_dram[bass.ds(bb * 2 + j, 1)].rearrange("o p c -> p (o c)"))\
                    .then_inc(s_xr[j % 2].sem, 16)

            def store_y(bb, j):
                s_y.wait(sp, bb, 2 * (j + 1), 1)
                sp.dma_start(io["out"][bass.ds(bb * 2 + j, 1)].rearrange("o (i p) c -> p (o i) c", p=P),
                             yout[:, j % 2, :].rearrange("p (i c) -> p i c", i=TT))\
                    .then_inc(s_yst[j % 2].sem, 16)

            by_blocks(sp, [(0, load_x), (1, store_y)])
            for k in range(2):
                s_yst[k].wait_all(sp, B // 2)

        @block.gpsimd
        def _(pool):
            pool.memset(run[:, :], 0.0).then_inc(s_zero.sem, 1)
            pool.memset(magic[:, 0:1], MAGIC).then_inc(s_zero.sem, 1)
            pool.memset(magic[:, 1:2], 65536.0).then_inc(s_zero.sem, 1)
            pool.wait_ge(s_zero.sem, 3)
            red = bass.bass_isa.ReduceOp.max

            def carry(j):
                at = 1 + j % QUARTERS
                pool.tensor_tensor(held[:, at:at + 1], magic[:, 0:1], magic[:, 1:2], ALU.add)

            def sigmoids(bb, j):
                t = second4[j % QUARTERS]
                s_sig.wait(pool, bb, j + 1, 1)
                carry(j)
                pool.tensor_scalar(t, t, magic[:, 1:2], MAGIC, ALU.mult, ALU.add).then_inc(s_sr.sem, 1)

            pool.partition_all_reduce(tot[:, INP:INP + 1], hmax[:, :], P, red).then_inc(s_tot.sem, 1)
            s_run_a.wait_all(pool, B // 2)
            pool.partition_all_reduce(tot[:, GATE:UP + 1], run[:, GATE:UP + 1], P, red).then_inc(s_tot.sem, 1)
            staggered(pool, [(0, sigmoids)])
            s_run_b.wait_all(pool, BODIES)
            pool.partition_all_reduce(tot[:, PROD:PROD + 1], run[:, PROD:PROD + 1], P, red)\
                .then_inc(s_tot.sem, 1)
            s_run_c.wait_all(pool, BODIES)
            pool.partition_all_reduce(tot[:, OUTQ:OUTQ + 1], run[:, OUTQ:OUTQ + 1], P, red)\
                .then_inc(s_tot.sem, 1)

        @block.tensor
        def _(pe):
            prime(pe, s_gu_ps, s_y_ps)
            for n in range(3):
                pe.wait_ge(s_wop.sem, 7 * (n + 1))
                rows, cols = ((IT, CT), (IT, CT), (CT, IT))[n]
                w = wq[:, :].rearrange("p (r c) -> p r c", r=rows)
                order = [(r, c) for c in range(cols) for r in range(rows)]
                for k, (r, c) in enumerate(order):
                    q = 12 * n + k
                    if q >= 8 and k % 4 == 0:
                        pe.wait_ge(s_wl.sem, q // 4 - 1)
                    m = pe.transpose(ps[:, (q // 4) % 2, (q % 4) * P:(q % 4 + 1) * P],
                                     w[:, r, c * P:(c + 1) * P], ident[:, :])
                    if k % 4 == 3:
                        m.then_inc(s_wt_ps.sem, 1)
            pe.wait_ge(s_wl.sem, 9)

            def product(out, left, right, start, stop):
                pe.matmul(out, left[0], right[0], start=start, stop=False)
                pe.matmul(out, left[0], right[1], start=False, stop=False)
                return pe.matmul(out, left[1], right[0], start=False, stop=stop)

            def gate_and_up(bb, j):
                s_hl.wait(pe, bb, j + 1, 1)
                for it in range(IT):
                    n = j * IT + it
                    s_gu.wait(pe, bb, n + 1 - 6, 1)
                    s_gum.wait(pe, bb, n + 1 - 6, 1)
                    for w in range(2):
                        for c in range(CT):
                            m = product(ps[:, n % 6, w * T:(w + 1) * T],
                                        [t[:, c, it * P:(it + 1) * P] for t in wT[w]],
                                        [t[:, j, c * T:(c + 1) * T] for t in hq2],
                                        start=(c == 0), stop=(c == CT - 1))
                    m.then_inc(s_gu_ps.sem, 1)

            by_blocks(pe, [(0, gate_and_up)])

            def down(bb, j):
                s_oq.wait(pe, bb, 2 * j + 2, 1)
                for i in range(TT):
                    n = 2 * j + i
                    s_y.wait(pe, bb, n + 1 - 4, 1)
                    for it in range(IT):
                        at = slice(it * T + i * P, it * T + (i + 1) * P)
                        m = product(ps[:, n, 0:C], [t[:, j, at] for t in oq2], [t[:, it, :] for t in wT[2]],
                                    start=(it == 0), stop=(it == IT - 1))
                    m.then_inc(s_y_ps.sem, 1)

            by_blocks(pe, [(0, down)])

        def raised(act, out, src, stage, sig):
            act.activation(out, src, ACT.Copy, scale=inv[:, stage:stage + 1], bias=MAGIC).then_inc(sig.sem, 1)

        @block.scalar
        def _(act):
            prime(act, s_gu, s_hr, s_ur)
            for q in range(9):
                act.wait_ge(s_wt_ps.sem, q + 1)
                n, k = q // 3, q % 3
                upper = wT[n][0][:, :, :].rearrange("p a b -> p (a b)")
                act.activation(upper[:, k * 512:(k + 1) * 512], ps[:, q % 2, :], ACT.Copy, scale=WSCALE)\
                    .then_inc(s_wt.sem, 1)
            act.wait_ge(s_sc.sem, 4)

            def raise_h(bb, j):
                s_h[j].wait(act, bb, 16)
                s_hq.wait(act, bb, j + 1 - 2, 1)
                raised(act, t1[:, j * CT * T:(j + 1) * CT * T], hin[:, j, :], INP, s_hr)

            def upper_h(bb, j):
                s_hq.wait(act, bb, j + 1, 1)
                s_gu_ps.wait(act, bb, IT * (j + 1 - 2), 1)
                act.activation(hq2[0][:, j, :], hq[:, j, :], ACT.Copy).then_inc(s_hh.sem, 1)

            def copy_gu(bb, j):
                b_, k = lag_pass(bb, j)
                s_ust[k].wait(act, b_, 0)
                for it in range(IT):
                    n = j * IT + it
                    s_gu_ps.wait(act, bb, n + 1, 1)
                    act.activation(at_block(bb * 2 + j)[:, it * T:(it + 1) * T], ps[:, n % 6, 0:T], ACT.Copy,
                                   scale=1.0 / WSCALE)
                    act.activation(ubuf[:, k, it * T:(it + 1) * T], ps[:, n % 6, T:2 * T], ACT.Copy,
                                   scale=1.0 / WSCALE).then_inc(s_gu.sem, 1)

            by_blocks(act, [(0, raise_h), (0, upper_h), (1, copy_gu)])
            act.wait_ge(s_sc.sem, 12)

            def raise_gates(bb, j):
                s_gp.wait(act, bb, j + 1 - QUARTERS, 1)
                raised(act, first4[j % QUARTERS], at_half(bb, j), GATE, s_gr)

            def sigmoid(bb, j):
                s_gq.wait(act, bb, j + 1, 1)
                act.activation(second4[j % QUARTERS], first4[j % QUARTERS], ACT.Sigmoid,
                               scale=sc[:, GATE:GATE + 1]).then_inc(s_sig.sem, 1)

            staggered(act, [(0, raise_gates), (1, sigmoid)])
            act.wait_ge(s_sc.sem, 18)

            def raise_factors(bb, j):
                s_op.wait(act, bb, j + 1 - QUARTERS, 1)
                n, half = j // 2, j % 2
                s_u[n].wait(act, bb, 16)
                raised(act, first4[j % QUARTERS], ubuf[:, n, half * HB:(half + 1) * HB], UP, s_ur)
                raised(act, second4[j % QUARTERS], at_half(bb, j), PROD, s_pr)

            staggered(act, [(0, raise_factors)])
            act.wait_ge(s_sc.sem, 23)

            def raise_o(bb, j):
                s_oq.wait(act, bb, 2 * (j + 1 - 2), 1)
                raised(act, (t2, t3)[j][:, :], at_block(bb * 2 + j), OUTQ, s_or)

            def upper_o(bb, j):
                s_oq.wait(act, bb, 2 * j + 1, 1)
                s_y_ps.wait(act, bb, 2 * (j + 1 - 2), 1)
                act.activation(oq2[0][:, j, :], (t2, t3)[j][:, :], ACT.Copy).then_inc(s_oh.sem, 1)

            by_blocks(act, [(0, raise_o), (0, upper_o)])

        @block.vector
        def _(dve):
            prime(dve, s_gp, s_gum, s_hq, s_op, s_oq, s_y)
            for n in range(3):
                k = 7 * n
                op = lambda ins: ins.then_inc(s_wop.sem, 1)
                wb = wn[:, :].rearrange("p (n e) -> p n e", e=BLK)
                qb = wq[:, :].rearrange("p (n e) -> p n e", e=BLK)
                dve.wait_ge(s_wn.sem, 16 * (n + 1))
                if n:
                    dve.wait_ge(s_wt_ps.sem, 3 * n)
                op(dve.tensor_reduce(wmax[:, :], wb, AX.X, ALU.max, apply_absolute_value=True))
                dve.wait_ge(s_wop.sem, k + 1)
                op(dve.tensor_scalar(wscale[:, :], wmax[:, :], 1.0 / 7.0, 1e-12, ALU.mult, ALU.max))
                dve.wait_ge(s_wop.sem, k + 2)
                op(dve.reciprocal(winv[:, :], wscale[:, :]))
                dve.wait_ge(s_wop.sem, k + 3)
                bc = lambda a: a[:, :].unsqueeze(2).to_broadcast([P, NB, BLK])
                op(dve.tensor_tensor(qb, wb, bc(winv), ALU.mult))
                dve.wait_ge(s_wop.sem, k + 4)
                op(dve.tensor_scalar(wq[:, :], wq[:, :], MAGIC, None, ALU.add))
                dve.wait_ge(s_wop.sem, k + 5)
                op(dve.tensor_scalar(wq[:, :], wq[:, :], MAGIC, 7.0, ALU.subtract, ALU.min))
                dve.wait_ge(s_wop.sem, k + 6)
                op(dve.scalar_tensor_tensor(qb, qb, -8.0, bc(wscale), ALU.max, ALU.mult))
                for k3 in range(3):
                    q = 3 * n + k3
                    dve.wait_ge(s_wt.sem, q + 1)
                    up, low = [t[:, :, :].rearrange("p a b -> p (a b)")[:, k3 * 512:(k3 + 1) * 512] for t in wT[n]]
                    dve.scalar_tensor_tensor(low, ps[:, q % 2, :], WSCALE, up, ALU.mult, ALU.subtract)\
                        .then_inc(s_wl.sem, 1)

            def scales(first, stage, unit):
                n = first
                t, s, v = tot[:, stage:stage + 1], sc[:, stage:stage + 1], inv[:, stage:stage + 1]
                m = tmp[:, stage:stage + 1]
                if unit is None:
                    dve.tensor_scalar(m, t, 1.0, None, ALU.mult).then_inc(s_sc.sem, 1)
                else:
                    dve.tensor_scalar(m, t, unit, None, ALU.mult).then_inc(s_sc.sem, 1)
                dve.wait_ge(s_sc.sem, n + 1)
                dve.tensor_scalar(s, m, 1.0 / QMAX, 1e-12, ALU.mult, ALU.max).then_inc(s_sc.sem, 1)
                dve.wait_ge(s_sc.sem, n + 2)
                dve.reciprocal(v, s).then_inc(s_sc.sem, 1)
                dve.wait_ge(s_sc.sem, n + 3)
                if unit is None:
                    dve.tensor_scalar(v, v, 1.0, None, ALU.mult).then_inc(s_sc.sem, 1)
                else:
                    dve.tensor_scalar(v, v, unit, None, ALU.mult).then_inc(s_sc.sem, 1)
                return n + 4

            dve.wait_ge(s_zero.sem, 3)
            dve.wait_ge(s_tot.sem, 1)
            n = scales(0, INP, None)
            dve.wait_ge(s_sc.sem, n)

            def clip_h(bb, j):
                s_hr.wait(dve, bb, j + 1, 1)
                dve.tensor_scalar(hq[:, j, :], t1[:, j * CT * T:(j + 1) * CT * T], MAGIC, QMAX,
                                  ALU.subtract, ALU.min).then_inc(s_hq.sem, 1)

            def lower_h(bb, j):
                s_hh.wait(dve, bb, j + 1, 1)
                dve.tensor_tensor(hq2[1][:, j, :], hq[:, j, :], hq2[0][:, j, :], ALU.subtract)\
                    .then_inc(s_hl.sem, 1)

            def largest_gu(bb, j):
                for it in range(IT):
                    n_ = j * IT + it
                    s_gu_ps.wait(dve, bb, n_ + 1, 1)
                    s_gu.wait(dve, bb, n_ + 1, 1)
                    dve.tensor_reduce(am[:, it, :], ps[:, n_ % 6, :].rearrange("p (a t) -> p a t", a=2),
                                      AX.X, ALU.max, apply_absolute_value=True).then_inc(s_gum.sem, 1)
                s_gum.wait(dve, bb, (j + 1) * IT, 1)
                dve.tensor_reduce(amc[:, :], am[:, :, :].rearrange("p i a -> p a i"), AX.X, ALU.max)\
                    .then_inc(s_run_a.sem, 1)
                s_run_a.wait(dve, bb, 2 * j + 1, 1)
                dve.scalar_tensor_tensor(run[:, 0:2], amc[:, :], 1.0 / WSCALE, run[:, 0:2], ALU.mult, ALU.max)\
                    .then_inc(s_run_a.sem, 1)
                s_run_a.wait(dve, bb, 2 * j + 2, 1)

            by_blocks(dve, [(0, clip_h), (0, lower_h), (1, largest_gu)])
            dve.wait_ge(s_tot.sem, 2)
            n = scales(4, GATE, sc[:, INP:INP + 1])
            n = scales(n, UP, sc[:, INP:INP + 1])
            dve.wait_ge(s_sc.sem, n)

            def largest(bb, j, stage, made, run_):
                made.wait(dve, bb, j + 1, 1)
                dve.tensor_copy(held[:, 0:1], magic[:, 0:1])
                dve.tensor_reduce(amc[:, 0:1], at_half(bb, j), AX.X, ALU.max, apply_absolute_value=True)\
                    .then_inc(run_.sem, 1)
                run_.wait(dve, bb, 2 * j + 1, 1)
                dve.tensor_tensor(run[:, stage:stage + 1], run[:, stage:stage + 1], amc[:, 0:1], ALU.max)\
                    .then_inc(run_.sem, 1)

            def clip_gates(bb, j):
                s_gr.wait(dve, bb, j + 1, 1)
                t = first4[j % QUARTERS]
                dve.tensor_scalar(t, t, MAGIC, QMAX, ALU.subtract, ALU.min).then_inc(s_gq.sem, 1)

            def clip_sigmoids(bb, j):
                s_sr.wait(dve, bb, j + 1, 1)
                t = second4[j % QUARTERS]
                dve.tensor_scalar(t, t, MAGIC, 65535.0, ALU.subtract, ALU.min).then_inc(s_sqz.sem, 1)

            def gate_products(bb, j):
                s_sqz.wait(dve, bb, j + 1, 1)
                dve.tensor_tensor(at_half(bb, j), first4[j % QUARTERS], second4[j % QUARTERS], ALU.mult)\
                    .then_inc(s_gp.sem, 1)
                largest(bb, j, PROD, s_gp, s_run_b)

            staggered(dve, [(0, clip_gates), (2, clip_sigmoids), (3, gate_products)])
            s_run_b.wait_all(dve, BODIES)
            dve.wait_ge(s_tot.sem, 3)
            dve.tensor_scalar(raw[:, PROD:PROD + 1], sc[:, GATE:GATE + 1], 1.0 / 65536.0, None, ALU.mult)\
                .then_inc(s_sc.sem, 1)
            dve.wait_ge(s_sc.sem, 13)
            n = scales(13, PROD, raw[:, PROD:PROD + 1])
            dve.wait_ge(s_sc.sem, n)
            dve.tensor_scalar(raw[:, OUTQ:OUTQ + 1], sc[:, PROD:PROD + 1], sc[:, UP:UP + 1], None, ALU.mult)\
                .then_inc(s_sc.sem, 1)

            def clip_factors(bb, j):
                for raised_, t in ((s_ur, first4[j % QUARTERS]), (s_pr, second4[j % QUARTERS])):
                    raised_.wait(dve, bb, j + 1, 1)
                    dve.tensor_scalar(t, t, MAGIC, QMAX, ALU.subtract, ALU.min).then_inc(s_cq.sem, 1)

            def output_products(bb, j):
                s_cq.wait(dve, bb, 2 * j + 2, 1)
                dve.tensor_tensor(at_half(bb, j), first4[j % QUARTERS], second4[j % QUARTERS], ALU.mult)\
                    .then_inc(s_op.sem, 1)
                largest(bb, j, OUTQ, s_op, s_run_c)

            staggered(dve, [(0, clip_factors), (1, output_products)])
            dve.wait_ge(s_tot.sem, 4)
            dve.wait_ge(s_sc.sem, 18)
            n = scales(18, OUTQ, raw[:, OUTQ:OUTQ + 1])
            dve.wait_ge(s_sc.sem, n)
            dve.tensor_scalar(raw[:, INP:INP + 1], sc[:, OUTQ:OUTQ + 1], 1.0 / WSCALE, None, ALU.mult)\
                .then_inc(s_sc.sem, 1)
            dve.wait_ge(s_sc.sem, n + 1)

            def clip_o(bb, j):
                s_or.wait(dve, bb, j + 1, 1)
                t = (t2, t3)[j]
                dve.tensor_scalar(t[:, :], t[:, :], MAGIC, QMAX, ALU.subtract, ALU.min).then_inc(s_oq.sem, 1)

            def lower_o(bb, j):
                s_oh.wait(dve, bb, j + 1, 1)
                dve.tensor_tensor(oq2[1][:, j, :], (t2, t3)[j][:, :], oq2[0][:, j, :], ALU.subtract)\
                    .then_inc(s_oq.sem, 1)

            def outputs(bb, j):
                b_, k = lag_pass(bb, j)
                s_xr[k].wait(dve, b_, 16)
                s_yst[k].wait(dve, b_, 0)
                for i in range(TT):
                    s_y_ps.wait(dve, bb, 2 * j + i + 1, 1)
                    dve.scalar_tensor_tensor(yout[:, k, i * C:(i + 1) * C], ps[:, 2 * k + i, 0:C],
                                             raw[:, INP:INP + 1], xres[:, k, i * C:(i + 1) * C],
                                             ALU.mult, ALU.add).then_inc(s_y.sem, 1)

            by_blocks(dve, [(0, clip_o), (0, lower_o), (1, outputs)])



def _layouts(i):
    f = np.float32

    def rows(w):
        return w.reshape(w.shape[0] // P, P, -1).transpose(1, 0, 2)

    def below(w, first):
        out = np.zeros((P, w.shape[1]), f)
        out[first:first + w.shape[0]] = w
        return out

    def grouped(nope, rope):
        n = nope.shape[0]
        both = np.concatenate([nope.reshape(n, HEADS, 1, PART), rope.reshape(n, HEADS, 2, PART)], axis=2)
        return both.reshape(n, GROUPS, GROUP, PARTS, PART).transpose(0, 1, 3, 2, 4).reshape(n, -1)

    def split(w):
        w = w.reshape(w.shape[0], HEADS, DK)
        return grouped(w[:, :, :PART], w[:, :, PART:])

    a = {k: np.asarray(v) for k, v in i.items()}
    att = lambda n: a["L0_attn_" + n]
    xat = lambda n: a["L0_xattn_" + n]
    t = np.arange(T, dtype=f)
    freq = (1.0 / np.power(f(10000.0), np.arange(0, 2 * PART, 2, dtype=f) / f(2 * PART))).astype(f)
    angle = np.outer(t, freq).astype(f)
    cos, sin = np.cos(angle).T, np.sin(angle).T
    table = np.stack([np.tile(cos, (GROUP, 1)), np.tile(sin, (GROUP, 1))], 1).astype(f)
    p = np.arange(P)
    mask = np.where(p[None, :] > p[:, None], MASKED, 0.0).astype(f)
    kr = att("w_krope")
    bf = mybir.dt.np(BF16)
    return {
        "x": a["x"],
        "ctxT": a["ctx_1024"].transpose(0, 2, 1),
        "w_lat": rows(np.concatenate([att("w_cq"), att("w_ckv"), att("w_gate")[:, GATE_ORDER]], axis=1)),
        "w_imp": rows(np.tile(att("w_imp"), (1, P))),
        "w_win": rows(split(att("w_wink"))),
        "w_sel": rows(split(att("w_selk"))),
        "w_winv": rows(att("w_winv")),
        "w_selv": rows(att("w_selv")),
        "w_q": below(grouped(att("w_dq_nope"), att("w_dq_rope")), 0),
        "w_kn": below(att("w_dk_nope"), QL),
        "w_v1": below(att("w_dv"), QL),
        "w_kr": rows(np.concatenate([np.tile(kr[:, :PART], (1, GROUP)), np.tile(kr[:, PART:], (1, GROUP))], 1)),
        "w_proj": rows(att("w_proj")),
        "w_x": np.stack([rows(xat(n).T) for n in ("Wq", "Wk", "Wv", "Wo")], axis=1),
        "g_lat": np.concatenate([att("g_qnorm"), att("g_kvnorm")])[:, None],
        "rope_k": table,
        "rope_q": (table * f(DK ** -0.5)).astype(f),
        "maskb": np.concatenate([mask, mask], axis=1).astype(bf),
        "identb": np.eye(P).astype(bf),
        "before": np.stack([(np.arange(T)[None, :] < (p + n * P)[:, None]) for n in range(TT)], 1).astype(f),
        "uptri": np.concatenate([(p[:, None] < p[None, :]).astype(f), np.ones((P, P), f)], axis=1),
        "iota64": np.tile(np.arange(KEEP, dtype=f), (P, 1)),
        "own16": (p[:, None] // XD == np.arange(XH)[None, :]).astype(f),
        "meanw": np.full((P, P), 1.0 / T, f),
        "xb": np.stack([xat("bq").reshape(CT, P).T, xat("bk").reshape(CT, P).T], axis=1),
        "xrow": np.stack([np.tile(xat("bv"), (P, 1)), np.tile(xat("bo"), (P, 1))], axis=1),
        "ident": np.eye(P, dtype=f),
        "ffn_gate": rows(a["L0_ffn_w_gate"]).reshape(P, -1),
        "ffn_up": rows(a["L0_ffn_w_up"]).reshape(P, -1),
        "ffn_down": rows(a["L0_ffn_w_down"]).reshape(P, -1),
    }


def kernel(**inputs):
    import concourse.bacc as bacc
    from concourse.bass_utils import run_bass_kernel_spmd

    nc = bacc.Bacc("TRN2", target_bir_lowering=False, num_devices=1)
    arrays = {"in_" + k: np.ascontiguousarray(v) for k, v in _layouts(inputs).items()}
    io = {k[3:]: nc.dram_tensor(k, v.shape, mybir.dt.from_np(v.dtype), kind="ExternalInput").ap()
          for k, v in arrays.items()}
    io["out"] = nc.dram_tensor("out", (B, T, C), F32, kind="ExternalOutput").ap()
    build(nc, io)
    r = run_bass_kernel_spmd(nc, [arrays], core_ids=[0])
    return r.results[0]["out"]
```
